# Optimizing a Trainium2 kernel written in Bass

```python
import numpy as np
import jax
import jax.numpy as jnp

def _softmax(x, axis=-1):
    return jax.nn.softmax(x, axis=axis)

def _gelu(x):
    return jax.nn.gelu(x, approximate=True)

def _silu(x):
    return jax.nn.silu(x)

def _sigmoid(x):
    return jax.nn.sigmoid(x)

def _layernorm(x, axis=-1, eps=1e-05):
    m = jnp.mean(x, axis=axis, keepdims=True)
    v = jnp.var(x, axis=axis, keepdims=True)
    return (x - m) / jnp.sqrt(v + eps)

def _scatter_add(tgt, idx, src, axis=0):
    return tgt.at[idx].add(src)

def _segment_sum(src, seg, n):
    return jax.ops.segment_sum(src, seg, n)
kernel_name = 'mk_early_fusion_d2_tok_img768_r4_059a9d'

def setup_inputs(seed: int=0):
    np.random.seed(seed)
    _w = jnp.asarray

    def _rec_inputs():
        import jax
        import jax.numpy as jnp
        _rk = jax.random.key(seed)
        x = -0.00040386 + 0.999972 * jax.random.normal(jax.random.fold_in(_rk, 1), (16, 3, 128, 128), jnp.float32)
        txt = 0.198809 + 1.28268 * jax.random.normal(jax.random.fold_in(_rk, 2), (16, 32, 192), jnp.float32)
        return (x, txt)
    x, txt = _rec_inputs()

    def _L0_tok_setup():
        import jax, jax.numpy as jnp
        import numpy as np
        P = 16
        WIN = 64
        NH = 12

        def _layernorm(x, g, b, eps=1e-05):
            m = x.mean(-1, keepdims=True)
            v = ((x - m) ** 2).mean(-1, keepdims=True)
            return (x - m) * jax.lax.rsqrt(v + eps) * g + b

        def _sinusoidal_pe(n, d):
            pos = jnp.arange(n, dtype=jnp.float32)[:, None]
            i = jnp.arange(d // 2, dtype=jnp.float32)[None, :]
            ang = pos / jnp.power(10000.0, 2.0 * i / d)
            pe = jnp.zeros((n, d), jnp.float32)
            pe = pe.at[:, 0::2].set(jnp.sin(ang)).at[:, 1::2].set(jnp.cos(ang))
            return pe
        key = jax.random.key(seed)
        ks = jax.random.split(key, 8)
        B, C, H, W, D, F = (16, 3, 128, 128, 192, 768)
        s = lambda k, shape: jax.random.normal(k, shape, jnp.float32) * 0.02
        return {'input': jax.random.normal(ks[0], (B, C, H, W), jnp.float32), 'patch_w': s(ks[1], (D, C, P, P)), 'patch_b': jnp.zeros((D,), jnp.float32), 'ln_g': jnp.ones((D,), jnp.float32), 'ln_b': jnp.zeros((D,), jnp.float32), 'qkv_w': s(ks[2], (D, 3 * D)), 'qkv_b': jnp.zeros((3 * D,), jnp.float32), 'proj_w': s(ks[3], (D, D)), 'proj_b': jnp.zeros((D,), jnp.float32), 'ff1_w': s(ks[4], (D, F)), 'ff1_b': jnp.zeros((F,), jnp.float32), 'ff2_w': s(ks[5], (F, D)), 'ff2_b': jnp.zeros((D,), jnp.float32)}
    _L0_tok_all = _L0_tok_setup()
    _L0_tok_in = {k: v for k, v in _L0_tok_all.items() if k in ('patch_w', 'patch_b', 'ln_g', 'ln_b', 'qkv_w', 'qkv_b', 'proj_w', 'proj_b', 'ff1_w', 'ff1_b', 'ff2_w', 'ff2_b')}
    del _L0_tok_all

    def _L0_attn_setup():
        import jax, jax.numpy as jnp
        import numpy as np
        B, N, C, H = (4, 512, 192, 12)
        D = C // H
        SCALE = D ** (-0.5)
        key = jax.random.key(seed)
        k1, k2, k3 = jax.random.split(key, 3)
        x = jax.random.normal(k1, (B, N, C), dtype=jnp.float32)
        w_qkv = jax.random.normal(k2, (C, 3 * C), dtype=jnp.float32) * 0.02
        w_proj = jax.random.normal(k3, (C, C), dtype=jnp.float32) * 0.02
        b_proj = jnp.zeros((C,), dtype=jnp.float32)
        temperature = jnp.ones((H, 1, 1), dtype=jnp.float32) * 0.5
        return {'x': x, 'w_qkv': w_qkv, 'w_proj': w_proj, 'b_proj': b_proj, 'temperature': temperature}
    _L0_attn_all = _L0_attn_setup()
    _L0_attn_in = {k: v for k, v in _L0_attn_all.items() if k in ('w_qkv', 'w_proj', 'b_proj', 'temperature')}
    del _L0_attn_all

    def _L0_ffn_setup():
        import jax, jax.numpy as jnp
        import numpy as np
        E, D, H = (16, 192, 192)
        B, N = (32, 197)
        key = jax.random.key(seed)
        ks = jax.random.split(key, 7)
        s = 0.02
        return {'x': jax.random.normal(ks[0], (B, N, D), dtype=jnp.float32), 'W1': jax.random.normal(ks[1], (E, H, D), dtype=jnp.float32) * s, 'b1': jax.random.normal(ks[2], (E, H), dtype=jnp.float32) * s, 'W2': jax.random.normal(ks[3], (E, D, H), dtype=jnp.float32) * s, 'b2': jax.random.normal(ks[4], (E, D), dtype=jnp.float32) * s, 'Wg': jax.random.normal(ks[5], (E, D), dtype=jnp.float32) * s, 'bg': jnp.zeros((E,), dtype=jnp.float32)}
    _L0_ffn_all = _L0_ffn_setup()
    _L0_ffn_in = {k: v for k, v in _L0_ffn_all.items() if k in ('W1', 'b1', 'W2', 'b2', 'Wg', 'bg')}
    del _L0_ffn_all

    def _L1_attn_setup():
        import jax, jax.numpy as jnp
        import numpy as np
        KERNEL = 5
        NUM_HEADS = 4

        def _window_starts(L, k):
            pad = k // 2
            return jnp.clip(jnp.arange(L) - pad, 0, L - k)

        def _neighborhood_attention_2d(xs, qkv_w, qkv_b, rpb, proj_w, proj_b):
            H, W, D = xs.shape
            nh, k = (NUM_HEADS, KERNEL)
            dh = D // nh
            qkv = xs @ qkv_w.T + qkv_b
            qkv = qkv.reshape(H, W, 3, nh, dh).transpose(2, 3, 0, 1, 4)
            q, kmat, vmat = (qkv[0], qkv[1], qkv[2])
            q = q * dh ** (-0.5)
            sh = _window_starts(H, k)
            sw = _window_starts(W, k)
            off = jnp.arange(k)
            idx_h = sh[:, None] + off[None, :]
            idx_w = sw[:, None] + off[None, :]
            kk = kmat[:, idx_h][:, :, :, idx_w]
            vv = vmat[:, idx_h][:, :, :, idx_w]
            logits = jnp.einsum('nhwd,nhawbd->nhwab', q, kk)
            bh = idx_h - jnp.arange(H)[:, None] + (k - 1)
            bw = idx_w - jnp.arange(W)[:, None] + (k - 1)
            bias = rpb[:, bh[:, None, :, None], bw[None, :, None, :]]
            logits = logits + bias
            attn = jax.nn.softmax(logits.reshape(nh, H, W, k * k), axis=-1).reshape(nh, H, W, k, k)
            out = jnp.einsum('nhwab,nhawbd->nhwd', attn, vv)
            out = out.transpose(1, 2, 0, 3).reshape(H, W, D)
            return out @ proj_w.T + proj_b
        H, W = (96, 96)
        IN_D, HID, OUT_D = (192, 96, 192)
        key = jax.random.key(seed)
        ks = jax.random.split(key, 16)
        s = 0.02
        return {'x': jax.random.normal(ks[0], (H, W, IN_D), dtype=jnp.float32), 'fc1_w': jax.random.normal(ks[1], (HID, IN_D), dtype=jnp.float32) * s, 'fc1_b': jnp.zeros((HID,), dtype=jnp.float32), 'convA_w': jax.random.normal(ks[2], (64, HID), dtype=jnp.float32) * s, 'convA_b': jnp.zeros((64,), dtype=jnp.float32), 'convB_w': jax.random.normal(ks[3], (HID, 64), dtype=jnp.float32) * s, 'convB_b': jnp.zeros((HID,), dtype=jnp.float32), 'qkv_w': jax.random.normal(ks[4], (3 * HID, HID), dtype=jnp.float32) * s, 'qkv_b': jnp.zeros((3 * HID,), dtype=jnp.float32), 'rpb': jax.random.normal(ks[5], (NUM_HEADS, 2 * KERNEL - 1, 2 * KERNEL - 1), dtype=jnp.float32) * s, 'proj_w': jax.random.normal(ks[6], (HID, HID), dtype=jnp.float32) * s, 'proj_b': jnp.zeros((HID,), dtype=jnp.float32), 'fc2_w': jax.random.normal(ks[7], (OUT_D, HID), dtype=jnp.float32) * s, 'fc2_b': jnp.zeros((OUT_D,), dtype=jnp.float32)}
    _L1_attn_all = _L1_attn_setup()
    _L1_attn_in = {k: v for k, v in _L1_attn_all.items() if k in ('fc1_w', 'fc1_b', 'convA_w', 'convA_b', 'convB_w', 'convB_b', 'qkv_w', 'qkv_b', 'rpb', 'proj_w', 'proj_b', 'fc2_w', 'fc2_b')}
    del _L1_attn_all

    def _L1_ffn_setup():
        import jax, jax.numpy as jnp
        import numpy as np
        H = 192
        I = 96
        E = 16
        G = 4
        TOPK_GROUP = 2
        TOP_K = 4
        SCALE = 2.5
        N_SHARED = 2
        IS = I * N_SHARED
        B, S = (1, 512)

        def _route(x, router_w, router_b, corr_bias):
            logits = x.astype(jnp.float32) @ router_w.T + router_b
            scores = jax.nn.sigmoid(logits)
            sfc = scores + corr_bias[None, :]
            grp = sfc.reshape(-1, G, E // G)
            group_scores = jax.lax.top_k(grp, 2)[0].sum(-1)
            _, gidx = jax.lax.top_k(group_scores, TOPK_GROUP)
            gmask = jax.nn.one_hot(gidx, G, dtype=sfc.dtype).sum(axis=1)
            score_mask = jnp.repeat(gmask, E // G, axis=-1)
            sfc = jnp.where(score_mask > 0, sfc, 0.0)
            _, idx = jax.lax.top_k(sfc, TOP_K)
            w = jnp.take_along_axis(scores, idx, axis=1)
            w = w / (w.sum(-1, keepdims=True) + 1e-20)
            return (idx, w * SCALE)

        def _forward(x3, router_w, router_b, corr_bias, gWg, gbg, gWu, gbu, gWd, gbd, sWg, sbg, sWu, sbu, sWd, sbd):
            orig_shape = x3.shape
            x = x3.reshape(-1, H)
            idx, w = _route(x, router_w, router_b, corr_bias)
            c = (jax.nn.one_hot(idx, E, dtype=w.dtype) * w[..., None]).sum(1)
            h = jax.nn.silu(jnp.einsum('th,ehi->tei', x, gWg) + gbg) * (jnp.einsum('th,ehi->tei', x, gWu) + gbu)
            out_e = jnp.einsum('tei,eih->teh', h, gWd) + gbd
            moe_out = jnp.einsum('te,teh->th', c, out_e)
            hs = jax.nn.silu(x @ sWg + sbg) * (x @ sWu + sbu)
            shared = hs @ sWd + sbd
            return (moe_out + shared).reshape(orig_shape)
        key = jax.random.key(seed)
        ks = jax.random.split(key, 16)
        s = lambda k, shape, fan: jax.random.normal(k, shape, jnp.float32) * fan ** (-0.5)
        return {'hidden_states': jax.random.normal(ks[0], (B, S, H), jnp.float32), 'router_w': s(ks[1], (E, H), H), 'router_b': jnp.zeros((E,), jnp.float32), 'corr_bias': jnp.zeros((E,), jnp.float32), 'gWg': s(ks[2], (E, H, I), H), 'gbg': jnp.zeros((E, I), jnp.float32), 'gWu': s(ks[3], (E, H, I), H), 'gbu': jnp.zeros((E, I), jnp.float32), 'gWd': s(ks[4], (E, I, H), I), 'gbd': jnp.zeros((E, H), jnp.float32), 'sWg': s(ks[5], (H, IS), H), 'sbg': jnp.zeros((IS,), jnp.float32), 'sWu': s(ks[6], (H, IS), H), 'sbu': jnp.zeros((IS,), jnp.float32), 'sWd': s(ks[7], (IS, H), IS), 'sbd': jnp.zeros((H,), jnp.float32)}
    _L1_ffn_all = _L1_ffn_setup()
    _L1_ffn_in = {k: v for k, v in _L1_ffn_all.items() if k in ('router_w', 'router_b', 'corr_bias', 'gWg', 'gbg', 'gWu', 'gbu', 'gWd', 'gbd', 'sWg', 'sbg', 'sWu', 'sbu', 'sWd', 'sbd')}
    del _L1_ffn_all
    return {'x': x, 'txt': txt, 'L0_tok_patch_w': _L0_tok_in['patch_w'], 'L0_tok_patch_b': _L0_tok_in['patch_b'], 'L0_tok_ln_g': _L0_tok_in['ln_g'], 'L0_tok_ln_b': _L0_tok_in['ln_b'], 'L0_tok_qkv_w': _L0_tok_in['qkv_w'], 'L0_tok_qkv_b': _L0_tok_in['qkv_b'], 'L0_tok_proj_w': _L0_tok_in['proj_w'], 'L0_tok_proj_b': _L0_tok_in['proj_b'], 'L0_tok_ff1_w': _L0_tok_in['ff1_w'], 'L0_tok_ff1_b': _L0_tok_in['ff1_b'], 'L0_tok_ff2_w': _L0_tok_in['ff2_w'], 'L0_tok_ff2_b': _L0_tok_in['ff2_b'], 'L0_attn_w_qkv': _L0_attn_in['w_qkv'], 'L0_attn_w_proj': _L0_attn_in['w_proj'], 'L0_attn_b_proj': _L0_attn_in['b_proj'], 'L0_attn_temperature': _L0_attn_in['temperature'], 'L0_ffn_W1': _L0_ffn_in['W1'], 'L0_ffn_b1': _L0_ffn_in['b1'], 'L0_ffn_W2': _L0_ffn_in['W2'], 'L0_ffn_b2': _L0_ffn_in['b2'], 'L0_ffn_Wg': _L0_ffn_in['Wg'], 'L0_ffn_bg': _L0_ffn_in['bg'], 'L1_attn_fc1_w': _L1_attn_in['fc1_w'], 'L1_attn_fc1_b': _L1_attn_in['fc1_b'], 'L1_attn_convA_w': _L1_attn_in['convA_w'], 'L1_attn_convA_b': _L1_attn_in['convA_b'], 'L1_attn_convB_w': _L1_attn_in['convB_w'], 'L1_attn_convB_b': _L1_attn_in['convB_b'], 'L1_attn_qkv_w': _L1_attn_in['qkv_w'], 'L1_attn_qkv_b': _L1_attn_in['qkv_b'], 'L1_attn_rpb': _L1_attn_in['rpb'], 'L1_attn_proj_w': _L1_attn_in['proj_w'], 'L1_attn_proj_b': _L1_attn_in['proj_b'], 'L1_attn_fc2_w': _L1_attn_in['fc2_w'], 'L1_attn_fc2_b': _L1_attn_in['fc2_b'], 'L1_ffn_router_w': _L1_ffn_in['router_w'], 'L1_ffn_router_b': _L1_ffn_in['router_b'], 'L1_ffn_corr_bias': _L1_ffn_in['corr_bias'], 'L1_ffn_gWg': _L1_ffn_in['gWg'], 'L1_ffn_gbg': _L1_ffn_in['gbg'], 'L1_ffn_gWu': _L1_ffn_in['gWu'], 'L1_ffn_gbu': _L1_ffn_in['gbu'], 'L1_ffn_gWd': _L1_ffn_in['gWd'], 'L1_ffn_gbd': _L1_ffn_in['gbd'], 'L1_ffn_sWg': _L1_ffn_in['sWg'], 'L1_ffn_sbg': _L1_ffn_in['sbg'], 'L1_ffn_sWu': _L1_ffn_in['sWu'], 'L1_ffn_sbu': _L1_ffn_in['sbu'], 'L1_ffn_sWd': _L1_ffn_in['sWd'], 'L1_ffn_sbd': _L1_ffn_in['sbd']}

def reference(x, txt, L0_tok_patch_w, L0_tok_patch_b, L0_tok_ln_g, L0_tok_ln_b, L0_tok_qkv_w, L0_tok_qkv_b, L0_tok_proj_w, L0_tok_proj_b, L0_tok_ff1_w, L0_tok_ff1_b, L0_tok_ff2_w, L0_tok_ff2_b, L0_attn_w_qkv, L0_attn_w_proj, L0_attn_b_proj, L0_attn_temperature, L0_ffn_W1, L0_ffn_b1, L0_ffn_W2, L0_ffn_b2, L0_ffn_Wg, L0_ffn_bg, L1_attn_fc1_w, L1_attn_fc1_b, L1_attn_convA_w, L1_attn_convA_b, L1_attn_convB_w, L1_attn_convB_b, L1_attn_qkv_w, L1_attn_qkv_b, L1_attn_rpb, L1_attn_proj_w, L1_attn_proj_b, L1_attn_fc2_w, L1_attn_fc2_b, L1_ffn_router_w, L1_ffn_router_b, L1_ffn_corr_bias, L1_ffn_gWg, L1_ffn_gbg, L1_ffn_gWu, L1_ffn_gbu, L1_ffn_gWd, L1_ffn_gbd, L1_ffn_sWg, L1_ffn_sbg, L1_ffn_sWu, L1_ffn_sbu, L1_ffn_sWd, L1_ffn_sbd):
    import jax
    import jax.numpy as jnp

    def _L0_tok_ref(input, patch_w, patch_b, ln_g, ln_b, qkv_w, qkv_b, proj_w, proj_b, ff1_w, ff1_b, ff2_w, ff2_b):
        import jax, jax.numpy as jnp
        import numpy as np
        P = 16
        WIN = 64
        NH = 12

        def _layernorm(x, g, b, eps=1e-05):
            m = x.mean(-1, keepdims=True)
            v = ((x - m) ** 2).mean(-1, keepdims=True)
            return (x - m) * jax.lax.rsqrt(v + eps) * g + b

        def _sinusoidal_pe(n, d):
            pos = jnp.arange(n, dtype=jnp.float32)[:, None]
            i = jnp.arange(d // 2, dtype=jnp.float32)[None, :]
            ang = pos / jnp.power(10000.0, 2.0 * i / d)
            pe = jnp.zeros((n, d), jnp.float32)
            pe = pe.at[:, 0::2].set(jnp.sin(ang)).at[:, 1::2].set(jnp.cos(ang))
            return pe
        B, C, H, W = input.shape
        D = patch_w.shape[0]
        dh = D // NH
        xp = input.reshape(B, C, H // P, P, W // P, P)
        x = jnp.einsum('bchpwq,dcpq->bhwd', xp, patch_w) + patch_b
        x = x.reshape(B, -1, D)
        x = _layernorm(x, ln_g, ln_b)
        N = x.shape[1]
        x = x + _sinusoidal_pe(N, D)

        def ff(y):
            return jax.nn.gelu(y @ ff1_w + ff1_b) @ ff2_w + ff2_b

        def sparse_attn(y):
            nW = N // WIN
            qkv = (y @ qkv_w + qkv_b).reshape(B, nW, WIN, 3, NH, dh)
            q, k, v = (qkv[:, :, :, 0], qkv[:, :, :, 1], qkv[:, :, :, 2])
            scores = jnp.einsum('bwqhd,bwkhd->bwhqk', q, k) * dh ** (-0.5)
            a = jax.nn.softmax(scores, axis=-1)
            o = jnp.einsum('bwhqk,bwkhd->bwqhd', a, v).reshape(B, N, D)
            return o @ proj_w + proj_b
        identity = x
        x = ff(x)
        x = sparse_attn(x)
        x = x + identity
        identity = x
        x = ff(x)
        x = x + identity
        return x

    def _L0_attn_ref(x, w_qkv, w_proj, b_proj, temperature):
        import jax, jax.numpy as jnp
        import numpy as np
        B, N, C, H = (4, 512, 192, 12)
        D = C // H
        SCALE = D ** (-0.5)
        b, n, c = x.shape
        h, d = (H, c // H)
        qkv = (x @ w_qkv).reshape(b, n, 3, h, d)
        q, k, v = jnp.moveaxis(qkv, 2, 0)
        q = q.transpose(0, 2, 1, 3)
        k = k.transpose(0, 2, 1, 3)
        v = v.transpose(0, 2, 1, 3)
        attn = jnp.einsum('bhnd,bhmd->bhnm', q, k) * SCALE
        eye = jnp.eye(n, dtype=attn.dtype)
        attn = attn * (1.0 - temperature[None] * eye)
        attn = jax.nn.softmax(attn, axis=-1)
        out = jnp.einsum('bhnm,bhmd->bhnd', attn, v)
        out = out.transpose(0, 2, 1, 3).reshape(b, n, c)
        return out @ w_proj + b_proj

    def _L0_ffn_ref(x, W1, b1, W2, b2, Wg, bg):
        import jax, jax.numpy as jnp
        import numpy as np
        E, D, H = (16, 192, 192)
        B, N = (32, 197)
        Bx, Nx, Dx = x.shape
        t = x.reshape(-1, Dx)
        logits = t @ Wg.T + bg
        idx = jnp.argmax(logits, axis=-1)
        out = jnp.zeros_like(t)
        for e in range(W1.shape[0]):
            mask = (idx == e).astype(t.dtype)[:, None]
            h = jax.nn.gelu(t @ W1[e].T + b1[e], approximate=False)
            y = h @ W2[e].T + b2[e]
            out = out + mask * y
        return out.reshape(Bx, Nx, Dx)

    def _L1_attn_ref(x, fc1_w, fc1_b, convA_w, convA_b, convB_w, convB_b, qkv_w, qkv_b, rpb, proj_w, proj_b, fc2_w, fc2_b):
        import jax, jax.numpy as jnp
        import numpy as np
        KERNEL = 5
        NUM_HEADS = 4

        def _window_starts(L, k):
            pad = k // 2
            return jnp.clip(jnp.arange(L) - pad, 0, L - k)

        def _neighborhood_attention_2d(xs, qkv_w, qkv_b, rpb, proj_w, proj_b):
            H, W, D = xs.shape
            nh, k = (NUM_HEADS, KERNEL)
            dh = D // nh
            qkv = xs @ qkv_w.T + qkv_b
            qkv = qkv.reshape(H, W, 3, nh, dh).transpose(2, 3, 0, 1, 4)
            q, kmat, vmat = (qkv[0], qkv[1], qkv[2])
            q = q * dh ** (-0.5)
            sh = _window_starts(H, k)
            sw = _window_starts(W, k)
            off = jnp.arange(k)
            idx_h = sh[:, None] + off[None, :]
            idx_w = sw[:, None] + off[None, :]
            kk = kmat[:, idx_h][:, :, :, idx_w]
            vv = vmat[:, idx_h][:, :, :, idx_w]
            logits = jnp.einsum('nhwd,nhawbd->nhwab', q, kk)
            bh = idx_h - jnp.arange(H)[:, None] + (k - 1)
            bw = idx_w - jnp.arange(W)[:, None] + (k - 1)
            bias = rpb[:, bh[:, None, :, None], bw[None, :, None, :]]
            logits = logits + bias
            attn = jax.nn.softmax(logits.reshape(nh, H, W, k * k), axis=-1).reshape(nh, H, W, k, k)
            out = jnp.einsum('nhwab,nhawbd->nhwd', attn, vv)
            out = out.transpose(1, 2, 0, 3).reshape(H, W, D)
            return out @ proj_w.T + proj_b
        xs = x @ fc1_w.T + fc1_b
        a = xs @ convA_w.T + convA_b
        b = a @ convB_w.T + convB_b
        xs = b * 1.0 + xs
        xs = jax.nn.gelu(xs, approximate=False)
        xs = _neighborhood_attention_2d(xs, qkv_w, qkv_b, rpb, proj_w, proj_b)
        xs = xs @ fc2_w.T + fc2_b
        return x + xs

    def _L1_ffn_ref(hidden_states, router_w, router_b, corr_bias, gWg, gbg, gWu, gbu, gWd, gbd, sWg, sbg, sWu, sbu, sWd, sbd):
        import jax, jax.numpy as jnp
        import numpy as np
        H = 192
        I = 96
        E = 16
        G = 4
        TOPK_GROUP = 2
        TOP_K = 4
        SCALE = 2.5
        N_SHARED = 2
        IS = I * N_SHARED
        B, S = (1, 512)

        def _route(x, router_w, router_b, corr_bias):
            logits = x.astype(jnp.float32) @ router_w.T + router_b
            scores = jax.nn.sigmoid(logits)
            sfc = scores + corr_bias[None, :]
            grp = sfc.reshape(-1, G, E // G)
            group_scores = jax.lax.top_k(grp, 2)[0].sum(-1)
            _, gidx = jax.lax.top_k(group_scores, TOPK_GROUP)
            gmask = jax.nn.one_hot(gidx, G, dtype=sfc.dtype).sum(axis=1)
            score_mask = jnp.repeat(gmask, E // G, axis=-1)
            sfc = jnp.where(score_mask > 0, sfc, 0.0)
            _, idx = jax.lax.top_k(sfc, TOP_K)
            w = jnp.take_along_axis(scores, idx, axis=1)
            w = w / (w.sum(-1, keepdims=True) + 1e-20)
            return (idx, w * SCALE)

        def _forward(x3, router_w, router_b, corr_bias, gWg, gbg, gWu, gbu, gWd, gbd, sWg, sbg, sWu, sbu, sWd, sbd):
            orig_shape = x3.shape
            x = x3.reshape(-1, H)
            idx, w = _route(x, router_w, router_b, corr_bias)
            c = (jax.nn.one_hot(idx, E, dtype=w.dtype) * w[..., None]).sum(1)
            h = jax.nn.silu(jnp.einsum('th,ehi->tei', x, gWg) + gbg) * (jnp.einsum('th,ehi->tei', x, gWu) + gbu)
            out_e = jnp.einsum('tei,eih->teh', h, gWd) + gbd
            moe_out = jnp.einsum('te,teh->th', c, out_e)
            hs = jax.nn.silu(x @ sWg + sbg) * (x @ sWu + sbu)
            shared = hs @ sWd + sbd
            return (moe_out + shared).reshape(orig_shape)
        return _forward(hidden_states, router_w, router_b, corr_bias, gWg, gbg, gWu, gbu, gWd, gbd, sWg, sbg, sWu, sbu, sWd, sbd)
    h = _L0_tok_ref(x, L0_tok_patch_w, L0_tok_patch_b, L0_tok_ln_g, L0_tok_ln_b, L0_tok_qkv_w, L0_tok_qkv_b, L0_tok_proj_w, L0_tok_proj_b, L0_tok_ff1_w, L0_tok_ff1_b, L0_tok_ff2_w, L0_tok_ff2_b)
    h = jnp.concatenate([h, txt], axis=1)
    h = h + _L0_attn_ref(_layernorm(h, axis=-1), L0_attn_w_qkv, L0_attn_w_proj, L0_attn_b_proj, L0_attn_temperature)
    h = h + _L0_ffn_ref(_layernorm(h, axis=-1), L0_ffn_W1, L0_ffn_b1, L0_ffn_W2, L0_ffn_b2, L0_ffn_Wg, L0_ffn_bg)
    h = h + _L1_attn_ref(_layernorm(h, axis=-1), L1_attn_fc1_w, L1_attn_fc1_b, L1_attn_convA_w, L1_attn_convA_b, L1_attn_convB_w, L1_attn_convB_b, L1_attn_qkv_w, L1_attn_qkv_b, L1_attn_rpb, L1_attn_proj_w, L1_attn_proj_b, L1_attn_fc2_w, L1_attn_fc2_b)
    h = h + _L1_ffn_ref(_layernorm(h, axis=-1), L1_ffn_router_w, L1_ffn_router_b, L1_ffn_corr_bias, L1_ffn_gWg, L1_ffn_gbg, L1_ffn_gWu, L1_ffn_gbu, L1_ffn_gWd, L1_ffn_gbd, L1_ffn_sWg, L1_ffn_sbg, L1_ffn_sWu, L1_ffn_sbu, L1_ffn_sWd, L1_ffn_sbd)
    return h

_drawn_inputs = setup_inputs


def setup_inputs(seed=0):
    import zlib

    import numpy as np

    out = dict(_drawn_inputs(seed))
    spreads = {'L0_tok_patch_b': (0.0, 0.1),
     'L0_tok_ln_g': (1.0, 0.2),
     'L0_tok_ln_b': (0.0, 0.1),
     'L0_tok_qkv_b': (0.0, 0.1),
     'L0_tok_proj_b': (0.0, 0.1),
     'L0_tok_ff1_b': (0.0, 0.1),
     'L0_tok_ff2_b': (0.0, 0.1),
     'L0_attn_b_proj': (0.0, 0.1),
     'L0_attn_temperature': (0.5, 0.6),
     'L0_ffn_bg': (0.0, 0.1),
     'L1_attn_fc1_b': (0.0, 0.8),
     'L1_attn_convA_b': (0.0, 0.8),
     'L1_attn_convB_b': (0.0, 0.8),
     'L1_attn_qkv_b': (0.0, 0.501),
     'L1_attn_proj_b': (0.0, 0.343),
     'L1_attn_fc2_b': (0.0, 0.1),
     'L1_ffn_router_b': (0.0, 0.1),
     'L1_ffn_corr_bias': (0.0, 0.1),
     'L1_ffn_gbg': (0.0, 0.1),
     'L1_ffn_gbu': (0.0, 0.268),
     'L1_ffn_gbd': (0.0, 0.1),
     'L1_ffn_sbg': (0.0, 0.358),
     'L1_ffn_sbu': (0.0, 0.307),
     'L1_ffn_sbd': (0.0, 0.1)}
    factors = {'L0_tok_qkv_w': 2.918,
     'L0_ffn_b1': 3.916,
     'L1_attn_fc1_w': 8.0,
     'L1_attn_convA_w': 8.0,
     'L1_attn_convB_w': 8.0,
     'L1_attn_qkv_w': 8.0,
     'L1_attn_rpb': 24.376,
     'L1_attn_proj_w': 4.651}
    for name, (base, spread) in spreads.items():
        noise = np.random.default_rng([zlib.crc32(name.encode()), seed]).standard_normal(out[name].shape)
        drawn = base * np.exp(spread * noise) if base else spread * noise
        out[name] = jnp.asarray(drawn.astype(out[name].dtype))
    for name, factor in factors.items():
        out[name] = (out[name] * factor).astype(out[name].dtype)
    return out
```

```python
import concourse.bass as bass
from concourse import mybir
from contextlib import ExitStack
import numpy as np

F32 = mybir.dt.float32
U32 = mybir.dt.uint32
I32 = mybir.dt.int32
ALU = mybir.AluOpType
ACT = mybir.ActivationFunctionType
AX = mybir.AxisListType
ds = bass.ds

B = 16
NI, NT = 64, 32
NA = NI + NT
D = 192
HALF = 96
FF = 768
KC = FF // 128
NH = 12
DH = D // NH
QUADS = NH // 4
TOK = B * NA
NTILE = TOK // 128
E = 16
SORT_TILES = TOK // 128 + E - 1
EPS = 1e-5
WIN = 5
NH2, DH2 = 4, 24
HID = 96
QR, QC = 8, 16
KR, KCOL = 10, 20
NKEY = KR * KCOL
HKEY = NKEY // 2
COLS = NA // QC
PAIRS = E // 2 + 1
I2 = 96


def steady(eng, step, n, first, last):
    assert first % 2 == 0 and (last - first) % 2 == 0 and first >= 2
    for s in range(first):
        step(s, s % 2)
    with eng.Fori(first // 2, last // 2) as i:
        step(2 * i, 0)
        step(2 * i + 1, 1)
    for s in range(last, n):
        step(s, s % 2)


def within(s, n):
    return 0 <= s < n if isinstance(s, int) else True


def wait(eng, sem, value):
    if not isinstance(value, int) or value > 0:
        eng.wait_ge(sem, value)


class Scope:

    def __init__(self, W, ctx, tag):
        self.nc, self.whole, self.ctx, self.tag = W["nc"], W["whole"], ctx, tag

    def sb(self, name, shape, dt=F32):
        return self.ctx.enter_context(self.nc.sbuf_tensor(f"{self.tag}_{name}", shape, dt))

    def sem(self, name):
        return self.whole.enter_context(self.nc.semaphore(f"{self.tag}_{name}"))


def norm_stats(nc, dve, mv, st, n):
    sv = st[:, 0:6 * n].rearrange("p (n s) -> p n s", s=6)
    mean, var, dif = mv[:, 0:n], mv[:, n:2 * n], mv[:, 2 * n:3 * n]
    dve.drain()
    nc.vector.tensor_tensor(mean, sv[:, :, 1], sv[:, :, 4], ALU.add)
    nc.vector.tensor_tensor(dif, sv[:, :, 1], sv[:, :, 4], ALU.subtract)
    nc.vector.tensor_tensor(var, sv[:, :, 2], sv[:, :, 5], ALU.add)
    dve.drain()
    nc.vector.tensor_scalar(mean, mean, 0.5, None, ALU.mult)
    nc.vector.tensor_scalar(var, var, 1.0 / D, EPS, ALU.mult, ALU.add)
    nc.vector.tensor_tensor(dif, dif, dif, ALU.mult)
    dve.drain()
    return nc.vector.scalar_tensor_tensor(var, dif, 0.25, var, ALU.mult, ALU.add)


def embed(nc, W, ps, x_dram, x0T):
    with ExitStack() as ctx:
        S = Scope(W, ctx, "em")
        n = B * NI // 128
        xt = [S.sb(f"xt{p}", [128, KC * 128]) for p in range(2)]
        t1 = S.sb("t1", [128, D])
        x0 = [S.sb(f"x0{p}", [128, D]) for p in range(2)]
        st = S.sb("st", [128, 6])
        mv = S.sb("mv", [128, 2])
        rs = S.sb("rs", [128, 1])
        loaded = [S.sem(f"loaded{p}") for p in range(2)]
        patched, var_ready, rstd_ready, x0_ready, turned, x0T_ready = map(
            S.sem, ["patched", "var_ready", "rstd_ready", "x0_ready", "turned", "x0T_ready"])
        block = ctx.enter_context(nc.Block())

        @block.sync
        def _(sp):
            def step(s, p):
                wait(sp, patched, s - 1)
                sp.dma_start(xt[p][:, :], x_dram[:, ds(s * KC * 128, KC * 128)]).then_inc(loaded[p], 16)
            steady(sp, step, n, 2, n)

        @block.tensor
        def _(pe):
            pe.wait_ge(W["sem"]["embed"], W["count"]["embed"])
            pe.wait_ge(W["sem"]["ident"], 16)

            def step(s, p):
                if within(s, n):
                    pe.wait_ge(loaded[p], 8 * (s - p) + 16)
                    for k in range(KC):
                        mm = nc.tensor.matmul(ps[:, p, 0:D], xt[p][:, 128 * k:128 * k + 128],
                                              W["pw"][:, k * D:k * D + D], start=k == 0, stop=k == KC - 1)
                    mm.then_inc(patched, 1)
                if within(s - 1, n):
                    wait(pe, x0_ready, s)
                    wait(pe, x0T_ready, s - 2)
                    for k in range(2):
                        mm = nc.tensor.transpose(ps[0:HALF, 3 - p, 128 * k:128 * k + 128],
                                                 x0[1 - p][:, HALF * k:HALF * k + HALF], W["ident"][:, :])
                    mm.then_inc(turned, 1)
            steady(pe, step, n + 1, 2, n)

        @block.gpsimd
        def _(pool):
            def step(s, p):
                pool.wait_ge(var_ready, s + 1)
                nc.gpsimd.tensor_tensor(rs[:, :], mv[:, 1:2], W["mhalf"][:, 0:1], ALU.pow).then_inc(rstd_ready, 1)
            steady(pool, step, n, 2, n)

        @block.vector
        def _(dve):
            def step(s, p):
                dve.wait_ge(patched, s + 1)
                nc.vector.tensor_tensor(t1[:, :], ps[:, p, 0:D], W["pb"][:, :], ALU.add)
                dve.drain()
                nc.vector.bn_stats(st[:, :], t1[:, :])
                dve.drain()
                nc.vector.bn_aggr(mv[:, :], st[:, :])
                dve.drain()
                nc.vector.tensor_scalar(mv[:, 1:2], mv[:, 1:2], EPS, None, ALU.add).then_inc(var_ready, 1)
                dve.wait_ge(rstd_ready, s + 1)
                wait(dve, turned, s - 1)
                nc.vector.tensor_scalar(x0[p][:, :], t1[:, :], mv[:, 0:1], rs[:, :], ALU.subtract, ALU.mult)
                dve.drain()
                nc.vector.tensor_tensor(x0[p][:, :], x0[p][:, :], W["lng"][:, :], ALU.mult)
                dve.drain()
                nc.vector.tensor_tensor(x0[p][:, :], x0[p][:, :], W["lnbpe"][:, :], ALU.add).then_inc(x0_ready, 1)
            dve.wait_ge(W["sem"]["embed"], W["count"]["embed"])
            nc.vector.tensor_tensor(W["lnbpe"][:, :], W["lnb"][:, :], W["pe"][:, :], ALU.add)
            dve.drain()
            steady(dve, step, n, 2, n)

        @block.scalar
        def _(act):
            def step(s, p):
                act.wait_ge(turned, s + 1)
                for k in range(2):
                    cp = nc.scalar.copy(x0T[:, ds(k * B * NI + 128 * s, 128)],
                                        ps[0:HALF, 2 + p, 128 * k:128 * k + 128])
                cp.then_inc(x0T_ready, 1)
            steady(act, step, n, 2, n)


def feed_forward(nc, W, ps, tag, xin, out, res, h96=None):
    with ExitStack() as ctx:
        S = Scope(W, ctx, tag)
        N = B * NI // 2
        T = B * NI
        g = [S.sb(f"g{c}", [128, KC * N]) for c in range(2)]
        hidden, gelu_done, summed, out_ready, turned, h_ready = map(
            S.sem, ["hidden", "gelu_done", "summed", "out_ready", "turned", "h_ready"])
        block = ctx.enter_context(nc.Block())

        @block.tensor
        def _(pe):
            pe.wait_ge(W["sem"]["ff"], W["count"]["ff"])

            def up(c):
                for f in range(KC):
                    i = c * KC + f
                    wait(pe, gelu_done, i - 3)
                    for k in range(2):
                        mm = nc.tensor.matmul(ps[:, i % 4, :], W["ff1"][:, k * FF + 128 * f:k * FF + 128 * f + 128],
                                              xin[0:HALF, k * T + c * N:k * T + c * N + N],
                                              start=k == 0, stop=k == 1)
                    mm.then_inc(hidden, 1)

            def down(c):
                pe.wait_ge(gelu_done, KC * (c + 1))
                for m in range(2):
                    for f in range(KC):
                        mm = nc.tensor.matmul(ps[0:HALF, 4 + 2 * c + m, :],
                                              W["ff2"][:, f * D + HALF * m:f * D + HALF * m + HALF],
                                              g[c][:, f * N:f * N + N], start=f == 0, stop=f == KC - 1)
                    mm.then_inc(summed, 1)
            up(0)
            up(1)
            down(0)
            down(1)
            if h96 is not None:
                for b in range(0, B, 2):
                    i = b // 2
                    pe.wait_ge(out_ready, 2 if b < B // 2 else 4)
                    wait(pe, h_ready, i - 3)
                    for j in range(2):
                        for k in range(2):
                            mm = nc.tensor.transpose(ps[0:NI, i % 4, D * j + HALF * k:D * j + HALF * k + HALF],
                                                     out[0:HALF, k * T + NI * (b + j):k * T + NI * (b + j) + NI],
                                                     W["ident"][0:HALF, 0:HALF])
                    mm.then_inc(turned, 1)

        @block.scalar
        def _(act):
            for c in range(2):
                for f in range(KC):
                    i = c * KC + f
                    act.wait_ge(hidden, i + 1)
                    nc.scalar.activation(g[c][:, f * N:f * N + N], ps[:, i % 4, :], ACT.Gelu_apprx_tanh,
                                         bias=W["ff1b"][:, f:f + 1]).then_inc(gelu_done, 1)

        @block.vector
        def _(dve):
            for c in range(2):
                for m in range(2):
                    dve.wait_ge(summed, 2 * c + m + 1)
                    src = ps[0:HALF, 4 + 2 * c + m, :]
                    at = slice(m * T + c * N, m * T + c * N + N)
                    if res is None:
                        nc.vector.tensor_scalar(out[0:HALF, at], src, W["ff2b"][:, m:m + 1], None,
                                                ALU.add).then_inc(out_ready, 1)
                    else:
                        nc.vector.scalar_tensor_tensor(out[0:HALF, at], src, W["ff2b"][:, m:m + 1],
                                                       res[0:HALF, at], ALU.add, ALU.add).then_inc(out_ready, 1)
            if h96 is not None:
                for i in range(B // 2):
                    dve.wait_ge(turned, i + 1)
                    nc.vector.tensor_copy(h96[0:NI, 2 * D * i:2 * D * i + 2 * D],
                                          ps[0:NI, i % 4, 0:2 * D]).then_inc(h_ready, 1)


def attention(nc, W, ps, tag, T, w, yT, x0T, x1T, h96, h_dram):
    full = h96 is not None
    n = B if full else B * NI // T
    TI = B * NI
    with ExitStack() as ctx:
        S = Scope(W, ctx, tag)
        xb = [S.sb(f"xb{p}", [HALF + 1, 2 * T]) for p in range(2)]
        qs = [S.sb(f"qs{p}", [128, QUADS * T]) for p in range(2)]
        ks = [S.sb(f"ks{p}", [128, QUADS * T]) for p in range(2)]
        v = [S.sb(f"v{p}", [T, NH * (DH + 1)]) for p in range(2)]
        p_ = S.sb("p", [T, NH * T])
        pT = S.sb("pT", [T, NH * T])
        nmax = S.sb("nmax", [T, NH])
        rec = S.sb("rec", [T, NH])
        on = S.sb("on", [T, D])
        oT = S.sb("oT", [HALF + 1, 2 * T])
        (xb_ready, qkv_done, q_ready, k_ready, v_ready, scored, shifted, exp_done, p_turned, pT_act, pT_dve,
         weighed, on_ready, o_turned, oT_ready, projected, added, ones_set) = map(S.sem, [
             "xb_ready", "qkv_done", "q_ready", "k_ready", "v_ready", "scored", "shifted", "exp_done",
             "p_turned", "pT_act", "pT_dve", "weighed", "on_ready", "o_turned", "oT_ready", "projected",
             "added", "ones_set"])
        if full:
            xn_ready, x_turned, stored, stat_done, rstd_ready = map(
                S.sem, ["xn_ready", "x_turned", "stored", "stat_done", "rstd_ready"])
            dm = S.sb("dm", [T, NH * T])
            ntemp = S.sb("ntemp", [T, NH])
            xn = [S.sb(f"xn{p}", [T, D]) for p in range(2)]
            st = S.sb("st", [T, 6 * B])
            mv = S.sb("mv", [T, 3 * B])
            rs = S.sb("rs", [T, B])
        scores = ps[0:T, 0:4, 0:QUADS * T]
        bq, bk, bo, bt = 4, 5, 6, 7
        XC = QUADS * NA
        VC = 2 * T
        block = ctx.enter_context(nc.Block())

        if full:
            @block.sync
            def _(sp):
                def step(s, p):
                    sp.wait_ge(added, s + 1)
                    sp.dma_start(h_dram[ds(s * NA, NA), :], h96[:, ds(s * D, D)]).then_inc(stored, 16)
                steady(sp, step, B, 2, B)
                sp.wait_ge(stored, 16 * B)

        @block.gpsimd
        def _(pool):
            if full:
                pool.wait_ge(stat_done, 1)
                nc.gpsimd.tensor_tensor(rs[:, :], mv[:, B:2 * B], W["mhalf"][0:T, 0:1].broadcast_to([T, B]),
                                        ALU.pow).then_inc(rstd_ready, 1)
            else:
                def step(s, p):
                    wait(pool, qkv_done, s - 1)
                    for k in range(2):
                        cp = nc.gpsimd.tensor_copy(xb[p][0:HALF, T * k:T * k + T], yT[:, ds(k * TI + s * T, T)])
                    cp.then_inc(xb_ready, 1)
                steady(pool, step, n, 2, n)

        @block.tensor
        def _(pe):
            pe.wait_ge(ones_set, 5)
            pe.wait_ge(W["sem"][w], W["count"][w])

            def front(b, p):
                if full:
                    pe.wait_ge(xn_ready, b + 1)
                    for k in range(2):
                        mm = nc.tensor.transpose(ps[0:HALF, bk, XC + T * k:XC + T * k + T],
                                                 xn[p][:, HALF * k:HALF * k + HALF], W["ident"][0:T, 0:T])
                    mm.then_inc(x_turned, 1)
                pe.wait_ge(xb_ready, b + 1)
                for at, bank in ((0, bq), (QUADS * 128, bk)):
                    for g in range(QUADS):
                        for k in range(2):
                            mm = nc.tensor.matmul(ps[:, bank, T * g:T * g + T],
                                                  W["qk"][w][0:HALF + k, k * 768 + at + 128 * g:k * 768 + at + 128 * g + 128],
                                                  xb[p][0:HALF + k, T * k:T * k + T], start=k == 0, stop=k == 1)
                for k in range(2):
                    mm = nc.tensor.matmul(ps[0:T, bt, VC:VC + D], xb[p][0:HALF + k, T * k:T * k + T],
                                          W["v"][w][0:HALF + k, k * D:k * D + D], start=k == 0, stop=k == 1)
                mm.then_inc(qkv_done, 1)

            def score(b, p):
                pe.wait_ge(q_ready, b + 1)
                pe.wait_ge(k_ready, b + 1)
                for g in range(QUADS):
                    for r in range(4):
                        mm = nc.tensor.matmul(ps[0:T, r, T * g:T * g + T], qs[p][32 * r:32 * r + 32, T * g:T * g + T],
                                              ks[p][32 * r:32 * r + 32, T * g:T * g + T], start=True, stop=True)
                mm.then_inc(scored, 1)

            def back(b, p):
                pe.wait_ge(exp_done, b + 1)
                for c in range(3):
                    for j in range(4):
                        mm = nc.tensor.transpose(ps[0:T, c, T * j:T * j + T],
                                                 p_[:, T * (4 * c + j):T * (4 * c + j) + T], W["ident"][0:T, 0:T])
                    mm.then_inc(p_turned, 1)
                pe.wait_ge(pT_act, b + 1)
                pe.wait_ge(pT_dve, b + 1)
                wait(pe, added, b)
                for j in range(NH):
                    h = j
                    mm = nc.tensor.matmul(ps[0:T, bo, (DH + 1) * h:(DH + 1) * (h + 1)], pT[:, T * j:T * j + T],
                                          v[p][:, (DH + 1) * h:(DH + 1) * (h + 1)], start=True, stop=True)
                mm.then_inc(weighed, 1)
                pe.wait_ge(on_ready, b + 1)
                for k in range(2):
                    mm = nc.tensor.transpose(ps[0:HALF, bt, T * k:T * k + T], on[:, HALF * k:HALF * k + HALF],
                                             W["ident"][0:T, 0:T])
                mm.then_inc(o_turned, 1)
                pe.wait_ge(oT_ready, b + 1)
                if full:
                    for k in range(2):
                        mm = nc.tensor.matmul(ps[0:T, bo, 256:256 + D], oT[0:HALF + k, T * k:T * k + T],
                                              W["proj"][w][0:HALF + k, k * D:k * D + D], start=k == 0, stop=k == 1)
                else:
                    for m in range(2):
                        for k in range(2):
                            mm = nc.tensor.matmul(ps[0:HALF, bo, 256 + T * m:256 + T * m + T],
                                                  W["proj"][w][0:HALF + k, k * D + HALF * m:k * D + HALF * m + HALF],
                                                  oT[0:HALF + k, T * k:T * k + T], start=k == 0, stop=k == 1)
                mm.then_inc(projected, 1)

            def step(s, p):
                if within(s, n):
                    front(s, p)
                    pe.wait_ge(v_ready, s + 1)
                if within(s - 1, n):
                    back(s - 1, 1 - p)
                if within(s, n):
                    score(s, p)
            steady(pe, step, n + 1, 2, n)

        @block.scalar
        def _(act):
            act.wait_ge(ones_set, 5)

            def front(b, p):
                if full:
                    act.wait_ge(x_turned, b + 1)
                    nc.scalar.copy(xb[p][0:HALF, :], ps[0:HALF, bk, XC:XC + 2 * T]).then_inc(xb_ready, 1)
                act.wait_ge(qkv_done, b + 1)
                nc.scalar.copy(qs[p][:, :], ps[:, bq, 0:QUADS * T]).then_inc(q_ready, 1)
                nc.scalar.copy(v[p][:, :].rearrange("t (h d) -> t h d", h=NH)[:, :, 0:DH],
                               ps[0:T, bt, VC:VC + D].rearrange("t (h d) -> t h d", h=NH)).then_inc(v_ready, 1)

            def back(b, p):
                act.wait_ge(shifted, b + 1)
                nc.scalar.activation(p_[:, :], p_[:, :], ACT.Exp, scale=DH ** -0.5).then_inc(exp_done, 1)
                act.wait_ge(p_turned, 3 * b + 2)
                nc.scalar.copy(pT[:, 0:8 * T].rearrange("t (c n) -> t c n", c=2),
                               ps[0:T, 0:2, 0:4 * T]).then_inc(pT_act, 1)
                act.wait_ge(o_turned, b + 1)
                nc.scalar.copy(oT[0:HALF, :], ps[0:HALF, bt, 0:2 * T]).then_inc(oT_ready, 1)

            def step(s, p):
                if within(s, n):
                    front(s, p)
                if within(s - 1, n):
                    back(s - 1, 1 - p)
            steady(act, step, n + 1, 2, n)

        @block.vector
        def _(dve):
            for p in range(2):
                nc.vector.memset(xb[p][HALF:HALF + 1, :], 1.0).then_inc(ones_set, 1)
                nc.vector.memset(v[p][:, :], 1.0).then_inc(ones_set, 1)
            nc.vector.memset(oT[HALF:HALF + 1, :], 1.0).then_inc(ones_set, 1)
            dve.wait_ge(W["sem"][w], W["count"][w])
            if full:
                nc.vector.tensor_scalar(ntemp[:, :], W["temp"][:, :], -1.0, None, ALU.mult)
                dve.drain()
                for j in range(NH):
                    nc.vector.tensor_scalar(dm[:, T * j:T * j + T], W["ident"][0:T, 0:T], ntemp[:, j:j + 1], 1.0,
                                            ALU.mult, ALU.add)
                with dve.Fori(0, B) as b:
                    nc.vector.bn_stats(st[:, ds(6 * b, 6)], h96[:, ds(b * D, D)])
                norm_stats(nc, dve, mv, st, B).then_inc(stat_done, 1)
                dve.wait_ge(rstd_ready, 1)

            def norm(b, p):
                wait(dve, x_turned, b - 1)
                nc.vector.tensor_scalar(xn[p][:, :], h96[:, ds(b * D, D)], mv[:, ds(b, 1)], rs[:, ds(b, 1)],
                                        ALU.subtract, ALU.mult).then_inc(xn_ready, 1)

            def softmax(b, p):
                dve.wait_ge(scored, b + 1)
                p4 = p_[:, :].rearrange("t (r n) -> t r n", r=4)
                ph = p_[:, :].rearrange("t (h n) -> t h n", h=NH)
                if full:
                    nc.vector.tensor_tensor(p4, scores, dm[:, :].rearrange("t (r n) -> t r n", r=4), ALU.mult)
                    dve.drain()
                    nc.vector.tensor_reduce(nmax[:, :], ph, AX.X, ALU.max, negate=True)
                    dve.drain()
                    nc.vector.tensor_tensor(ph, ph, nmax[:, :, None].broadcast_to([T, NH, T]),
                                            ALU.add).then_inc(shifted, 1)
                else:
                    nc.vector.tensor_tensor(p_[:, :].rearrange("t (r g n) -> t r g n", r=4, g=QUADS),
                                            scores.rearrange("t r (g n) -> t r g n", g=QUADS),
                                            W["apart"][:, None, None, :].broadcast_to([T, 4, QUADS, T]), ALU.add)
                    dve.drain()
                    nc.vector.tensor_reduce(nmax[:, :], ph, AX.X, ALU.max, negate=True)
                    dve.drain()
                    nc.vector.tensor_tensor(ph, ph, nmax[:, :, None].broadcast_to([T, NH, T]),
                                            ALU.add).then_inc(shifted, 1)

            def copy_k(b, p):
                dve.wait_ge(qkv_done, b + 1)
                nc.vector.tensor_copy(ks[p][:, :], ps[:, bk, 0:QUADS * T]).then_inc(k_ready, 1)

            def finish(b, p):
                dve.wait_ge(p_turned, 3 * b + 3)
                nc.vector.tensor_copy(pT[:, 8 * T:12 * T], ps[0:T, 2, 0:4 * T]).then_inc(pT_dve, 1)
                dve.wait_ge(weighed, b + 1)
                o = ps[0:T, bo, 0:NH * (DH + 1)].rearrange("t (h d) -> t h d", h=NH)
                nc.vector.reciprocal(rec[:, :], o[:, :, DH])
                dve.drain()
                nc.vector.tensor_tensor(on[:, :].rearrange("t (h d) -> t h d", h=NH), o[:, :, 0:DH],
                                        rec[:, :, None].broadcast_to([T, NH, DH]), ALU.mult).then_inc(on_ready, 1)
                dve.wait_ge(projected, b + 1)
                if full:
                    nc.vector.tensor_tensor(h96[:, ds(b * D, D)], h96[:, ds(b * D, D)], ps[0:T, bo, 256:256 + D],
                                            ALU.add).then_inc(added, 1)
                else:
                    out = x1T[:, :].rearrange("f (k t) -> f k t", k=2)[:, :, ds(b * T, T)]
                    res = x0T[:, :].rearrange("f (k t) -> f k t", k=2)[:, :, ds(b * T, T)]
                    nc.vector.tensor_tensor(out, ps[0:HALF, bo, 256:256 + 2 * T].rearrange("f (k t) -> f k t", k=2),
                                            res, ALU.add).then_inc(added, 1)

            def step(s, p):
                if within(s, n) and full:
                    norm(s, p)
                if within(s - 1, n):
                    softmax(s - 1, 1 - p)
                if within(s, n):
                    copy_k(s, p)
                if within(s - 1, n):
                    finish(s - 1, 1 - p)
            steady(dve, step, n + 1, 2, n)


def prefix_sum(nc, dve, bufs, lead, n, width):
    a, b, d = bufs[0], bufs[1], 1
    P = a.shape[0]
    while d < n:
        o = lead * width
        nc.vector.tensor_tensor(b[:, o:o + n * width], a[:, o:o + n * width],
                                a[:, o - d * width:o + (n - d) * width], ALU.add)
        dve.drain()
        a, b, d = b, a, 2 * d
    return a


def choose(nc, dve, top, at, values, n):
    for t in range(n):
        nc.vector.max(top[:, 8 * t:8 * t + 8], values[:, E * t:E * t + E])
    dve.drain()
    for t in range(n):
        nc.vector.max_index(at[:, 8 * t:8 * t + 8], top[:, 8 * t:8 * t + 8], values[:, E * t:E * t + E])
    dve.drain()


def route(nc, W, ps, H, h_dram, sorted_dram, xn_all, slot, owner):
    with ExitStack() as ctx:
        S = Scope(W, ctx, "rt")
        n = NTILE
        st, mv, rs = S.sb("st", [128, 6 * n]), S.sb("mv", [128, 3 * n]), S.sb("rs", [128, n])
        xn = [S.sb(f"xn{p}", [128, D]) for p in range(2)]
        xT = [S.sb(f"xT{p}", [HALF + 1, 256]) for p in range(2)]
        logits = S.sb("logits", [128, n * E])
        top, at = S.sb("top", [128, 8 * n]), S.sb("at", [128, 8 * n], U32)
        first = S.sb("first", [128, n])
        oh = S.sb("oh", [128, n * E])
        LEAD = 8
        cum = [S.sb(f"cum{i}", [128, (LEAD + n) * E]) for i in range(2)]
        cnt = [S.sb(f"cnt{i}", [128, LEAD + E]) for i in range(2)]
        over = S.sb("over", [128, E * n])
        tiles, base = S.sb("tiles", [128, E]), S.sb("base", [128, E])
        rank = S.sb("rank", [128, n * E])
        posf = S.sb("posf", [128, n])
        before = S.sb("before", [1, SORT_TILES * E])
        ownf = S.sb("ownf", [1, SORT_TILES])
        (loaded, stat_done, rstd_ready, xn_ready, kept, turned, xT_ready, gated, ones_set, oh_ready, counted,
         slot_ready, scattered, zeroed) = map(S.sem, [
             "loaded", "stat_done", "rstd_ready", "xn_ready", "kept", "turned", "xT_ready", "gated",
             "ones_set", "oh_ready", "counted", "slot_ready", "scattered", "zeroed"])
        block = ctx.enter_context(nc.Block())

        @block.sync
        def _(sp):
            sp.dma_start(H[:, :].rearrange("p (t d) -> p t d", t=n),
                         h_dram.rearrange("(t p) d -> p t d", p=128)).then_inc(loaded, 16)
            sp.dma_start(sorted_dram.rearrange("(t p) d -> p t d", p=128),
                         W["zero"][:, None, :].broadcast_to([128, SORT_TILES, D])).then_inc(zeroed, 16)

        @block.gpsimd
        def _(pool):
            pool.wait_ge(stat_done, 1)
            nc.gpsimd.tensor_tensor(rs[:, :], mv[:, n:2 * n], W["mhalf"][:, 0:1].broadcast_to([128, n]),
                                    ALU.pow).then_inc(rstd_ready, 1)

            def step(s, p):
                pool.wait_ge(xn_ready, s + 1)
                nc.gpsimd.tensor_copy(xn_all[:, ds(s * D, D)], xn[p][:, :]).then_inc(kept, 1)
            steady(pool, step, n, 2, n)
            pool.wait_ge(slot_ready, 1)
            pool.wait_ge(zeroed, 16)
            pool.wait_ge(kept, n)
            for t in range(n):
                nc.gpsimd.indirect_dma_start(
                    out=sorted_dram, out_offset=bass.IndirectOffsetOnAxis(ap=slot[:, t:t + 1], axis=0),
                    in_=xn_all[:, t * D:t * D + D], in_offset=None).then_inc(scattered, 16)
            pool.wait_ge(scattered, 16 * n)

        @block.tensor
        def _(pe):
            pe.wait_ge(ones_set, 2)
            pe.wait_ge(W["sem"]["moe1"], W["count"]["moe1"])

            def step(s, p):
                if within(s, n):
                    pe.wait_ge(xn_ready, s + 1)
                    wait(pe, xT_ready, s - 1)
                    for k in range(2):
                        mm = nc.tensor.transpose(ps[0:HALF, p, 128 * k:128 * k + 128],
                                                 xn[p][:, HALF * k:HALF * k + HALF], W["ident"][:, :])
                    mm.then_inc(turned, 1)
                if within(s - 1, n):
                    wait(pe, xT_ready, s)
                    for k in range(2):
                        mm = nc.tensor.matmul(ps[:, 2, ds(E * (s - 1), E)], xT[1 - p][0:HALF + k, 128 * k:128 * k + 128],
                                              W["gate"][0:HALF + k, E * k:E * k + E], start=k == 0, stop=k == 1)
                    mm.then_inc(gated, 1)
            steady(pe, step, n + 1, 2, n)
            pe.wait_ge(oh_ready, 1)
            nc.tensor.matmul(ps[:, 3, 0:n * E], W["below"][:, :], oh[:, :], start=True, stop=True)
            nc.tensor.matmul(ps[:, 4, 0:n * E], W["ones"][:, :], oh[:, :], start=True, stop=True).then_inc(counted, 1)

        @block.scalar
        def _(act):
            def step(s, p):
                act.wait_ge(turned, s + 1)
                wait(act, gated, s - 1)
                nc.scalar.copy(xT[p][0:HALF, :], ps[0:HALF, p, 0:256]).then_inc(xT_ready, 1)
            act.wait_ge(ones_set, 2)
            steady(act, step, n, 2, n)

        @block.vector
        def _(dve):
            for p in range(2):
                nc.vector.memset(xT[p][HALF:HALF + 1, :], 1.0).then_inc(ones_set, 1)
            dve.wait_ge(loaded, 16)
            with dve.Fori(0, n) as t:
                nc.vector.bn_stats(st[:, ds(6 * t, 6)], H[:, ds(t * D, D)])
            norm_stats(nc, dve, mv, st, n).then_inc(stat_done, 1)
            for c in cum + cnt:
                nc.vector.memset(c[:, :], 0.0)
            dve.wait_ge(rstd_ready, 1)

            def step(s, p):
                wait(dve, turned, s - 1)
                wait(dve, kept, s - 1)
                nc.vector.tensor_scalar(xn[p][:, :], H[:, ds(s * D, D)], mv[:, ds(s, 1)], rs[:, ds(s, 1)],
                                        ALU.subtract, ALU.mult).then_inc(xn_ready, 1)
            steady(dve, step, n, 2, n)
            dve.wait_ge(gated, n)
            nc.vector.tensor_copy(logits[:, :], ps[:, 2, 0:n * E])
            dve.drain()
            choose(nc, dve, top, at, logits, n)
            nc.vector.tensor_copy(first[:, :], at[:, 0:8 * n:8])
            dve.drain()
            nc.vector.tensor_tensor(oh[:, :].rearrange("p (t e) -> p t e", t=n),
                                    W["iota"][:, None, 0:E].broadcast_to([128, n, E]),
                                    first[:, :, None].broadcast_to([128, n, E]), ALU.is_equal).then_inc(oh_ready, 1)
            dve.wait_ge(counted, 1)
            nc.vector.tensor_copy(cum[0][:, LEAD * E:], ps[:, 4, 0:n * E])
            dve.drain()
            c = prefix_sum(nc, dve, cum, LEAD, n, E)
            total = c[:, (LEAD + n - 1) * E:(LEAD + n) * E]
            nc.vector.tensor_tensor(over[:, :].rearrange("p (e k) -> p e k", e=E),
                                    total[:, :, None].broadcast_to([128, E, n]),
                                    W["steps"][:, None, 0:n].broadcast_to([128, E, n]), ALU.is_gt)
            dve.drain()
            nc.vector.tensor_reduce(tiles[:, :], over[:, :].rearrange("p (e k) -> p e k", e=E), AX.X, ALU.add)
            dve.drain()
            nc.vector.tensor_copy(cnt[0][:, LEAD:], tiles[:, :])
            dve.drain()
            ends = prefix_sum(nc, dve, cnt, LEAD, E, 1)[:, LEAD:]
            nc.vector.tensor_tensor(base[:, :], ends, tiles[:, :], ALU.subtract)
            nc.vector.tensor_tensor(before[:, :].rearrange("p (j e) -> p j e", j=SORT_TILES),
                                    ends[0:1, None, :].broadcast_to([1, SORT_TILES, E]),
                                    W["iota"][0:1, 0:SORT_TILES, None].broadcast_to([1, SORT_TILES, E]), ALU.is_le)
            nc.vector.tensor_tensor(rank[:, :], ps[:, 3, 0:n * E], c[:, (LEAD - 1) * E:(LEAD + n - 1) * E], ALU.add)
            dve.drain()
            nc.vector.tensor_scalar(base[:, :], base[:, :], 128.0, None, ALU.mult)
            nc.vector.tensor_reduce(ownf[:, :], before[:, :].rearrange("p (j e) -> p j e", j=SORT_TILES), AX.X,
                                    ALU.add)
            dve.drain()
            r3 = rank[:, :].rearrange("p (t e) -> p t e", t=n)
            nc.vector.tensor_tensor(r3, r3, base[:, None, :].broadcast_to([128, n, E]), ALU.add)
            nc.vector.tensor_scalar(owner[:, :], ownf[:, :], float(E - 1), None, ALU.min)
            dve.drain()
            nc.vector.tensor_tensor(rank[:, :], rank[:, :], oh[:, :], ALU.mult)
            dve.drain()
            nc.vector.tensor_reduce(posf[:, :], r3, AX.X, ALU.add)
            dve.drain()
            nc.vector.tensor_copy(slot[:, :], posf[:, :]).then_inc(slot_ready, 1)


def experts_one(nc, W, ps, H, sorted_dram, done_dram, xn_all, slot, owner):
    with ExitStack() as ctx:
        S = Scope(W, ctx, "e1")
        n = SORT_TILES
        xr = [S.sb(f"xr{p}", [128, D]) for p in range(2)]
        xT = [S.sb(f"xT{p}", [HALF + 1, 256]) for p in range(2)]
        g = [S.sb(f"g{p}", [128, D]) for p in range(2)]
        gT = [S.sb(f"gT{p}", [HALF + 1, 256]) for p in range(2)]
        y = [S.sb(f"y{p}", [128, D]) for p in range(2)]
        loaded = [S.sem(f"loaded{p}") for p in range(2)]
        stored = [S.sem(f"stored{p}") for p in range(2)]
        (x_turned, xT_ready, up_done, g_ready, g_turned, gT_ready, down_done, y_ready, ones_set,
         gathered) = map(S.sem, [
             "x_turned", "xT_ready", "up_done", "g_ready", "g_turned", "gT_ready", "down_done", "y_ready",
             "ones_set", "gathered"])
        block = ctx.enter_context(nc.Block())
        WE = 2 * D

        @block.sync
        def _(sp):
            def step(s, p):
                if within(s, n):
                    wait(sp, x_turned, s - 1)
                    sp.dma_start(xr[p][:, :], sorted_dram[ds(128 * s, 128), :]).then_inc(loaded[p], 16)
                if within(s - 3, n):
                    wait(sp, y_ready, s - 2)
                    sp.dma_start(done_dram[ds(128 * (s - 3), 128), :], y[1 - p][:, :]).then_inc(stored[1 - p], 16)
            steady(sp, step, n + 3, 4, n - 1)
            sp.wait_ge(stored[0], 16 * ((n + 1) // 2))
            sp.wait_ge(stored[1], 16 * (n // 2))

        @block.tensor
        def _(pe):
            pe.wait_ge(ones_set, 4)
            pe.wait_ge(W["sem"]["moe1"], W["count"]["moe1"])

            def expert(s):
                return pe.value_load(owner[0:1, ds(s, 1)], min_val=0, max_val=E - 1)

            def step(s, p):
                if within(s, n):
                    pe.wait_ge(loaded[p], 8 * (s - p) + 16)
                    for k in range(2):
                        mm = nc.tensor.transpose(ps[0:HALF, p, 128 * k:128 * k + 128],
                                                 xr[p][:, HALF * k:HALF * k + HALF], W["ident"][:, :])
                    mm.then_inc(x_turned, 1)
                if within(s - 1, n):
                    e = expert(s - 1)
                    wait(pe, xT_ready, s)
                    for k in range(2):
                        mm = nc.tensor.matmul(ps[:, 3 - p, 0:D], xT[1 - p][0:HALF + k, 128 * k:128 * k + 128],
                                              W["w1"][0:HALF + k, ds(e * WE + D * k, D)], start=k == 0, stop=k == 1)
                    mm.then_inc(up_done, 1)
                if within(s - 2, n):
                    wait(pe, g_ready, s - 1)
                    for k in range(2):
                        mm = nc.tensor.transpose(ps[0:HALF, 4 + p, 128 * k:128 * k + 128],
                                                 g[p][:, HALF * k:HALF * k + HALF], W["ident"][:, :])
                    mm.then_inc(g_turned, 1)
                if within(s - 3, n):
                    e = expert(s - 3)
                    wait(pe, gT_ready, s - 2)
                    wait(pe, y_ready, s - 4)
                    for k in range(2):
                        mm = nc.tensor.matmul(ps[:, 7 - p, 0:D], gT[1 - p][0:HALF + k, 128 * k:128 * k + 128],
                                              W["w2"][0:HALF + k, ds(e * WE + D * k, D)], start=k == 0, stop=k == 1)
                    mm.then_inc(down_done, 1)
            steady(pe, step, n + 3, 6, n - 1)

        @block.scalar
        def _(act):
            act.wait_ge(ones_set, 4)

            def step(s, p):
                if within(s, n):
                    act.wait_ge(x_turned, s + 1)
                    nc.scalar.copy(xT[p][0:HALF, :], ps[0:HALF, p, 0:256]).then_inc(xT_ready, 1)
                if within(s - 1, n):
                    wait(act, up_done, s)
                    nc.scalar.activation(g[1 - p][:, :], ps[:, 3 - p, 0:D], ACT.Gelu).then_inc(g_ready, 1)
            steady(act, step, n + 1, 2, n - 1)

        @block.vector
        def _(dve):
            for x in xT + gT:
                nc.vector.memset(x[HALF:HALF + 1, :], 1.0).then_inc(ones_set, 1)
            dve.wait_ge(ones_set, 4)

            def step(s, p):
                if within(s - 2, n):
                    wait(dve, g_turned, s - 1)
                    nc.vector.tensor_copy(gT[p][0:HALF, :], ps[0:HALF, 4 + p, 0:256]).then_inc(gT_ready, 1)
                if within(s - 3, n):
                    wait(dve, down_done, s - 2)
                    if not isinstance(s, int) or s >= 5:
                        dve.wait_ge(stored[1 - p], 8 * (s - 5 - (1 - p)) + 16)
                    nc.vector.tensor_copy(y[1 - p][:, :], ps[:, 7 - p, 0:D]).then_inc(y_ready, 1)
            steady(dve, step, n + 3, 6, n - 1)
            dve.wait_ge(gathered, 16 * NTILE)
            nc.vector.tensor_tensor(H[:, :], H[:, :], xn_all[:, :], ALU.add)

        @block.gpsimd
        def _(pool):
            pool.wait_ge(stored[0], 16 * ((n + 1) // 2))
            pool.wait_ge(stored[1], 16 * (n // 2))
            for t in range(NTILE):
                nc.gpsimd.indirect_dma_start(
                    out=xn_all[:, t * D:t * D + D], out_offset=None, in_=done_dram,
                    in_offset=bass.IndirectOffsetOnAxis(ap=slot[:, t:t + 1], axis=0)).then_inc(gathered, 16)


def squeeze(nc, W, ps, H, xsT):
    with ExitStack() as ctx:
        S = Scope(W, ctx, "sq")
        n, N = NTILE, 512
        st, mv, rs = S.sb("st", [128, 6 * n]), S.sb("mv", [128, 3 * n]), S.sb("rs", [128, n])
        xn = [S.sb(f"xn{p}", [128, D]) for p in range(2)]
        xnT = S.sb("xnT", [HALF, 2 * TOK])
        chunks = TOK // N
        f1 = [S.sb(f"f1{c}", [HID, N]) for c in range(chunks)]
        ca = [S.sb(f"ca{c}", [64, N]) for c in range(chunks)]
        cb = [S.sb(f"cb{c}", [HID, N]) for c in range(chunks)]
        (stat_done, rstd_ready, xn_ready, summed, turned, xnT_ready, fc_done, fc_ready, a_done, a_ready,
         b_done, b_ready) = map(S.sem, [
             "stat_done", "rstd_ready", "xn_ready", "summed", "turned", "xnT_ready", "fc_done", "fc_ready",
             "a_done", "a_ready", "b_done", "b_ready"])
        block = ctx.enter_context(nc.Block())

        @block.gpsimd
        def _(pool):
            pool.wait_ge(stat_done, 1)
            nc.gpsimd.tensor_tensor(rs[:, :], mv[:, n:2 * n], W["mhalf"][:, 0:1].broadcast_to([128, n]),
                                    ALU.pow).then_inc(rstd_ready, 1)

            def step(s, p):
                pool.wait_ge(xn_ready, s + 1)
                nc.gpsimd.tensor_tensor(H[:, ds(s * D, D)], H[:, ds(s * D, D)], xn[p][:, :],
                                        ALU.add).then_inc(summed, 1)
            steady(pool, step, n, 2, n)

        @block.tensor
        def _(pe):
            pe.wait_ge(W["sem"]["nat"], W["count"]["nat"])

            def step(s, p):
                pe.wait_ge(xn_ready, s + 1)
                wait(pe, xnT_ready, s - 1)
                for k in range(2):
                    mm = nc.tensor.transpose(ps[0:HALF, p, 128 * k:128 * k + 128],
                                             xn[p][:, HALF * k:HALF * k + HALF], W["ident"][:, :])
                mm.then_inc(turned, 1)
            steady(pe, step, n, 2, n)
            for s in range(chunks + 2):
                if s < chunks:
                    pe.wait_ge(xnT_ready, N // 128 * (s + 1))
                    wait(pe, fc_ready, s - 1)
                    for k in range(2):
                        mm = nc.tensor.matmul(ps[0:HID, 2 + s % 2, :], W["fc1"][:, HID * k:HID * k + HID],
                                              xnT[:, k * TOK + s * N:k * TOK + s * N + N], start=k == 0, stop=k == 1)
                    mm.then_inc(fc_done, 1)
                if 0 <= s - 1 < chunks:
                    pe.wait_ge(fc_ready, s)
                    nc.tensor.matmul(ps[0:64, 4 + (s - 1) % 2, :], W["conva"][:, :], f1[s - 1][:, :],
                                     start=True, stop=True).then_inc(a_done, 1)
                if 0 <= s - 2 < chunks:
                    pe.wait_ge(a_ready, s - 1)
                    nc.tensor.matmul(ps[0:HID, 6 + (s - 2) % 2, :], W["convb"][:, :], ca[s - 2][:, :],
                                     start=True, stop=True).then_inc(b_done, 1)

        @block.scalar
        def _(act):
            def step(s, p):
                act.wait_ge(turned, s + 1)
                nc.scalar.copy(xnT[:, :].rearrange("f (k t) -> f k t", k=2)[:, :, ds(128 * s, 128)],
                               ps[0:HALF, p, 0:256].rearrange("f (k t) -> f k t", k=2)).then_inc(xnT_ready, 1)
            steady(act, step, n, 2, n)
            for s in range(chunks):
                act.wait_ge(b_ready, s + 1)
                nc.scalar.activation(xsT[0:HID, s * N:s * N + N], cb[s][:, :], ACT.Gelu)

        @block.vector
        def _(dve):
            nc.vector.memset(xsT[HID:HID + 1, :], 1.0)
            with dve.Fori(0, n) as t:
                nc.vector.bn_stats(st[:, ds(6 * t, 6)], H[:, ds(t * D, D)])
            norm_stats(nc, dve, mv, st, n).then_inc(stat_done, 1)
            dve.wait_ge(rstd_ready, 1)
            dve.wait_ge(W["sem"]["nat"], W["count"]["nat"])

            def step(s, p):
                wait(dve, turned, s - 1)
                wait(dve, summed, s - 1)
                nc.vector.tensor_scalar(xn[p][:, :], H[:, ds(s * D, D)], mv[:, ds(s, 1)], rs[:, ds(s, 1)],
                                        ALU.subtract, ALU.mult).then_inc(xn_ready, 1)
            steady(dve, step, n, 2, n)
            for s in range(chunks + 2):
                if s < chunks:
                    dve.wait_ge(fc_done, s + 1)
                    nc.vector.tensor_scalar(f1[s][:, :], ps[0:HID, 2 + s % 2, :], W["fc1b"][:, :], None,
                                            ALU.add).then_inc(fc_ready, 1)
                if 0 <= s - 1 < chunks:
                    dve.wait_ge(a_done, s)
                    nc.vector.tensor_scalar(ca[s - 1][:, :], ps[0:64, 4 + (s - 1) % 2, :], W["convab"][:, :], None,
                                            ALU.add).then_inc(a_ready, 1)
                if 0 <= s - 2 < chunks:
                    dve.wait_ge(b_done, s - 1)
                    nc.vector.scalar_tensor_tensor(cb[s - 2][:, :], ps[0:HID, 6 + (s - 2) % 2, :],
                                                   W["convbb"][:, :], f1[s - 2][:, :], ALU.add,
                                                   ALU.add).then_inc(b_ready, 1)


def neighborhood(nc, W, ps, xsT, near_dram):
    with ExitStack() as ctx:
        S = Scope(W, ctx, "nb")
        N = 512
        qT, kT = S.sb("qT", [128, TOK]), S.sb("kT", [128, TOK])
        bias = [[S.sb(f"bias{c}{g}", [128, NH2 * NKEY]) for g in range(2)] for c in range(3)]
        xw = [S.sb(f"xw{p}", [HID + 1, NKEY]) for p in range(2)]
        qw = [S.sb(f"qw{p}", [128, 128]) for p in range(2)]
        kw = [S.sb(f"kw{p}", [128, NKEY]) for p in range(2)]
        v = [S.sb(f"v{p}", [HKEY, 2 * HID]) for p in range(2)]
        pr = S.sb("pr", [128, NH2 * NKEY])
        nmax, total, rec = S.sb("nmax", [128, NH2]), S.sb("total", [128, NH2]), S.sb("rec", [128, NH2])
        pT = S.sb("pT", [HKEY, 2 * NH2 * 128])
        on = S.sb("on", [128, HID])
        oT = S.sb("oT", [HID, 128])
        zT = S.sb("zT", [HID + 1, 128])
        y = [S.sb(f"y{p}", [128, D]) for p in range(2)]
        stored = [S.sem(f"stored{p}") for p in range(2)]
        (qk_done, q_ready, k_ready, bias_ready, window_ready, fronted, v_ready, shifted, exp_done, p_turned,
         pT_act, pT_dve, weighed, on_ready, o_turned, oT_ready, proj_done, zT_ready, out_done, y_ready,
         ones_set) = map(S.sem, [
             "qk_done", "q_ready", "k_ready", "bias_ready", "window_ready", "fronted", "v_ready", "shifted",
             "exp_done", "p_turned", "pT_act", "pT_dve", "weighed", "on_ready", "o_turned", "oT_ready",
             "proj_done", "zT_ready", "out_done", "y_ready", "ones_set"])
        block = ctx.enter_context(nc.Block())
        xs3 = xsT[0:HID + 1, :].rearrange("f (i j) -> f i j", i=B)
        q3 = qT[:, :].rearrange("f (i j) -> f i j", i=B)
        k3 = kT[:, :].rearrange("f (i j) -> f i j", i=B)
        n = 2 * COLS

        def columns(tile):
            def both(c, kind):
                for g in range(2):
                    tile(2 * c + g, c, kind, g)
            return both

        def all_columns(eng, both):
            both(0, 0)
            with eng.Fori(1, COLS - 2) as c:
                both(c, 1)
            both(COLS - 2, 1)
            both(COLS - 1, 2)

        def keys(c, kind):
            return {0: 0, 1: QC * c - WIN // 2, 2: NA - KCOL}[kind]

        def following(c, kind, g):
            return (c, kind, 1) if g == 0 else (c + 1, 2 if isinstance(c, int) and c + 1 == COLS - 1 else 1, 0)

        @block.sync
        def _(sp):
            def tile(u, c, kind, g):
                sp.wait_ge(y_ready, u + 1)
                sp.dma_start(near_dram.rearrange("(i j) d -> i j d", i=B)[QR * g:QR * g + QR, ds(QC * c, QC), :],
                             y[g][:, :]).then_inc(stored[g], 16)
            all_columns(sp, columns(tile))
            for g in range(2):
                sp.wait_ge(stored[g], 16 * COLS)

        @block.gpsimd
        def _(pool):
            pool.wait_ge(W["sem"]["nat"], W["count"]["nat"])
            t4 = W["toep"][:, :].rearrange("p (n a b) -> p n a b", n=NH2, a=KR + 2)
            for c in range(3):
                for g in range(2):
                    a0, b0 = (2, 0)[g], (4, 2, 0)[c]
                    for h in range(NH2):
                        i = nc.gpsimd.tensor_tensor(
                            bias[c][g][:, h * NKEY:(h + 1) * NKEY].rearrange("p (a b) -> p a b", a=KR),
                            t4[:, h, a0:a0 + KR, b0:b0 + KCOL],
                            W["outside"][:, (2 * c + g) * NKEY:(2 * c + g + 1) * NKEY].rearrange("p (a b) -> p a b", a=KR),
                            ALU.add)
            i.then_inc(bias_ready, 1)
            pool.wait_ge(q_ready, TOK // N)
            pool.wait_ge(k_ready, TOK // N)

            def tile(u, c, kind, g):
                wait(pool, fronted, u - 1)
                nc.gpsimd.tensor_copy(xw[g][:, :].rearrange("f (a b) -> f a b", a=KR),
                                      xs3[:, (B - KR) * g:(B - KR) * g + KR, ds(keys(c, kind), KCOL)])
                nc.gpsimd.tensor_copy(kw[g][:, :].rearrange("f (a b) -> f a b", a=KR),
                                      k3[:, (B - KR) * g:(B - KR) * g + KR, ds(keys(c, kind), KCOL)])
                nc.gpsimd.tensor_copy(qw[g][:, :].rearrange("f (a b) -> f a b", a=QR),
                                      q3[:, QR * g:QR * g + QR, ds(QC * c, QC)]).then_inc(window_ready, 1)
            all_columns(pool, columns(tile))

        @block.tensor
        def _(pe):
            pe.wait_ge(W["sem"]["nat"], W["count"]["nat"])
            for s in range(TOK // N):
                for j, w in enumerate((W["nq"], W["nk"])):
                    wait(pe, (q_ready, k_ready)[j], s)
                    mm = nc.tensor.matmul(ps[:, j, :], w[:, :], xsT[0:HID + 1, s * N:s * N + N],
                                          start=True, stop=True)
                    mm.then_inc(qk_done, 1)
            pe.wait_ge(q_ready, TOK // N)
            pe.wait_ge(k_ready, TOK // N)
            pe.wait_ge(ones_set, 1)

            def front(u, c, kind, g):
                pe.wait_ge(window_ready, u + 1)
                for h in range(2):
                    mm = nc.tensor.matmul(ps[0:HKEY, 4, HID * h:HID * h + HID], xw[g][:, HKEY * h:HKEY * h + HKEY],
                                          W["nv"][:, :], start=True, stop=True)
                wait(pe, shifted, u)
                for h in range(NH2):
                    mm = nc.tensor.matmul(
                        ps[:, h, 0:NKEY], qw[g][32 * h:32 * h + 32, :], kw[g][32 * h:32 * h + 32, :],
                        start=True, stop=True)
                mm.then_inc(fronted, 1)

            def back(u, g):
                pe.wait_ge(exp_done, u + 1)
                for h in range(NH2):
                    for j in range(2):
                        i = 2 * h + j
                        mm = nc.tensor.transpose(ps[0:HKEY, 5 + i // 4, 128 * (i % 4):128 * (i % 4) + 128],
                                                 pr[:, HKEY * i:HKEY * i + HKEY], W["ident"][:, :])
                    if h % 2:
                        mm.then_inc(p_turned, 1)
                pe.wait_ge(pT_act, u + 1)
                pe.wait_ge(pT_dve, u + 1)
                wait(pe, y_ready, u)
                for h in range(NH2):
                    for j in range(2):
                        mm = nc.tensor.matmul(ps[:, 7, DH2 * h:DH2 * h + DH2], pT[:, 128 * (2 * h + j):128 * (2 * h + j + 1)],
                                              v[g][:, HID * j + DH2 * h:HID * j + DH2 * h + DH2],
                                              start=j == 0, stop=j == 1)
                mm.then_inc(weighed, 1)
                pe.wait_ge(on_ready, u + 1)
                nc.tensor.transpose(ps[0:HID, 7, 128:256], on[:, :], W["ident"][:, :]).then_inc(o_turned, 1)
                pe.wait_ge(oT_ready, u + 1)
                nc.tensor.matmul(ps[0:HID, 7, 256:384], W["np"][:, :], oT[:, :], start=True,
                                 stop=True).then_inc(proj_done, 1)
                pe.wait_ge(zT_ready, u + 1)
                nc.tensor.matmul(ps[:, 7, 0:D], zT[:, :], W["fc2"][:, :], start=True, stop=True).then_inc(out_done, 1)

            front(0, 0, 0, 0)

            def tile(u, c, kind, g):
                if not (isinstance(u, int) and u == n - 1):
                    pe.wait_ge(v_ready, u + 1)
                    front(u + 1, *following(c, kind, g))
                back(u, g)
            all_columns(pe, columns(tile))

        @block.scalar
        def _(act):
            for s in range(TOK // N):
                act.wait_ge(qk_done, 2 * s + 1)
                nc.scalar.mul(qT[:, s * N:s * N + N], ps[:, 0, :], DH2 ** -0.5).then_inc(q_ready, 1)
            act.wait_ge(ones_set, 1)

            def copy_v(u, g):
                act.wait_ge(fronted, u + 1)
                nc.scalar.copy(v[g][:, :], ps[0:HKEY, 4, 0:2 * HID]).then_inc(v_ready, 1)
            copy_v(0, 0)

            def tile(u, c, kind, g):
                if not (isinstance(u, int) and u == n - 1):
                    copy_v(u + 1, 1 - g)
                act.wait_ge(shifted, u + 1)
                for h in range(NH2):
                    e = nc.scalar.activation(pr[:, h * NKEY:(h + 1) * NKEY], pr[:, h * NKEY:(h + 1) * NKEY],
                                             ACT.Exp, bias=nmax[:, h:h + 1], accum_out=total[:, h:h + 1])
                e.then_inc(exp_done, 1)
                act.wait_ge(p_turned, 2 * u + 1)
                nc.scalar.copy(pT[:, 0:512], ps[0:HKEY, 5, :]).then_inc(pT_act, 1)
                act.wait_ge(o_turned, u + 1)
                nc.scalar.copy(oT[:, :], ps[0:HID, 7, 128:256]).then_inc(oT_ready, 1)
                act.wait_ge(proj_done, u + 1)
                nc.scalar.activation(zT[0:HID, :], ps[0:HID, 7, 256:384], ACT.Identity,
                                     bias=W["npb"][:, :]).then_inc(zT_ready, 1)
            all_columns(act, columns(tile))

        @block.vector
        def _(dve):
            nc.vector.memset(zT[HID:HID + 1, :], 1.0).then_inc(ones_set, 1)
            for s in range(TOK // N):
                dve.wait_ge(qk_done, 2 * s + 2)
                nc.vector.tensor_copy(kT[:, s * N:s * N + N], ps[:, 1, :]).then_inc(k_ready, 1)
            dve.wait_ge(bias_ready, 1)

            def tile(u, c, kind, g):
                dve.wait_ge(fronted, u + 1)
                p3 = pr[:, :].rearrange("p (h n) -> p h n", h=NH2)
                nc.vector.tensor_tensor(p3, ps[:, 0:NH2, 0:NKEY],
                                        bias[kind][g][:, :].rearrange("p (h n) -> p h n", h=NH2), ALU.add)
                dve.drain()
                nc.vector.tensor_reduce(nmax[:, :], p3, AX.X, ALU.max, negate=True).then_inc(shifted, 1)
                dve.wait_ge(p_turned, 2 * u + 2)
                nc.vector.tensor_copy(pT[:, 512:1024], ps[0:HKEY, 6, :]).then_inc(pT_dve, 1)
                dve.wait_ge(weighed, u + 1)
                nc.vector.reciprocal(rec[:, :], total[:, :])
                dve.drain()
                nc.vector.tensor_tensor(on[:, :].rearrange("p (h d) -> p h d", h=NH2),
                                        ps[:, 7, 0:HID].rearrange("p (h d) -> p h d", h=NH2),
                                        rec[:, :, None].broadcast_to([128, NH2, DH2]), ALU.mult).then_inc(on_ready, 1)
                dve.wait_ge(out_done, u + 1)
                if not (isinstance(c, int) and c == 0):
                    dve.wait_ge(stored[g], 16 * c)
                nc.vector.tensor_copy(y[g][:, :], ps[:, 7, 0:D]).then_inc(y_ready, 1)
            all_columns(dve, columns(tile))


def route_four(nc, W, ps, H, near_dram, xnT, share):
    with ExitStack() as ctx:
        S = Scope(W, ctx, "rf")
        n, G = NTILE, 4
        add = S.sb("add", [128, n * D])
        st, mv, rs = S.sb("st", [128, 6 * n]), S.sb("mv", [128, 3 * n]), S.sb("rs", [128, n])
        xn = [S.sb(f"xn{p}", [128, D]) for p in range(2)]
        xT = [S.sb(f"xT{p}", [HALF + 1, 256]) for p in range(2)]
        sc, sfc = S.sb("sc", [128, n * E]), S.sb("sfc", [128, n * E])
        pair = S.sb("pair", [128, n * G * 6])
        gs = S.sb("gs", [128, n * G])
        ge, gt = S.sb("ge", [128, n * G * G]), S.sb("gt", [128, n * G * G])
        gm = S.sb("gm", [128, n * G])
        top, at = S.sb("top", [128, 8 * n]), S.sb("at", [128, 8 * n], U32)
        atf = S.sb("atf", [128, 8 * n])
        hit = S.sb("hit", [128, n * 4 * E])
        sel = S.sb("sel", [128, n * E])
        tot = S.sb("tot", [128, n])
        (loaded, stat_done, rstd_ready, xn_ready, turned, xT_ready, gated, ones_set, kept, sig_done) = map(S.sem, [
            "loaded", "stat_done", "rstd_ready", "xn_ready", "turned", "xT_ready", "gated", "ones_set", "kept",
            "sig_done"])
        block = ctx.enter_context(nc.Block())

        @block.sync
        def _(sp):
            sp.dma_start(add[:, :].rearrange("p (t d) -> p t d", t=n),
                         near_dram.rearrange("(t p) d -> p t d", p=128)).then_inc(loaded, 16)

        @block.gpsimd
        def _(pool):
            pool.wait_ge(stat_done, 1)
            nc.gpsimd.tensor_tensor(rs[:, :], mv[:, n:2 * n], W["mhalf"][:, 0:1].broadcast_to([128, n]),
                                    ALU.pow).then_inc(rstd_ready, 1)

            def step(s, p):
                pool.wait_ge(xT_ready, s + 1)
                nc.gpsimd.tensor_copy(xnT[0:HALF, :].rearrange("f (k t) -> f k t", k=2)[:, :, ds(128 * s, 128)],
                                      xT[p][0:HALF, :].rearrange("f (k t) -> f k t", k=2)).then_inc(kept, 1)
            steady(pool, step, n, 2, n)

        @block.tensor
        def _(pe):
            pe.wait_ge(ones_set, 2)
            pe.wait_ge(W["sem"]["moe2"], W["count"]["moe2"])

            def step(s, p):
                if within(s, n):
                    pe.wait_ge(xn_ready, s + 1)
                    for k in range(2):
                        mm = nc.tensor.transpose(ps[0:HALF, p, 128 * k:128 * k + 128],
                                                 xn[p][:, HALF * k:HALF * k + HALF], W["ident"][:, :])
                    mm.then_inc(turned, 1)
                if within(s - 1, n):
                    wait(pe, xT_ready, s)
                    for k in range(2):
                        mm = nc.tensor.matmul(ps[:, 2, ds(E * (s - 1), E)], xT[1 - p][0:HALF + k, 128 * k:128 * k + 128],
                                              W["router"][0:HALF + k, E * k:E * k + E], start=k == 0, stop=k == 1)
                    mm.then_inc(gated, 1)
            steady(pe, step, n + 1, 2, n)

        @block.scalar
        def _(act):
            act.wait_ge(ones_set, 2)

            def step(s, p):
                act.wait_ge(turned, s + 1)
                wait(act, gated, s - 1)
                wait(act, kept, s - 1)
                nc.scalar.copy(xT[p][0:HALF, :], ps[0:HALF, p, 0:256]).then_inc(xT_ready, 1)
            steady(act, step, n, 2, n)
            act.wait_ge(gated, n)
            nc.scalar.activation(sc[:, :], ps[:, 2, 0:n * E], ACT.Sigmoid).then_inc(sig_done, 1)

        @block.vector
        def _(dve):
            for p in range(2):
                nc.vector.memset(xT[p][HALF:HALF + 1, :], 1.0).then_inc(ones_set, 1)
            dve.wait_ge(loaded, 16)
            nc.vector.tensor_tensor(H[:, :], H[:, :], add[:, :], ALU.add)
            dve.drain()
            with dve.Fori(0, n) as t:
                nc.vector.bn_stats(st[:, ds(6 * t, 6)], H[:, ds(t * D, D)])
            norm_stats(nc, dve, mv, st, n).then_inc(stat_done, 1)
            dve.wait_ge(rstd_ready, 1)

            def step(s, p):
                wait(dve, turned, s - 1)
                nc.vector.tensor_scalar(xn[p][:, :], H[:, ds(s * D, D)], mv[:, ds(s, 1)], rs[:, ds(s, 1)],
                                        ALU.subtract, ALU.mult).then_inc(xn_ready, 1)
            steady(dve, step, n, 2, n)
            dve.wait_ge(sig_done, 1)
            dve.wait_ge(W["sem"]["moe2"], W["count"]["moe2"])
            t3 = lambda x: x[:, :].rearrange("p (t e) -> p t e", t=n)
            nc.vector.tensor_tensor(t3(sfc), t3(sc), W["corr"][:, None, :].broadcast_to([128, n, E]), ALU.add)
            dve.drain()
            s4 = sfc[:, :].rearrange("p (g e) -> p g e", e=4)
            p6 = pair[:, :].rearrange("p (g e) -> p g e", e=6)
            nc.vector.tensor_tensor(p6[:, :, 0:3], s4[:, :, 0:3], s4[:, :, 1:4], ALU.add)
            nc.vector.tensor_tensor(p6[:, :, 3:5], s4[:, :, 0:2], s4[:, :, 2:4], ALU.add)
            nc.vector.tensor_tensor(p6[:, :, 5:6], s4[:, :, 0:1], s4[:, :, 3:4], ALU.add)
            dve.drain()
            nc.vector.tensor_reduce(gs[:, :], p6, AX.X, ALU.max)
            dve.drain()
            mine = gs[:, :].rearrange("p (t g) -> p t g", g=G)[:, :, :, None].broadcast_to([128, n, G, G])
            other = gs[:, :].rearrange("p (t g) -> p t g", g=G)[:, :, None, :].broadcast_to([128, n, G, G])
            q4 = lambda x: x[:, :].rearrange("p (t g h) -> p t g h", g=G, h=G)
            q3 = lambda x: x[:, :].rearrange("p (t g) -> p t g", g=G * G)
            nc.vector.tensor_tensor(q4(ge), other, mine, ALU.is_ge)
            nc.vector.tensor_tensor(q4(gt), other, mine, ALU.is_gt)
            dve.drain()
            nc.vector.tensor_tensor(q3(ge), q3(ge), W["earlier"][:, None, :].broadcast_to([128, n, G * G]), ALU.mult)
            nc.vector.tensor_tensor(q3(gt), q3(gt), W["later"][:, None, :].broadcast_to([128, n, G * G]), ALU.mult)
            dve.drain()
            nc.vector.tensor_tensor(ge[:, :], ge[:, :], gt[:, :], ALU.add)
            dve.drain()
            nc.vector.tensor_reduce(gm[:, :], ge[:, :].rearrange("p (g h) -> p g h", h=G), AX.X, ALU.add)
            dve.drain()
            nc.vector.tensor_scalar(gm[:, :], gm[:, :], 1.5, None, ALU.is_lt)
            dve.drain()
            nc.vector.tensor_tensor(s4, s4, gm[:, :, None].broadcast_to([128, n * G, 4]), ALU.mult)
            dve.drain()
            choose(nc, dve, top, at, sfc, n)
            nc.vector.tensor_copy(atf[:, :], at[:, :])
            dve.drain()
            h4 = hit[:, :].rearrange("p (t k e) -> p t k e", t=n, k=4)
            nc.vector.tensor_tensor(
                h4, W["iota"][:, None, None, 0:E].broadcast_to([128, n, 4, E]),
                atf[:, :].rearrange("p (t k) -> p t k", t=n)[:, :, 0:4, None].broadcast_to([128, n, 4, E]),
                ALU.is_equal)
            dve.drain()
            nc.vector.tensor_reduce(t3(sel), hit[:, :].rearrange("p (t k e) -> p t e k", t=n, k=4), AX.X, ALU.add)
            dve.drain()
            nc.vector.tensor_tensor(sel[:, :], sel[:, :], sc[:, :], ALU.mult)
            dve.drain()
            nc.vector.tensor_reduce(tot[:, :], t3(sel), AX.X, ALU.add)
            dve.drain()
            nc.vector.tensor_scalar(tot[:, :], tot[:, :], 1e-20, None, ALU.add)
            dve.drain()
            nc.vector.reciprocal(tot[:, :], tot[:, :])
            dve.drain()
            nc.vector.tensor_tensor(t3(sel), t3(sel), tot[:, :, None].broadcast_to([128, n, E]), ALU.mult)
            dve.drain()
            s18 = share[:, :].rearrange("p (t e) -> p t e", t=n)
            nc.vector.tensor_scalar(s18[:, :, 0:E], t3(sel), 2.5, None, ALU.mult)
            nc.vector.memset(s18[:, :, E:E + 2], 1.0)


def experts_four(nc, W, ps, H, xnT, share, out_dram):
    with ExitStack() as ctx:
        S = Scope(W, ctx, "e4")
        n, P3 = NTILE, 3
        WP = 4 * I2
        xb = [S.sb(f"xb{p}", [HALF + 1, 256]) for p in range(2)]
        sg = [S.sb(f"sg{i}", [128, 2 * I2]) for i in range(P3)]
        hh = [S.sb(f"hh{i}", [128, 2 * (I2 + 1)]) for i in range(P3)]
        hT = [S.sb(f"hT{i}", [I2 + 1, 256]) for i in range(P3)]
        y = [S.sb(f"y{p}", [128, D]) for p in range(2)]
        stored = [S.sem(f"stored{p}") for p in range(2)]
        (xb_ready, up_done, sg_ready, hh_ready, turned, hT_ready, summed, y_ready, ones_set) = map(S.sem, [
            "xb_ready", "up_done", "sg_ready", "hh_ready", "turned", "hT_ready", "summed", "y_ready", "ones_set"])
        block = ctx.enter_context(nc.Block())

        def tiles(eng, tile, after):
            steady(eng, tile, n, 2, n)
            after()

        def lagging(t, q, lag):
            if q >= lag:
                return t, q - lag
            if isinstance(t, int) and t == 0:
                return None
            return t - 1, q - lag + PAIRS

        @block.sync
        def _(sp):
            def tile(t, p):
                sp.wait_ge(y_ready, t + 1)
                sp.dma_start(out_dram[ds(128 * t, 128), :], y[p][:, :]).then_inc(stored[p], 16)
            tiles(sp, tile, lambda: None)
            for p in range(2):
                sp.wait_ge(stored[p], 8 * n)

        @block.gpsimd
        def _(pool):

            def tile(t, p):
                wait(pool, up_done, PAIRS * (t - 1))
                nc.gpsimd.tensor_copy(xb[p][0:HALF, :].rearrange("f (k t) -> f k t", k=2),
                                      xnT[0:HALF, :].rearrange("f (k t) -> f k t", k=2)[:, :, ds(128 * t, 128)]
                                      ).then_inc(xb_ready, 1)
            tiles(pool, tile, lambda: None)

        @block.tensor
        def _(pe):
            pe.wait_ge(ones_set, 2)

            def up(t, q, p):
                i = q % P3
                if q == 0:
                    pe.wait_ge(xb_ready, t + 1)
                wait(pe, hh_ready, PAIRS * t + q - 2)
                for k in range(2):
                    mm = nc.tensor.matmul(ps[:, i, 0:WP], xb[p][0:HALF + k, 128 * k:128 * k + 128],
                                          W["gu"][0:HALF + k, (2 * q + k) * WP:(2 * q + k + 1) * WP],
                                          start=k == 0, stop=k == 1)
                mm.then_inc(up_done, 1)

            def turn(t, q):
                i = q % P3
                pe.wait_ge(hh_ready, PAIRS * t + q + 1)
                for j in range(2):
                    mm = nc.tensor.transpose(ps[0:I2 + 1, 3 + i, 128 * j:128 * j + 128],
                                             hh[i][:, (I2 + 1) * j:(I2 + 1) * (j + 1)], W["ident"][:, :])
                mm.then_inc(turned, 1)

            def down(t, q):
                i = q % P3
                pe.wait_ge(hT_ready, PAIRS * t + q + 1)
                if q == 0:
                    wait(pe, y_ready, t)
                for j in range(2):
                    mm = nc.tensor.matmul(ps[:, 6, 0:D], hT[i][:, 128 * j:128 * j + 128],
                                          W["dn"][:, (2 * q + j) * D:(2 * q + j + 1) * D],
                                          start=q == 0 and j == 0, stop=q == PAIRS - 1 and j == 1)
                mm.then_inc(summed, 1)

            def tile(t, p):
                for q in range(PAIRS):
                    up(t, q, p)
                    if lagging(t, q, 1):
                        turn(*lagging(t, q, 1))
                    if lagging(t, q, 2):
                        down(*lagging(t, q, 2))

            def after():
                turn(n - 1, PAIRS - 1)
                down(n - 1, PAIRS - 2)
                down(n - 1, PAIRS - 1)
            tiles(pe, tile, after)

        @block.scalar
        def _(act):
            def gate(t, q):
                i = q % P3
                act.wait_ge(up_done, PAIRS * t + q + 1)
                nc.scalar.activation(sg[i][:, :].rearrange("p (j n) -> p j n", j=2),
                                     ps[:, i, 0:WP].rearrange("p (j u n) -> p j u n", j=2, u=2)[:, :, 0, :],
                                     ACT.Silu).then_inc(sg_ready, 1)

            def copy_h(t, q):
                i = q % P3
                act.wait_ge(turned, PAIRS * t + q + 1)
                nc.scalar.copy(hT[i][:, :], ps[0:I2 + 1, 3 + i, 0:256]).then_inc(hT_ready, 1)

            def tile(t, p):
                for q in range(PAIRS):
                    gate(t, q)
                    if lagging(t, q, 1):
                        copy_h(*lagging(t, q, 1))
            tiles(act, tile, lambda: copy_h(n - 1, PAIRS - 1))

        @block.vector
        def _(dve):
            for p in range(2):
                nc.vector.memset(xb[p][HALF:HALF + 1, :], 1.0).then_inc(ones_set, 1)
            def weigh(t, q):
                i = q % P3
                dve.wait_ge(sg_ready, PAIRS * t + q + 1)
                for j in range(2):
                    o = (I2 + 1) * j
                    c = share[:, ds(t * 2 * PAIRS + 2 * q + j, 1)]
                    last = nc.vector.scalar_tensor_tensor(
                        hh[i][:, o:o + I2], sg[i][:, I2 * j:I2 * j + I2], c,
                        ps[:, i, 2 * I2 * j + I2:2 * I2 * (j + 1)], ALU.mult, ALU.mult)
                nc.vector.tensor_copy(hh[i][:, I2:2 * (I2 + 1):I2 + 1],
                                      share[:, ds(t * 2 * PAIRS + 2 * q, 2)]).then_inc(hh_ready, 1)

            def finish(t, p):
                dve.wait_ge(summed, PAIRS * (t + 1))
                wait(dve, stored[p], 8 * (t - p))
                nc.vector.tensor_tensor(y[p][:, :], ps[:, 6, 0:D], H[:, ds(t * D, D)], ALU.add).then_inc(y_ready, 1)

            def tile(t, p):
                for q in range(PAIRS):
                    weigh(t, q)
                    if q == 1 and lagging(t, q, 2):
                        finish(t - 1, 1 - p)
            tiles(dve, tile, lambda: finish(n - 1, (n - 1) % 2))


WEIGHTS = {
    "ident": (128, 128, "ident"),
    "pw": (128, KC * D, "embed"), "pb": (128, D, "embed"), "lng": (128, D, "embed"), "lnb": (128, D, "embed"),
    "pe": (128, D, "embed"),
    "ff1": (HALF, 2 * FF, "ff"), "ff1b": (128, KC, "ff"), "ff2": (128, KC * D, "ff"), "ff2b": (HALF, 2, "ff"),
    "qk_a": (HALF + 1, 2 * 768, "a"), "v_a": (HALF + 1, 2 * D, "a"), "proj_a": (HALF + 1, 2 * D, "a"),
    "apart": (128, 128, "a"),
    "qk_b": (HALF + 1, 2 * 768, "b"), "v_b": (HALF + 1, 2 * D, "b"), "proj_b": (HALF + 1, 2 * D, "b"),
    "temp": (NA, NH, "b"),
    "gate": (HALF + 1, 2 * E, "moe1"), "w1": (HALF + 1, E * 2 * D, "moe1"), "w2": (HALF + 1, E * 2 * D, "moe1"),
    "iota": (128, 32, "moe1"), "steps": (128, 16, "moe1"), "below": (128, 128, "moe1"),
    "fc1": (HALF, 2 * HID, "nat"), "fc1b": (HID, 1, "nat"), "conva": (HID, 64, "nat"), "convab": (64, 1, "nat"),
    "convb": (64, HID, "nat"), "convbb": (HID, 1, "nat"), "nq": (HID + 1, 128, "nat"), "nk": (HID + 1, 128, "nat"),
    "nv": (HID + 1, HID, "nat"), "np": (HID, HID, "nat"), "npb": (HID, 1, "nat"), "fc2": (HID + 1, D, "nat"),
    "toep": (128, NH2 * (KR + 2) * (KCOL + 4), "nat"), "outside": (128, 6 * NKEY, "nat"),
    "router": (HALF + 1, 2 * E, "moe2"), "corr": (128, E, "moe2"),
    "earlier": (128, 16, "moe2"), "later": (128, 16, "moe2"),
    "gu": (HALF + 1, PAIRS * 2 * 4 * I2, "moe2"), "dn": (I2 + 1, PAIRS * 2 * D, "moe2"),
}


def build(nc, args):
    with ExitStack() as ctx:
        held = {name: ctx.enter_context(nc.sbuf_tensor("w_" + name, [p, c], F32))
                for name, (p, c, _) in WEIGHTS.items()}
        W = {"nc": nc, "whole": ctx, **held}
        S = Scope(W, ctx, "w")
        for m in ("qk", "v", "proj"):
            W[m] = {w: held[f"{m}_{w}"] for w in "ab"}
        for m, c in (("lnbpe", D), ("mhalf", 1), ("ones", 128), ("zero", D)):
            W[m] = S.sb(m, [128, c])
        groups = dict.fromkeys(g for _, _, g in WEIGHTS.values())
        W["sem"] = {g: S.sem("loaded_" + g) for g in groups}
        W["count"] = {g: 16 * sum(x[2] == g for x in WEIGHTS.values()) for g in groups}
        ps = ctx.enter_context(nc.psum_tensor("ps", [128, 8, 512], F32))
        slot = S.sb("slot", [128, NTILE], U32)
        owner = S.sb("owner", [1, SORT_TILES], I32)
        share = S.sb("share", [128, NTILE * 2 * PAIRS])
        set_ = S.sem("constants_set")
        h_dram = nc.dram_tensor("h_rows", (TOK, D), F32, kind="Internal").ap()
        near_dram = nc.dram_tensor("near_rows", (TOK, D), F32, kind="Internal").ap()
        sorted_dram = nc.dram_tensor("sorted_rows", (SORT_TILES * 128, D), F32, kind="Internal").ap()
        done_dram = nc.dram_tensor("done_rows", (SORT_TILES * 128, D), F32, kind="Internal").ap()

        with nc.Block() as block:
            @block.sync
            def _(sp):
                for name in WEIGHTS:
                    sp.dma_start(held[name][:, :], args[name]).then_inc(W["sem"][WEIGHTS[name][2]], 16)

            @block.gpsimd
            def _(pool):
                for t, v in ((W["mhalf"], -0.5), (W["ones"], 1.0), (W["zero"], 0.0)):
                    nc.gpsimd.memset(t[:, :], v).then_inc(set_, 1)

        with ExitStack() as early:
            E1 = Scope(W, early, "h")
            txt = E1.sem("txt_loaded")
            h96 = E1.sb("h96", [NA, B * D])
            with ExitStack() as first:
                A = Scope(W, first, "x")
                x0T, x1T, yT = (A.sb(m, [HALF, 2 * B * NI]) for m in ("x0T", "x1T", "yT"))
                embed(nc, W, ps, args["x"], x0T)
                feed_forward(nc, W, ps, "fa", x0T, yT, None)
                attention(nc, W, ps, "aa", 2 * NI, "a", yT, x0T, x1T, None, None)
                feed_forward(nc, W, ps, "fb", x1T, yT, x1T, h96)
            with nc.Block() as block:
                @block.sync
                def _(sp):
                    sp.dma_start(h96[NI:NA, :].rearrange("j (b d) -> j b d", b=B), args["txt"]).then_inc(txt, 16)
                    sp.wait_ge(txt, 16)
            attention(nc, W, ps, "ab", NA, "b", None, None, None, h96, h_dram)
        H = S.sb("H", [128, NTILE * D])
        with ExitStack() as mid:
            M = Scope(W, mid, "m")
            xn_all = M.sb("xn_all", [128, NTILE * D])
            route(nc, W, ps, H, h_dram, sorted_dram, xn_all, slot, owner)
            experts_one(nc, W, ps, H, sorted_dram, done_dram, xn_all, slot, owner)
        with ExitStack() as mid:
            xsT = Scope(W, mid, "s").sb("xsT", [HID + 1, TOK])
            squeeze(nc, W, ps, H, xsT)
            neighborhood(nc, W, ps, xsT, near_dram)
        xnT = S.sb("xnT", [HALF, 2 * TOK])
        route_four(nc, W, ps, H, near_dram, xnT, share)
        experts_four(nc, W, ps, H, xnT, share, args["out"])


def laid_out(i):
    f = np.float32

    def halves(w, bias=None):
        o = np.zeros((HALF + 1, 2, w.shape[1]), f)
        o[:HALF] = w.reshape(2, HALF, -1).transpose(1, 0, 2)
        if bias is not None:
            o[HALF, 1] = bias
        return o

    def with_row(w, bias):
        return np.concatenate([w, bias[None]], 0)

    def rows(v, p=128):
        return np.broadcast_to(v, (p, v.shape[-1]))

    def padded_heads(w, nh, dh):
        o = np.zeros(w.shape[:-1] + (nh // 4, 4, 32), f)
        o[..., :dh] = w.reshape(w.shape[:-1] + (4, nh // 4, dh)).swapaxes(-3, -2)
        return o.reshape(w.shape[:-1] + (nh * 32,))

    def qk(w, b):
        q = [padded_heads(halves(w[:, D * j:D * j + D], None if b is None else b[D * j:D * j + D]), NH, DH)
             for j in range(2)]
        return np.concatenate(q, 2)

    o = {"ident": np.eye(128, dtype=f)}
    x = i["x"].reshape(B, 3, 8, 16, 8, 16).transpose(1, 3, 5, 0, 2, 4).reshape(KC, 128, 8, 128)
    o["x"] = x.transpose(1, 2, 0, 3).reshape(128, 8 * KC * 128)
    o["txt"] = i["txt"].transpose(1, 0, 2)
    o["pw"] = i["L0_tok_patch_w"].reshape(D, KC, 128).transpose(2, 1, 0)
    o["pb"], o["lng"], o["lnb"] = (rows(i["L0_tok_" + m]) for m in ("patch_b", "ln_g", "ln_b"))
    ang = (np.arange(NI, dtype=f)[:, None] / np.power(f(10000.0), f(2.0) * np.arange(D // 2, dtype=f)[None] / f(D))).astype(f)
    pe = np.zeros((NI, D), f)
    pe[:, 0::2], pe[:, 1::2] = np.sin(ang), np.cos(ang)
    o["pe"] = np.concatenate([pe, pe], 0)
    o["ff1"] = halves(i["L0_tok_ff1_w"])[:HALF]
    o["ff1b"] = i["L0_tok_ff1_b"].reshape(KC, 128).T
    o["ff2"] = i["L0_tok_ff2_w"].reshape(KC, 128, D).transpose(1, 0, 2)
    o["ff2b"] = i["L0_tok_ff2_b"].reshape(2, HALF).T
    w, b = i["L0_tok_qkv_w"], i["L0_tok_qkv_b"]
    o["qk_a"], o["v_a"] = qk(w, b), halves(w[:, 2 * D:], b[2 * D:])
    o["proj_a"] = halves(i["L0_tok_proj_w"], i["L0_tok_proj_b"])
    o["apart"] = np.kron(1 - np.eye(2, dtype=f), np.full((NI, NI), -1e30, f))
    w = i["L0_attn_w_qkv"]
    o["qk_b"], o["v_b"] = qk(w, None), halves(w[:, 2 * D:])
    o["proj_b"] = halves(i["L0_attn_w_proj"], i["L0_attn_b_proj"])
    o["temp"] = rows(i["L0_attn_temperature"].reshape(1, NH), NA)
    o["gate"] = halves(i["L0_ffn_Wg"].T, i["L0_ffn_bg"])
    for m, w, b in (("w1", "W1", "b1"), ("w2", "W2", "b2")):
        o[m] = np.stack([halves(i["L0_ffn_" + w][e].T, i["L0_ffn_" + b][e]) for e in range(E)], 1)
    o["iota"] = rows(np.arange(32, dtype=f)[None])
    o["steps"] = rows(128 * np.arange(16, dtype=f)[None])
    o["below"] = np.triu(np.ones((128, 128), f), 1)
    n = lambda m: i["L1_attn_" + m]
    o["fc1"], o["fc1b"] = halves(n("fc1_w").T)[:HALF], n("fc1_b")[:, None]
    o["conva"], o["convab"] = n("convA_w").T, n("convA_b")[:, None]
    o["convb"], o["convbb"] = n("convB_w").T, n("convB_b")[:, None]
    w = with_row(n("qkv_w").T, n("qkv_b"))
    o["nq"], o["nk"] = (padded_heads(w[:, HID * j:HID * j + HID], NH2, DH2) for j in range(2))
    o["nv"] = w[:, 2 * HID:]
    o["np"], o["npb"] = n("proj_w").T, n("proj_b")[:, None]
    o["fc2"] = with_row(n("fc2_w").T, n("fc2_b"))
    R = 2 * WIN - 1
    wide = np.zeros((NH2, QR + KR + 2 + R, QC + KCOL + 4 + R), f)
    wide[:, QR:QR + R, QC:QC + R] = n("rpb")
    toep = np.zeros((QR, QC, NH2, KR + 2, KCOL + 4), f)
    for r in range(QR):
        for c in range(QC):
            toep[r, c] = wide[:, QR + 2 - r:QR + 2 - r + KR + 2, QC - c:QC - c + KCOL + 4]
    o["toep"] = toep
    first = lambda at, length: np.clip(at - WIN // 2, 0, length - WIN)
    outside = np.full((128, 3, 2, KR, KCOL), -1e30, f)
    for kind, c in enumerate((0, 1, COLS - 1)):
        k0 = (0, QC - WIN // 2, NA - KCOL)[kind]
        for g in range(2):
            for r in range(QR):
                for j in range(QC):
                    a = first(QR * g + r, B) - (B - KR) * g
                    b = first(QC * c + j, NA) - k0
                    outside[r * QC + j, kind, g, a:a + WIN, b:b + WIN] = 0.0
    o["outside"] = outside
    m = lambda k: i["L1_ffn_" + k]
    o["router"], o["corr"] = halves(m("router_w").T, m("router_b")), rows(m("corr_bias"))
    o["earlier"] = rows(np.tril(np.ones((4, 4), f), -1).reshape(1, 16))
    o["later"] = rows(np.triu(np.ones((4, 4), f), 1).reshape(1, 16))
    gates = [(m("gWg")[e], m("gbg")[e], m("gWu")[e], m("gbu")[e], m("gWd")[e], m("gbd")[e]) for e in range(E)]
    for j in range(2):
        c = slice(I2 * j, I2 * j + I2)
        gates.append((m("sWg")[:, c], m("sbg")[c], m("sWu")[:, c], m("sbu")[c], m("sWd")[c],
                      m("sbd") if j == 0 else np.zeros(D, f)))
    gu = [np.concatenate([halves(x[0], x[1]), halves(x[2], x[3])], 2) for x in gates]
    o["gu"] = np.stack([np.concatenate([gu[2 * q], gu[2 * q + 1]], 2) for q in range(PAIRS)], 1)
    o["dn"] = np.stack([with_row(x[4], x[5]) for x in gates], 1)
    for name, (p, c, _) in WEIGHTS.items():
        o[name] = np.ascontiguousarray(o[name]).reshape(p, c)
    return {k: np.ascontiguousarray(v, f) for k, v in o.items()}


def kernel(**inputs):
    import concourse.bacc as _bacc
    from concourse.bass_utils import run_bass_kernel_spmd as _run

    arrays = laid_out({k: np.asarray(v) for k, v in inputs.items()})
    nc = _bacc.Bacc("TRN2", target_bir_lowering=False, num_devices=1)
    args = {k: nc.dram_tensor("in_" + k, v.shape, F32, kind="ExternalInput").ap() for k, v in arrays.items()}
    args["out"] = nc.dram_tensor("out_rows", (TOK, D), F32, kind="ExternalOutput").ap()
    build(nc, args)
    r = _run(nc, [{"in_" + k: v for k, v in arrays.items()}], core_ids=[0])
    return r.results[0]["out_rows"].reshape(B, NA, D)
```

```python
import concourse.bass as bass
from concourse import mybir
from contextlib import ExitStack
import numpy as np

F32 = mybir.dt.float32
F32R = mybir.dt.float32r
U32 = mybir.dt.uint32
I32 = mybir.dt.int32
ALU = mybir.AluOpType
ACT = mybir.ActivationFunctionType
AX = mybir.AxisListType
ds = bass.ds

B = 16
NI, NT = 64, 32
NA = NI + NT
D = 192
HALF = 96
FF = 768
KC = FF // 128
NH = 12
DH = D // NH
QUADS = NH // 4
TOK = B * NA
NTILE = TOK // 128
E = 16
SORT_TILES = TOK // 128 + E - 1
EPS = 1e-5
WIN = 5
NH2, DH2 = 4, 24
HID = 96
QR, QC = 8, 16
KR, KCOL = 10, 20
NKEY = KR * KCOL
HKEY = NKEY // 2
COLS = NA // QC
PAIRS = E // 2 + 1
I2 = 96


def steady(eng, step, n, first, last, ring=2):
    assert first % ring == 0 and (last - first) % ring == 0 and first >= 2
    for s in range(first):
        step(s, s % ring)
    with eng.Fori(first // ring, last // ring) as i:
        for p in range(ring):
            step(ring * i + p, p)
    for s in range(last, n):
        step(s, s % ring)


def within(s, n):
    return 0 <= s < n if isinstance(s, int) else True


def wait(eng, sem, value):
    if not isinstance(value, int) or value > 0:
        eng.wait_ge(sem, value)


class Scope:

    def __init__(self, W, ctx, tag):
        self.nc, self.whole, self.ctx, self.tag = W["nc"], W["whole"], ctx, tag

    def sb(self, name, shape, dt=F32):
        return self.ctx.enter_context(self.nc.sbuf_tensor(f"{self.tag}_{name}", shape, dt))

    def sem(self, name):
        return self.whole.enter_context(self.nc.semaphore(f"{self.tag}_{name}"))


def norm_stats(nc, dve, mv, st, n):
    sv = st[:, 0:6 * n].rearrange("p (n s) -> p n s", s=6)
    mean, var, dif = mv[:, 0:n], mv[:, n:2 * n], mv[:, 2 * n:3 * n]
    dve.drain()
    nc.vector.tensor_tensor(mean, sv[:, :, 1], sv[:, :, 4], ALU.add)
    nc.vector.tensor_tensor(dif, sv[:, :, 1], sv[:, :, 4], ALU.subtract)
    nc.vector.tensor_tensor(var, sv[:, :, 2], sv[:, :, 5], ALU.add)
    dve.drain()
    nc.vector.tensor_scalar(mean, mean, 0.5, None, ALU.mult)
    nc.vector.tensor_scalar(var, var, 1.0 / D, EPS, ALU.mult, ALU.add)
    nc.vector.tensor_tensor(dif, dif, dif, ALU.mult)
    dve.drain()
    return nc.vector.scalar_tensor_tensor(var, dif, 0.25, var, ALU.mult, ALU.add)


def embed(nc, W, ps, args, x0T):
    with ExitStack() as ctx:
        S = Scope(W, ctx, "em")
        n = B * NI // 128
        xt = [S.sb(f"xt{p}", [128, KC * 128]) for p in range(2)]
        t1 = S.sb("t1", [128, D])
        x0 = [S.sb(f"x0{p}", [128, D]) for p in range(2)]
        st = S.sb("st", [128, 6])
        mv = S.sb("mv", [128, 2])
        rs = S.sb("rs", [128, 1])
        loaded = [S.sem(f"loaded{p}") for p in range(2)]
        patched, var_ready, rstd_ready, x0_ready, turned, x0T_ready = map(
            S.sem, ["patched", "var_ready", "rstd_ready", "x0_ready", "turned", "x0T_ready"])
        block = ctx.enter_context(nc.Block())

        @block.sync
        def _(sp):
            def step(s, p):
                wait(sp, patched, s - 1)
                sp.dma_start(xt[p][:, :], args["x"][:, ds(s * KC * 128, KC * 128)]).then_inc(loaded[p], 16)
            steady(sp, step, n, 2, n)
            load(nc, W, args, ("ff", "a", "b", "moe1"), sp)

        @block.tensor
        def _(pe):
            pe.wait_ge(W["sem"]["embed"], W["count"]["embed"])
            pe.wait_ge(W["sem"]["ident"], W["count"]["ident"])

            def step(s, p):
                if within(s, n):
                    pe.wait_ge(loaded[p], 8 * (s - p) + 16)
                    for k in range(KC):
                        mm = nc.tensor.matmul(ps[:, p, 0:D], xt[p][:, 128 * k:128 * k + 128],
                                              W["pw"][:, k * D:k * D + D], start=k == 0, stop=k == KC - 1)
                    mm.then_inc(patched, 1)
                if within(s - 1, n):
                    wait(pe, x0_ready, s)
                    wait(pe, x0T_ready, s - 2)
                    for k in range(2):
                        mm = nc.tensor.transpose(ps[0:HALF, 3 - p, 128 * k:128 * k + 128],
                                                 x0[1 - p][:, HALF * k:HALF * k + HALF], W["ident"][:, :])
                    mm.then_inc(turned, 1)
            steady(pe, step, n + 1, 2, n)

        @block.gpsimd
        def _(pool):
            def step(s, p):
                pool.wait_ge(var_ready, s + 1)
                nc.gpsimd.tensor_tensor(rs[:, :], mv[:, 1:2], W["mhalf"][:, 0:1], ALU.pow).then_inc(rstd_ready, 1)
            steady(pool, step, n, 2, n)

        @block.vector
        def _(dve):
            def step(s, p):
                dve.wait_ge(patched, s + 1)
                nc.vector.tensor_tensor(t1[:, :], ps[:, p, 0:D], W["pb"][:, :], ALU.add)
                dve.drain()
                nc.vector.bn_stats(st[:, :], t1[:, :])
                dve.drain()
                nc.vector.bn_aggr(mv[:, :], st[:, :])
                dve.drain()
                nc.vector.tensor_scalar(mv[:, 1:2], mv[:, 1:2], EPS, None, ALU.add).then_inc(var_ready, 1)
                dve.wait_ge(rstd_ready, s + 1)
                wait(dve, turned, s - 1)
                nc.vector.tensor_scalar(x0[p][:, :], t1[:, :], mv[:, 0:1], rs[:, :], ALU.subtract, ALU.mult)
                dve.drain()
                nc.vector.tensor_tensor(x0[p][:, :], x0[p][:, :], W["lng"][:, :], ALU.mult)
                dve.drain()
                nc.vector.tensor_tensor(x0[p][:, :], x0[p][:, :], W["lnbpe"][:, :], ALU.add).then_inc(x0_ready, 1)
            dve.wait_ge(W["sem"]["embed"], W["count"]["embed"])
            nc.vector.tensor_tensor(W["lnbpe"][:, :], W["lnb"][:, :], W["pe"][:, :], ALU.add)
            dve.drain()
            steady(dve, step, n, 2, n)

        @block.scalar
        def _(act):
            def step(s, p):
                act.wait_ge(turned, s + 1)
                for k in range(2):
                    cp = nc.scalar.copy(x0T[:, ds(k * B * NI + 128 * s, 128)],
                                        ps[0:HALF, 2 + p, 128 * k:128 * k + 128])
                cp.then_inc(x0T_ready, 1)
            steady(act, step, n, 2, n)


def feed_forward(nc, W, ps, tag, xin, out, res, h96=None):
    with ExitStack() as ctx:
        S = Scope(W, ctx, tag)
        N = B * NI // 2
        T = B * NI
        g = [S.sb(f"g{c}", [128, KC * N]) for c in range(2)]
        hidden, gelu_done, summed, out_ready, turned, h_ready = map(
            S.sem, ["hidden", "gelu_done", "summed", "out_ready", "turned", "h_ready"])
        block = ctx.enter_context(nc.Block())

        @block.tensor
        def _(pe):
            pe.wait_ge(W["sem"]["ff"], W["count"]["ff"])

            def up(c):
                for f in range(KC):
                    i = c * KC + f
                    wait(pe, gelu_done, i - 3)
                    for k in range(2):
                        mm = nc.tensor.matmul(ps[:, i % 4, :], W["ff1"][:, k * FF + 128 * f:k * FF + 128 * f + 128],
                                              xin[0:HALF, k * T + c * N:k * T + c * N + N],
                                              start=k == 0, stop=k == 1)
                    mm.then_inc(hidden, 1)

            def down(c):
                pe.wait_ge(gelu_done, KC * (c + 1))
                for m in range(2):
                    for f in range(KC):
                        mm = nc.tensor.matmul(ps[0:HALF, 4 + 2 * c + m, :],
                                              W["ff2"][:, f * D + HALF * m:f * D + HALF * m + HALF],
                                              g[c][:, f * N:f * N + N], start=f == 0, stop=f == KC - 1)
                    mm.then_inc(summed, 1)
            up(0)
            up(1)
            down(0)
            down(1)
            if h96 is not None:
                for b in range(0, B, 2):
                    i = b // 2
                    pe.wait_ge(out_ready, 2 if b < B // 2 else 4)
                    wait(pe, h_ready, i - 3)
                    for j in range(2):
                        for k in range(2):
                            mm = nc.tensor.transpose(ps[0:NI, i % 4, D * j + HALF * k:D * j + HALF * k + HALF],
                                                     out[0:HALF, k * T + NI * (b + j):k * T + NI * (b + j) + NI],
                                                     W["ident"][0:HALF, 0:HALF])
                    mm.then_inc(turned, 1)

        @block.scalar
        def _(act):
            for c in range(2):
                for f in range(KC):
                    i = c * KC + f
                    act.wait_ge(hidden, i + 1)
                    nc.scalar.activation(g[c][:, f * N:f * N + N], ps[:, i % 4, :], ACT.Gelu_apprx_tanh,
                                         bias=W["ff1b"][:, f:f + 1]).then_inc(gelu_done, 1)

        @block.vector
        def _(dve):
            for c in range(2):
                for m in range(2):
                    dve.wait_ge(summed, 2 * c + m + 1)
                    src = ps[0:HALF, 4 + 2 * c + m, :]
                    at = slice(m * T + c * N, m * T + c * N + N)
                    if res is None:
                        nc.vector.tensor_scalar(out[0:HALF, at], src, W["ff2b"][:, m:m + 1], None,
                                                ALU.add).then_inc(out_ready, 1)
                    else:
                        nc.vector.scalar_tensor_tensor(out[0:HALF, at], src, W["ff2b"][:, m:m + 1],
                                                       res[0:HALF, at], ALU.add, ALU.add).then_inc(out_ready, 1)
            if h96 is not None:
                for i in range(B // 2):
                    dve.wait_ge(turned, i + 1)
                    nc.vector.tensor_copy(h96[0:NI, 2 * D * i:2 * D * i + 2 * D],
                                          ps[0:NI, i % 4, 0:2 * D]).then_inc(h_ready, 1)


def attention(nc, W, ps, tag, T, w, yT, x0T, x1T, h96, h_dram):
    full = h96 is not None
    n = B if full else B * NI // T
    TI = B * NI
    with ExitStack() as ctx:
        S = Scope(W, ctx, tag)
        xb = [S.sb(f"xb{p}", [HALF + 1, 2 * T]) for p in range(2)]
        qs = [S.sb(f"qs{p}", [128, QUADS * T]) for p in range(2)]
        kd = [S.sb(f"kd{p}", [128, NH * T]) for p in range(2)]
        v = [S.sb(f"v{p}", [T, NH * (DH + 1)]) for p in range(2)]
        p_ = [S.sb(f"p{p}", [T, NH * T]) for p in range(2)]
        pT = S.sb("pT", [T, NH * T])
        nmax = S.sb("nmax", [T, NH])
        rec = S.sb("rec", [T, NH])
        on = S.sb("on", [T, D])
        oT = S.sb("oT", [HALF + 1, 2 * T])
        (xb_ready, q_done, keys_done, qkv_done, q_ready, k_ready, v_ready, scored, masked, shifted, exp_done, p_turned, 
         pT_ready, weighed, on_ready, o_turned, oT_ready, projected, added) = map(S.sem, [
             "xb_ready", "q_done", "keys_done", "qkv_done", "q_ready", "k_ready", "v_ready", "scored", "masked", "shifted",
             "exp_done", "p_turned", "pT_ready", "weighed", "on_ready", "o_turned", "oT_ready", "projected",
             "added"])
        if full:
            xn_ready, x_turned, stored = map(
                S.sem, ["xn_ready", "x_turned", "stored"])
            dm = S.sb("dm", [T, NH * T])
            ntemp = S.sb("ntemp", [T, NH])
            xn = [S.sb(f"xn{p}", [T, D]) for p in range(2)]
            st = S.sb("st", [T, 6 * B])
            mv = S.sb("mv", [T, 3 * B])
            rs = S.sb("rs", [T, B])
        scores = ps[0:T, 0:QUADS, 0:4 * T]
        bv, bq, bk, bo, bt = 3, 4, 5, 6, 7
        RC = 2 * T
        XC = QUADS * NA
        ones_set, ones_due = W["ones_set"], W["due"]("ones_set", 7)
        stat_done, rstd_ready, norm_due = W["stat_done"], W["rstd_ready"], W["due"]("norm", int(full))

        def key_rows(p, h):
            return kd[p][32 * h:32 * h + 32, :].rearrange("r (g m n) -> r g m n", g=QUADS, m=4)[:, :, h, :]
        block = ctx.enter_context(nc.Block())

        if full:
            @block.sync
            def _(sp):
                def step(s, p):
                    sp.wait_ge(added, s + 1)
                    sp.dma_start(h_dram[ds(s * NA, NA), :], h96[:, ds(s * D, D)]).then_inc(stored, 16)
                steady(sp, step, B, 2, B)
                sp.wait_ge(stored, 16 * B)

        @block.gpsimd
        def _(pool):
            if full:
                pool.wait_ge(stat_done, norm_due)
                nc.gpsimd.tensor_tensor(rs[:, :], mv[:, B:2 * B], W["mhalf"][0:T, 0:1].broadcast_to([T, B]),
                                        ALU.pow).then_inc(rstd_ready, 1)
            else:
                def step(s, p):
                    wait(pool, qkv_done, s - 1)
                    for k in range(2):
                        cp = nc.gpsimd.tensor_copy(xb[p][0:HALF, T * k:T * k + T], yT[:, ds(k * TI + s * T, T)])
                    cp.then_inc(xb_ready, 1)
                steady(pool, step, n, 2, n)

        @block.tensor
        def _(pe):
            pe.wait_ge(ones_set, ones_due)
            pe.wait_ge(W["sem"][w], W["count"][w])

            def turn_x(b, p):
                wait(pe, q_ready, b)
                pe.wait_ge(xn_ready, b + 1)
                for k in range(2):
                    mm = nc.tensor.transpose(ps[0:HALF, bq, XC + T * k:XC + T * k + T],
                                             xn[p][:, HALF * k:HALF * k + HALF], W["ident"][0:T, 0:T])
                mm.then_inc(x_turned, 1)

            def heads(p, at, bank):
                for g in range(QUADS):
                    for k in range(2):
                        mm = nc.tensor.matmul(ps[:, bank, T * g:T * g + T],
                                              W["qk"][w][0:HALF + k, k * 768 + at + 128 * g:k * 768 + at + 128 * g + 128],
                                              xb[p][0:HALF + k, T * k:T * k + T], start=k == 0, stop=k == 1)
                return mm

            def queries(b, p):
                pe.wait_ge(xb_ready, b + 1)
                heads(p, 0, bq).then_inc(q_done, 1)

            def keys(b, p):
                heads(p, QUADS * 128, bk).then_inc(keys_done, 1)

            def values(b, p):
                wait(pe, v_ready, b)
                for k in range(2):
                    mm = nc.tensor.matmul(ps[0:T, bv, 0:D], xb[p][0:HALF + k, T * k:T * k + T],
                                          W["v"][w][0:HALF + k, k * D:k * D + D], start=k == 0, stop=k == 1)
                mm.then_inc(qkv_done, 1)

            def score(b, p):
                pe.wait_ge(q_ready, b + 1)
                pe.wait_ge(k_ready, 2 * b + 2)
                for g in range(QUADS):
                    mm = nc.tensor.matmul(ps[0:T, g, 0:4 * T], qs[p][:, T * g:T * g + T],
                                          kd[p][:, 4 * T * g:4 * T * (g + 1)], start=True, stop=True)
                mm.then_inc(scored, 1)

            def turn_p(b, p):
                pe.wait_ge(exp_done, b + 1)
                pe.wait_ge(masked, min(b + 2, n) if isinstance(b, int) else b + 2)
                for c in range(3):
                    for j in range(4):
                        mm = nc.tensor.transpose(ps[0:T, c, T * j:T * j + T],
                                                 p_[p][:, T * (4 * c + j):T * (4 * c + j) + T], W["ident"][0:T, 0:T])
                    mm.then_inc(p_turned, 1)

            def weigh(b, p, heads):
                for h in heads:
                    mm = nc.tensor.matmul(ps[0:T, bo, (DH + 1) * h:(DH + 1) * (h + 1)], pT[:, T * h:T * h + T],
                                          v[p][:, (DH + 1) * h:(DH + 1) * (h + 1)], start=True, stop=True)
                return mm

            def weigh_first(b, p):
                pe.wait_ge(pT_ready, 2 * b + 2)
                pe.wait_ge(v_ready, b + 1)
                weigh(b, p, range(0, 4))

            def weigh_second(b, p):
                weigh(b, p, range(4, 8))

            def weigh_third(b, p):
                weigh(b, p, range(8, NH)).then_inc(weighed, 1)

            def turn_o(b, p):
                pe.wait_ge(on_ready, b + 1)
                wait(pe, added, b)
                for k in range(2):
                    mm = nc.tensor.transpose(ps[0:HALF, bt, T * k:T * k + T], on[:, HALF * k:HALF * k + HALF],
                                             W["ident"][0:T, 0:T])
                mm.then_inc(o_turned, 1)

            def project(b, p):
                pe.wait_ge(oT_ready, b + 1)
                if full:
                    for k in range(2):
                        mm = nc.tensor.matmul(ps[0:T, bt, RC:RC + D], oT[0:HALF + k, T * k:T * k + T],
                                              W["proj"][w][0:HALF + k, k * D:k * D + D], start=k == 0, stop=k == 1)
                else:
                    for m in range(2):
                        for k in range(2):
                            mm = nc.tensor.matmul(ps[0:HALF, bt, RC + T * m:RC + T * m + T],
                                                  W["proj"][w][0:HALF + k, k * D + HALF * m:k * D + HALF * m + HALF],
                                                  oT[0:HALF + k, T * k:T * k + T], start=k == 0, stop=k == 1)
                mm.then_inc(projected, 1)

            def step(s, p):
                for stage, lag in ((score, 2), (queries, 1), (weigh_third, 4), (turn_p, 3), (keys, 1), (turn_o, 4),
                                   (weigh_first, 3), (values, 1), (project, 4), (weigh_second, 3), (turn_x, 0)):
                    if within(s - lag, n) and (full or stage is not turn_x):
                        stage(s - lag, (p + lag) % 2)
            steady(pe, step, n + 4, 6, n)

        @block.scalar
        def _(act):
            act.wait_ge(ones_set, ones_due)

            def copy_q(b, p):
                act.wait_ge(q_done, b + 1)
                nc.scalar.copy(qs[p][:, :], ps[:, bq, 0:QUADS * T]).then_inc(q_ready, 1)

            def copy_pT(b, p):
                act.wait_ge(p_turned, 3 * b + 2)
                nc.scalar.copy(pT[:, 0:8 * T].rearrange("t (c n) -> t c n", c=2),
                               ps[0:T, 0:2, 0:4 * T]).then_inc(pT_ready, 1)

            def copy_k(b, p):
                act.wait_ge(keys_done, b + 1)
                for h in range(3):
                    cp = nc.scalar.copy(key_rows(p, h), ps[32 * h:32 * h + 32, bk, 0:QUADS * T].rearrange(
                        "r (g n) -> r g n", g=QUADS))
                cp.then_inc(k_ready, 1)

            def copy_v(b, p):
                act.wait_ge(qkv_done, b + 1)
                wait(act, weighed, b - 1)
                nc.scalar.copy(v[p][:, :].rearrange("t (h d) -> t h d", h=NH)[:, :, 0:DH],
                               ps[0:T, bv, 0:D].rearrange("t (h d) -> t h d", h=NH)).then_inc(v_ready, 1)

            def exp(b, p):
                act.wait_ge(shifted, b + 1)
                nc.scalar.activation(p_[p][:, :], p_[p][:, :], ACT.Exp, scale=DH ** -0.5).then_inc(exp_done, 1)

            def copy_x(b, p):
                act.wait_ge(x_turned, b + 1)
                nc.scalar.copy(xb[p][0:HALF, :], ps[0:HALF, bq, XC:XC + 2 * T]).then_inc(xb_ready, 1)

            def copy_o(b, p):
                act.wait_ge(o_turned, b + 1)
                nc.scalar.copy(oT[0:HALF, :], ps[0:HALF, bt, 0:2 * T]).then_inc(oT_ready, 1)

            def step(s, p):
                for stage, lag in ((copy_q, 1), (copy_v, 2), (copy_pT, 3), (copy_k, 1), (copy_o, 4), (exp, 2),
                                   (copy_x, 0)):
                    if within(s - lag, n) and (full or stage is not copy_x):
                        stage(s - lag, (p + lag) % 2)
            steady(act, step, n + 4, 6, n)

        @block.vector
        def _(dve):
            for p in range(2):
                nc.vector.memset(xb[p][HALF:HALF + 1, :], 1.0).then_inc(ones_set, 1)
                nc.vector.memset(v[p][:, :], 1.0).then_inc(ones_set, 1)
                nc.vector.memset(kd[p][:, :], 0.0).then_inc(ones_set, 1)
            nc.vector.memset(oT[HALF:HALF + 1, :], 1.0).then_inc(ones_set, 1)
            dve.wait_ge(W["sem"][w], W["count"][w])
            if full:
                nc.vector.tensor_scalar(ntemp[:, :], W["temp"][:, :], -1.0, None, ALU.mult)
                dve.drain()
                for j in range(NH):
                    nc.vector.tensor_scalar(dm[:, T * j:T * j + T], W["ident"][0:T, 0:T], ntemp[:, j:j + 1], 1.0,
                                            ALU.mult, ALU.add)
                with dve.Fori(0, B) as b:
                    nc.vector.bn_stats(st[:, ds(6 * b, 6)], h96[:, ds(b * D, D)])
                norm_stats(nc, dve, mv, st, B).then_inc(stat_done, 1)
                dve.wait_ge(rstd_ready, norm_due)

            def norm(b, p):
                wait(dve, x_turned, b - 1)
                nc.vector.tensor_scalar(xn[p][:, :], h96[:, ds(b * D, D)], mv[:, ds(b, 1)], rs[:, ds(b, 1)],
                                        ALU.subtract, ALU.mult).then_inc(xn_ready, 1)

            def mask(b, p):
                dve.wait_ge(scored, b + 1)
                if full:
                    nc.vector.tensor_tensor(p_[p][:, :].rearrange("t (g n) -> t g n", g=QUADS), scores,
                                            dm[:, :].rearrange("t (g n) -> t g n", g=QUADS), ALU.mult).then_inc(masked, 1)
                else:
                    nc.vector.tensor_tensor(p_[p][:, :].rearrange("t (g r n) -> t g r n", r=4, g=QUADS),
                                            scores.rearrange("t g (r n) -> t g r n", r=4),
                                            W["apart"][:, None, None, :].broadcast_to([T, QUADS, 4, T]),
                                            ALU.add).then_inc(masked, 1)

            def biggest(b, p):
                dve.drain()
                nc.vector.tensor_reduce(nmax[:, :], p_[p][:, :].rearrange("t (h n) -> t h n", h=NH), AX.X, ALU.max,
                                        negate=True)

            def copy_pT(b, p):
                dve.wait_ge(p_turned, 3 * b + 3)
                nc.vector.tensor_copy(pT[:, 8 * T:12 * T], ps[0:T, 2, 0:4 * T]).then_inc(pT_ready, 1)

            def copy_k(b, p):
                dve.wait_ge(keys_done, b + 1)
                nc.vector.tensor_copy(key_rows(p, 3), ps[96:128, bk, 0:QUADS * T].rearrange(
                    "r (g n) -> r g n", g=QUADS)).then_inc(k_ready, 1)

            def shift(b, p):
                ph = p_[p][:, :].rearrange("t (h n) -> t h n", h=NH)
                dve.drain()
                nc.vector.tensor_tensor(ph, ph, nmax[:, :, None].broadcast_to([T, NH, T]),
                                        ALU.add).then_inc(shifted, 1)

            def normalize(b, p):
                dve.wait_ge(weighed, b + 1)
                o = ps[0:T, bo, 0:NH * (DH + 1)].rearrange("t (h d) -> t h d", h=NH)
                nc.vector.reciprocal(rec[:, :], o[:, :, DH])
                dve.drain()
                nc.vector.tensor_tensor(on[:, :].rearrange("t (h d) -> t h d", h=NH), o[:, :, 0:DH],
                                        rec[:, :, None].broadcast_to([T, NH, DH]), ALU.mult).then_inc(on_ready, 1)

            def add(b, p):
                dve.wait_ge(projected, b + 1)
                if full:
                    nc.vector.tensor_tensor(h96[:, ds(b * D, D)], h96[:, ds(b * D, D)], ps[0:T, bt, RC:RC + D],
                                            ALU.add).then_inc(added, 1)
                else:
                    out = x1T[:, :].rearrange("f (k t) -> f k t", k=2)[:, :, ds(b * T, T)]
                    res = x0T[:, :].rearrange("f (k t) -> f k t", k=2)[:, :, ds(b * T, T)]
                    nc.vector.tensor_tensor(out, ps[0:HALF, bt, RC:RC + 2 * T].rearrange("f (k t) -> f k t", k=2),
                                            res, ALU.add).then_inc(added, 1)

            def step(s, p):
                for stage, lag in ((mask, 2), (normalize, 4), (biggest, 2), (copy_pT, 3), (norm, 0), (shift, 2),
                                   (copy_k, 1), (add, 4)):
                    if within(s - lag, n) and (full or stage is not norm):
                        stage(s - lag, (p + lag) % 2)
            steady(dve, step, n + 4, 6, n)


def prefix_sum(nc, dve, bufs, lead, n, width):
    a, b, d = bufs[0], bufs[1], 1
    P = a.shape[0]
    while d < n:
        o = lead * width
        nc.vector.tensor_tensor(b[:, o:o + n * width], a[:, o:o + n * width],
                                a[:, o - d * width:o + (n - d) * width], ALU.add)
        dve.drain()
        a, b, d = b, a, 2 * d
    return a


def choose(nc, dve, top, at, values, n):
    for t in range(n):
        nc.vector.max(top[:, 8 * t:8 * t + 8], values[:, E * t:E * t + E])
    dve.drain()
    for t in range(n):
        nc.vector.max_index(at[:, 8 * t:8 * t + 8], top[:, 8 * t:8 * t + 8], values[:, E * t:E * t + E])
    dve.drain()


def route(nc, W, ps, H, h_dram, sorted_dram, xn_all, slot, owner):
    with ExitStack() as ctx:
        S = Scope(W, ctx, "rt")
        n = NTILE
        st, mv, rs = S.sb("st", [128, 6 * n]), S.sb("mv", [128, 3 * n]), S.sb("rs", [128, n])
        xn = [S.sb(f"xn{p}", [128, D]) for p in range(2)]
        xT = [S.sb(f"xT{p}", [HALF + 1, 256]) for p in range(2)]
        logits = S.sb("logits", [128, n * E])
        top, at = S.sb("top", [128, 8 * n]), S.sb("at", [128, 8 * n], U32)
        first = S.sb("first", [128, n])
        oh = S.sb("oh", [128, n * E])
        LEAD = 8
        cum = [S.sb(f"cum{i}", [128, (LEAD + n) * E]) for i in range(2)]
        cnt = [S.sb(f"cnt{i}", [128, LEAD + E]) for i in range(2)]
        over = S.sb("over", [128, E * n])
        tiles, base = S.sb("tiles", [128, E]), S.sb("base", [128, E])
        rank = S.sb("rank", [128, n * E])
        posf = S.sb("posf", [128, n])
        before = S.sb("before", [1, SORT_TILES * E])
        ownf = S.sb("ownf", [1, SORT_TILES])
        (loaded, xn_ready, kept, turned, xT_ready, gated, oh_ready, counted,
         slot_ready, scattered, zeroed) = map(S.sem, [
             "loaded", "xn_ready", "kept", "turned", "xT_ready", "gated",
             "oh_ready", "counted", "slot_ready", "scattered", "zeroed"])
        ones_set, ones_due = W["ones_set"], W["due"]("ones_set", 2)
        stat_done, rstd_ready, norm_due = W["stat_done"], W["rstd_ready"], W["due"]("norm", 1)
        block = ctx.enter_context(nc.Block())

        @block.sync
        def _(sp):
            sp.dma_start(H[:, :].rearrange("p (t d) -> p t d", t=n),
                         h_dram.rearrange("(t p) d -> p t d", p=128)).then_inc(loaded, 16)
            sp.dma_start(sorted_dram.rearrange("(t p) d -> p t d", p=128),
                         W["zero"][:, None, :].broadcast_to([128, SORT_TILES, D])).then_inc(zeroed, 16)

        @block.gpsimd
        def _(pool):
            pool.wait_ge(stat_done, norm_due)
            nc.gpsimd.tensor_tensor(rs[:, :], mv[:, n:2 * n], W["mhalf"][:, 0:1].broadcast_to([128, n]),
                                    ALU.pow).then_inc(rstd_ready, 1)

            def step(s, p):
                pool.wait_ge(xn_ready, s + 1)
                nc.gpsimd.tensor_copy(xn_all[:, ds(s * D, D)], xn[p][:, :]).then_inc(kept, 1)
            steady(pool, step, n, 2, n)
            pool.wait_ge(slot_ready, 1)
            pool.wait_ge(zeroed, 16)
            pool.wait_ge(kept, n)
            for t in range(n):
                nc.gpsimd.indirect_dma_start(
                    out=sorted_dram, out_offset=bass.IndirectOffsetOnAxis(ap=slot[:, t:t + 1], axis=0),
                    in_=xn_all[:, t * D:t * D + D], in_offset=None).then_inc(scattered, 16)
            pool.wait_ge(scattered, 16 * n)

        @block.tensor
        def _(pe):
            pe.wait_ge(ones_set, ones_due)
            pe.wait_ge(W["sem"]["moe1"], W["count"]["moe1"])

            def step(s, p):
                if within(s, n):
                    pe.wait_ge(xn_ready, s + 1)
                    wait(pe, xT_ready, s - 1)
                    for k in range(2):
                        mm = nc.tensor.transpose(ps[0:HALF, p, 128 * k:128 * k + 128],
                                                 xn[p][:, HALF * k:HALF * k + HALF], W["ident"][:, :])
                    mm.then_inc(turned, 1)
                if within(s - 1, n):
                    wait(pe, xT_ready, s)
                    for k in range(2):
                        mm = nc.tensor.matmul(ps[:, 2, ds(E * (s - 1), E)], xT[1 - p][0:HALF + k, 128 * k:128 * k + 128],
                                              W["gate"][0:HALF + k, E * k:E * k + E], start=k == 0, stop=k == 1)
                    mm.then_inc(gated, 1)
            steady(pe, step, n + 1, 2, n)
            pe.wait_ge(oh_ready, 1)
            nc.tensor.matmul(ps[:, 3, 0:n * E], W["below"][:, :], oh[:, :], start=True, stop=True)
            nc.tensor.matmul(ps[:, 4, 0:n * E], W["ones"][:, :], oh[:, :], start=True, stop=True).then_inc(counted, 1)

        @block.scalar
        def _(act):
            def step(s, p):
                act.wait_ge(turned, s + 1)
                wait(act, gated, s - 1)
                nc.scalar.copy(xT[p][0:HALF, :], ps[0:HALF, p, 0:256]).then_inc(xT_ready, 1)
            act.wait_ge(ones_set, ones_due)
            steady(act, step, n, 2, n)

        @block.vector
        def _(dve):
            for p in range(2):
                nc.vector.memset(xT[p][HALF:HALF + 1, :], 1.0).then_inc(ones_set, 1)
            dve.wait_ge(loaded, 16)
            with dve.Fori(0, n) as t:
                nc.vector.bn_stats(st[:, ds(6 * t, 6)], H[:, ds(t * D, D)])
            norm_stats(nc, dve, mv, st, n).then_inc(stat_done, 1)
            for c in cum + cnt:
                nc.vector.memset(c[:, :], 0.0)
            dve.wait_ge(rstd_ready, norm_due)

            def step(s, p):
                wait(dve, turned, s - 1)
                wait(dve, kept, s - 1)
                nc.vector.tensor_scalar(xn[p][:, :], H[:, ds(s * D, D)], mv[:, ds(s, 1)], rs[:, ds(s, 1)],
                                        ALU.subtract, ALU.mult).then_inc(xn_ready, 1)
            steady(dve, step, n, 2, n)
            dve.wait_ge(gated, n)
            nc.vector.tensor_copy(logits[:, :], ps[:, 2, 0:n * E])
            dve.drain()
            choose(nc, dve, top, at, logits, n)
            nc.vector.tensor_copy(first[:, :], at[:, 0:8 * n:8])
            dve.drain()
            nc.vector.tensor_tensor(oh[:, :].rearrange("p (t e) -> p t e", t=n),
                                    W["iota"][:, None, 0:E].broadcast_to([128, n, E]),
                                    first[:, :, None].broadcast_to([128, n, E]), ALU.is_equal).then_inc(oh_ready, 1)
            dve.wait_ge(counted, 1)
            nc.vector.tensor_copy(cum[0][:, LEAD * E:], ps[:, 4, 0:n * E])
            dve.drain()
            c = prefix_sum(nc, dve, cum, LEAD, n, E)
            total = c[:, (LEAD + n - 1) * E:(LEAD + n) * E]
            nc.vector.tensor_tensor(over[:, :].rearrange("p (e k) -> p e k", e=E),
                                    total[:, :, None].broadcast_to([128, E, n]),
                                    W["steps"][:, None, 0:n].broadcast_to([128, E, n]), ALU.is_gt)
            dve.drain()
            nc.vector.tensor_reduce(tiles[:, :], over[:, :].rearrange("p (e k) -> p e k", e=E), AX.X, ALU.add)
            dve.drain()
            nc.vector.tensor_copy(cnt[0][:, LEAD:], tiles[:, :])
            dve.drain()
            ends = prefix_sum(nc, dve, cnt, LEAD, E, 1)[:, LEAD:]
            nc.vector.tensor_tensor(base[:, :], ends, tiles[:, :], ALU.subtract)
            nc.vector.tensor_tensor(before[:, :].rearrange("p (j e) -> p j e", j=SORT_TILES),
                                    ends[0:1, None, :].broadcast_to([1, SORT_TILES, E]),
                                    W["iota"][0:1, 0:SORT_TILES, None].broadcast_to([1, SORT_TILES, E]), ALU.is_le)
            nc.vector.tensor_tensor(rank[:, :], ps[:, 3, 0:n * E], c[:, (LEAD - 1) * E:(LEAD + n - 1) * E], ALU.add)
            dve.drain()
            nc.vector.tensor_scalar(base[:, :], base[:, :], 128.0, None, ALU.mult)
            nc.vector.tensor_reduce(ownf[:, :], before[:, :].rearrange("p (j e) -> p j e", j=SORT_TILES), AX.X,
                                    ALU.add)
            dve.drain()
            r3 = rank[:, :].rearrange("p (t e) -> p t e", t=n)
            nc.vector.tensor_tensor(r3, r3, base[:, None, :].broadcast_to([128, n, E]), ALU.add)
            nc.vector.tensor_scalar(owner[:, :], ownf[:, :], float(E - 1), None, ALU.min)
            dve.drain()
            nc.vector.tensor_tensor(rank[:, :], rank[:, :], oh[:, :], ALU.mult)
            dve.drain()
            nc.vector.tensor_reduce(posf[:, :], r3, AX.X, ALU.add)
            dve.drain()
            nc.vector.tensor_copy(slot[:, :], posf[:, :]).then_inc(slot_ready, 1)


def experts_one(nc, W, ps, H, sorted_dram, done_dram, xn_all, slot, owner):
    with ExitStack() as ctx:
        S = Scope(W, ctx, "e1")
        n = SORT_TILES
        RING = 4
        xr = [S.sb(f"xr{r}", [128, D]) for r in range(RING)]
        xT = [S.sb(f"xT{p}", [HALF + 1, 256]) for p in range(2)]
        g = [S.sb(f"g{p}", [128, D]) for p in range(2)]
        gT = [S.sb(f"gT{p}", [HALF + 1, 256]) for p in range(2)]
        y = [S.sb(f"y{r}", [128, D]) for r in range(RING)]
        loaded = [S.sem(f"loaded{r}") for r in range(RING)]
        stored = [S.sem(f"stored{r}") for r in range(RING)]
        (x_turned, xT_ready, up_done, g_ready, g_turned, gT_ready, down_done, y_ready,
         gathered) = map(S.sem, [
             "x_turned", "xT_ready", "up_done", "g_ready", "g_turned", "gT_ready", "down_done", "y_ready",
             "gathered"])
        ones_set, ones_due = W["ones_set"], W["due"]("ones_set", 4)
        block = ctx.enter_context(nc.Block())
        WE = 2 * D
        LAG = 7
        FIRST, LAST = 2 * RING, n - n % RING

        def each_stored(eng):
            for r in range(RING):
                eng.wait_ge(stored[r], 16 * len(range(r, n, RING)))

        @block.sync
        def _(sp):
            def step(s, r):
                if within(s, n):
                    wait(sp, x_turned, s - RING + 1)
                    sp.dma_start(xr[r][:, :], sorted_dram[ds(128 * s, 128), :]).then_inc(loaded[r], 16)
                if within(s - LAG, n):
                    ry = (r - LAG) % RING
                    sp.wait_ge(y_ready, s - LAG + 1)
                    sp.dma_start(done_dram[ds(128 * (s - LAG), 128), :], y[ry][:, :]).then_inc(stored[ry], 16)
            steady(sp, step, n + LAG, FIRST, LAST, RING)
            each_stored(sp)

        @block.tensor
        def _(pe):
            pe.wait_ge(ones_set, ones_due)
            pe.wait_ge(W["sem"]["moe1"], W["count"]["moe1"])

            def expert(s):
                return pe.value_load(owner[0:1, ds(s, 1)], min_val=0, max_val=E - 1)

            def step(s, r):
                p = r % 2
                if within(s, n):
                    pe.wait_ge(loaded[r], 16 // RING * (s - r) + 16)
                    for k in range(2):
                        mm = nc.tensor.transpose(ps[0:HALF, p, 128 * k:128 * k + 128],
                                                 xr[r][:, HALF * k:HALF * k + HALF], W["ident"][:, :])
                    mm.then_inc(x_turned, 1)
                if within(s - 1, n):
                    e = expert(s - 1)
                    pe.wait_ge(xT_ready, s)
                    for k in range(2):
                        mm = nc.tensor.matmul(ps[:, 3 - p, 0:D], xT[1 - p][0:HALF + k, 128 * k:128 * k + 128],
                                              W["w1"][0:HALF + k, ds(e * WE + D * k, D)], start=k == 0, stop=k == 1)
                    mm.then_inc(up_done, 1)
                if within(s - 2, n):
                    pe.wait_ge(g_ready, s - 1)
                    for k in range(2):
                        mm = nc.tensor.transpose(ps[0:HALF, 4 + p, 128 * k:128 * k + 128],
                                                 g[p][:, HALF * k:HALF * k + HALF], W["ident"][:, :])
                    mm.then_inc(g_turned, 1)
                if within(s - 3, n):
                    e = expert(s - 3)
                    pe.wait_ge(gT_ready, s - 2)
                    wait(pe, y_ready, s - 4)
                    for k in range(2):
                        mm = nc.tensor.matmul(ps[:, 7 - p, 0:D], gT[1 - p][0:HALF + k, 128 * k:128 * k + 128],
                                              W["w2"][0:HALF + k, ds(e * WE + D * k, D)], start=k == 0, stop=k == 1)
                    mm.then_inc(down_done, 1)
            steady(pe, step, n + 3, FIRST, LAST, RING)

        @block.scalar
        def _(act):
            act.wait_ge(ones_set, ones_due)

            def step(s, p):
                if within(s, n):
                    act.wait_ge(x_turned, s + 1)
                    nc.scalar.copy(xT[p][0:HALF, :], ps[0:HALF, p, 0:256]).then_inc(xT_ready, 1)
                if within(s - 1, n):
                    wait(act, up_done, s)
                    nc.scalar.activation(g[1 - p][:, :], ps[:, 3 - p, 0:D], ACT.Gelu).then_inc(g_ready, 1)
            steady(act, step, n + 1, 2, n - 1)

        @block.vector
        def _(dve):
            for x in xT + gT:
                nc.vector.memset(x[HALF:HALF + 1, :], 1.0).then_inc(ones_set, 1)
            dve.wait_ge(ones_set, ones_due)

            def step(s, r):
                p = r % 2
                if within(s - 2, n):
                    dve.wait_ge(g_turned, s - 1)
                    nc.vector.tensor_copy(gT[p][0:HALF, :], ps[0:HALF, 4 + p, 0:256]).then_inc(gT_ready, 1)
                if within(s - 3, n):
                    ry = (r - 3) % RING
                    dve.wait_ge(down_done, s - 2)
                    wait(dve, stored[ry], 16 // RING * (s - 3 - ry))
                    nc.vector.tensor_copy(y[ry][:, :], ps[:, 7 - p, 0:D]).then_inc(y_ready, 1)
            steady(dve, step, n + 3, FIRST, LAST, RING)
            dve.wait_ge(gathered, 16 * NTILE)
            nc.vector.tensor_tensor(H[:, :], H[:, :], xn_all[:, :], ALU.add)

        @block.gpsimd
        def _(pool):
            each_stored(pool)
            for t in range(NTILE):
                nc.gpsimd.indirect_dma_start(
                    out=xn_all[:, t * D:t * D + D], out_offset=None, in_=done_dram,
                    in_offset=bass.IndirectOffsetOnAxis(ap=slot[:, t:t + 1], axis=0)).then_inc(gathered, 16)


def squeeze(nc, W, ps, args, H, xsT, bias):
    with ExitStack() as ctx:
        S = Scope(W, ctx, "sq")
        n, N = NTILE, 512
        st, mv, rs = S.sb("st", [128, 6 * n]), S.sb("mv", [128, 3 * n]), S.sb("rs", [128, n])
        xn = [S.sb(f"xn{p}", [128, D]) for p in range(2)]
        xnT = S.sb("xnT", [HALF, 2 * TOK])
        chunks = TOK // N
        f1 = [S.sb(f"f1{c}", [HID, N]) for c in range(chunks)]
        ca = [S.sb(f"ca{c}", [64, N]) for c in range(chunks)]
        cb = [S.sb(f"cb{c}", [HID, N]) for c in range(chunks)]
        (xn_ready, summed, turned, xnT_ready, fc_done, fc_ready, a_done, a_ready,
         b_done, b_ready) = map(S.sem, [
             "xn_ready", "summed", "turned", "xnT_ready", "fc_done", "fc_ready",
             "a_done", "a_ready", "b_done", "b_ready"])
        stat_done, rstd_ready, norm_due = W["stat_done"], W["rstd_ready"], W["due"]("norm", 1)
        block = ctx.enter_context(nc.Block())

        @block.sync
        def _(sp):
            for g in LATE:
                load(nc, W, args, (g,), sp)

        @block.gpsimd
        def _(pool):
            pool.wait_ge(stat_done, norm_due)
            nc.gpsimd.tensor_tensor(rs[:, :], mv[:, n:2 * n], W["mhalf"][:, 0:1].broadcast_to([128, n]),
                                    ALU.pow).then_inc(rstd_ready, 1)

            def step(s, p):
                pool.wait_ge(xn_ready, s + 1)
                nc.gpsimd.tensor_tensor(H[:, ds(s * D, D)], H[:, ds(s * D, D)], xn[p][:, :],
                                        ALU.add).then_inc(summed, 1)
            steady(pool, step, n, 2, n)
            pool.wait_ge(W["sem"]["nat"], W["count"]["nat"])
            fill_bias(nc, W, bias)

        @block.tensor
        def _(pe):
            pe.wait_ge(W["sem"]["nat"], W["count"]["nat"])

            def step(s, p):
                pe.wait_ge(xn_ready, s + 1)
                wait(pe, xnT_ready, s - 1)
                for k in range(2):
                    mm = nc.tensor.transpose(ps[0:HALF, p, 128 * k:128 * k + 128],
                                             xn[p][:, HALF * k:HALF * k + HALF], W["ident"][:, :])
                mm.then_inc(turned, 1)
            steady(pe, step, n, 2, n)
            for s in range(chunks + 2):
                if s < chunks:
                    pe.wait_ge(xnT_ready, N // 128 * (s + 1))
                    wait(pe, fc_ready, s - 1)
                    for k in range(2):
                        mm = nc.tensor.matmul(ps[0:HID, 2 + s % 2, :], W["fc1"][:, HID * k:HID * k + HID],
                                              xnT[:, k * TOK + s * N:k * TOK + s * N + N], start=k == 0, stop=k == 1)
                    mm.then_inc(fc_done, 1)
                if 0 <= s - 1 < chunks:
                    pe.wait_ge(fc_ready, s)
                    nc.tensor.matmul(ps[0:64, 4 + (s - 1) % 2, :], W["conva"][:, :], f1[s - 1][:, :],
                                     start=True, stop=True).then_inc(a_done, 1)
                if 0 <= s - 2 < chunks:
                    pe.wait_ge(a_ready, s - 1)
                    nc.tensor.matmul(ps[0:HID, 6 + (s - 2) % 2, :], W["convb"][:, :], ca[s - 2][:, :],
                                     start=True, stop=True).then_inc(b_done, 1)

        @block.scalar
        def _(act):
            def step(s, p):
                act.wait_ge(turned, s + 1)
                nc.scalar.copy(xnT[:, :].rearrange("f (k t) -> f k t", k=2)[:, :, ds(128 * s, 128)],
                               ps[0:HALF, p, 0:256].rearrange("f (k t) -> f k t", k=2)).then_inc(xnT_ready, 1)
            steady(act, step, n, 2, n)
            for s in range(chunks):
                act.wait_ge(b_ready, s + 1)
                nc.scalar.activation(xsT[0:HID, s * N:s * N + N], cb[s][:, :], ACT.Gelu)

        @block.vector
        def _(dve):
            nc.vector.memset(xsT[HID:HID + 1, :], 1.0)
            with dve.Fori(0, n) as t:
                nc.vector.bn_stats(st[:, ds(6 * t, 6)], H[:, ds(t * D, D)])
            norm_stats(nc, dve, mv, st, n).then_inc(stat_done, 1)
            dve.wait_ge(rstd_ready, norm_due)
            dve.wait_ge(W["sem"]["nat"], W["count"]["nat"])

            def step(s, p):
                wait(dve, turned, s - 1)
                wait(dve, summed, s - 1)
                nc.vector.tensor_scalar(xn[p][:, :], H[:, ds(s * D, D)], mv[:, ds(s, 1)], rs[:, ds(s, 1)],
                                        ALU.subtract, ALU.mult).then_inc(xn_ready, 1)
            steady(dve, step, n, 2, n)
            for s in range(chunks + 2):
                if s < chunks:
                    dve.wait_ge(fc_done, s + 1)
                    nc.vector.tensor_scalar(f1[s][:, :], ps[0:HID, 2 + s % 2, :], W["fc1b"][:, :], None,
                                            ALU.add).then_inc(fc_ready, 1)
                if 0 <= s - 1 < chunks:
                    dve.wait_ge(a_done, s)
                    nc.vector.tensor_scalar(ca[s - 1][:, :], ps[0:64, 4 + (s - 1) % 2, :], W["convab"][:, :], None,
                                            ALU.add).then_inc(a_ready, 1)
                if 0 <= s - 2 < chunks:
                    dve.wait_ge(b_done, s - 1)
                    nc.vector.scalar_tensor_tensor(cb[s - 2][:, :], ps[0:HID, 6 + (s - 2) % 2, :],
                                                   W["convbb"][:, :], f1[s - 2][:, :], ALU.add,
                                                   ALU.add).then_inc(b_ready, 1)


def fill_bias(nc, W, bias):
    t4 = W["toep"][:, :].rearrange("p (n a b) -> p n a b", n=NH2, a=KR + 2)
    for c in range(3):
        for g in range(2):
            a0, b0 = (2, 0)[g], (4, 2, 0)[c]
            for h in range(NH2):
                nc.gpsimd.tensor_tensor(
                    bias[c][g][:, h * NKEY:(h + 1) * NKEY].rearrange("p (a b) -> p a b", a=KR),
                    t4[:, h, a0:a0 + KR, b0:b0 + KCOL],
                    W["outside"][:, (2 * c + g) * NKEY:(2 * c + g + 1) * NKEY].rearrange("p (a b) -> p a b", a=KR),
                    ALU.add)


def neighborhood(nc, W, ps, args, xsT, bias, near_dram):
    with ExitStack() as ctx:
        S = Scope(W, ctx, "nb")
        N = 512
        qT = S.sb("qT", [128, TOK])
        kd = S.sb("kd", [128, NH2 * TOK])
        xw = [S.sb(f"xw{p}", [HID + 1, NKEY]) for p in range(2)]
        qw = [S.sb(f"qw{p}", [128, 128]) for p in range(2)]
        v = [S.sb(f"v{p}", [HKEY, 2 * NH2 * HID]) for p in range(2)]
        pr = [S.sb(f"pr{p}", [128, NH2 * NKEY]) for p in range(2)]
        nmax = [S.sb(f"nmax{p}", [128, NH2]) for p in range(2)]
        total = [S.sb(f"total{p}", [128, NH2]) for p in range(2)]
        rec = S.sb("rec", [128, NH2])
        pT = S.sb("pT", [HKEY, 2 * NH2 * 128])
        oT = S.sb("oT", [HID, 128])
        zT = S.sb("zT", [HID + 1, 128])
        y = [S.sb(f"y{p}", [128, D]) for p in range(2)]
        piece = {m: [S.sb(f"{m}{p}", [w[0], w[1] // (2 * COLS)]) for p in range(2)] for m, w in SPLIT.items()}
        stored = [S.sem(f"stored{p}") for p in range(2)]
        piece_loaded = [S.sem(f"piece_loaded{p}") for p in range(2)]
        (qk_done, q_ready, k_ready, window_ready, scored, fronted, v_ready, masked, shifted, exp_done, p_ready,
         p_turned, pT_ready, weighed, oT_ready, proj_done, zT_ready, out_done, y_ready, high_ready,
         low_ready) = map(S.sem, [
             "qk_done", "q_ready", "k_ready", "window_ready", "scored", "fronted", "v_ready", "masked", "shifted",
             "exp_done", "p_ready", "p_turned", "pT_ready", "weighed", "oT_ready", "proj_done",
             "zT_ready", "out_done", "y_ready", "high_ready", "low_ready"])
        ones_set, ones_due = W["ones_set"], W["due"]("ones_set", 4)
        block = ctx.enter_context(nc.Block())
        xs3 = xsT[0:HID + 1, :].rearrange("f (i j) -> f i j", i=B)
        q3 = qT[:, :].rearrange("f (i j) -> f i j", i=B)
        k4 = kd[:, :].rearrange("f (h i j) -> f h i j", h=NH2, i=B)
        scores = ps[:, 0:2, 0:2 * NKEY]
        bt, bv, bo, bz, by = 2, 4, 5, 6, 7
        n = 2 * COLS
        FIRST, LAST = 6, n - 2

        def column(t, g):
            return (t - g) * (QC // 2)

        def kind(t):
            return 1 if not isinstance(t, int) or 2 <= t < n - 2 else 0 if t < 2 else 2

        def key_column(t, g):
            return (0, column(t, g) - WIN // 2, NA - KCOL)[kind(t)]

        def piece_columns(m, t):
            return ds(t * (SPLIT[m][1] // n), SPLIT[m][1] // n)

        def run(eng, stages):
            def step(s, p):
                for stage, lag in stages:
                    if within(s - lag, n):
                        stage(s - lag, (p + lag) % 2)
            steady(eng, step, n + 4, FIRST, LAST)

        @block.sync
        def _(sp):
            def store(t, g):
                sp.wait_ge(y_ready, t + 1)
                sp.dma_start(near_dram.rearrange("(i j) d -> i j d", i=B)[QR * g:QR * g + QR, ds(column(t, g), QC), :],
                             y[g][:, :]).then_inc(stored[g], 16)

            def load_piece(t, g):
                wait(sp, low_ready, t - 1)
                for m in SPLIT:
                    sp.dma_start(piece[m][g][:, :], args[m][:, piece_columns(m, t)]).then_inc(piece_loaded[g], 16)
            run(sp, [(load_piece, 0), (store, 4)])
            for g in range(2):
                sp.wait_ge(stored[g], 16 * COLS)

        @block.gpsimd
        def _(pool):
            nc.gpsimd.memset(kd[:, :], 0.0).then_inc(ones_set, 1)
            pool.wait_ge(q_ready, TOK // N)

            def window(t, g):
                wait(pool, fronted, t - 1)
                nc.gpsimd.tensor_copy(qw[g][:, :].rearrange("f (a b) -> f a b", a=QR),
                                      q3[:, QR * g:QR * g + QR, ds(column(t, g), QC)])
                nc.gpsimd.tensor_copy(xw[g][:, :].rearrange("f (a b) -> f a b", a=KR),
                                      xs3[:, (B - KR) * g:(B - KR) * g + KR, ds(key_column(t, g), KCOL)]
                                      ).then_inc(window_ready, 1)

            def split_low(t, g):
                pool.wait_ge(high_ready, t + 1)
                for m in SPLIT:
                    sub = nc.gpsimd.tensor_tensor(W[m + "_low"][:, piece_columns(m, t)], piece[m][g][:, :],
                                                  W[m + "_high"][:, piece_columns(m, t)].bitcast(F32), ALU.subtract)
                sub.then_inc(low_ready, 1)
            run(pool, [(window, 0), (split_low, 2)])

        @block.tensor
        def _(pe):
            pe.wait_ge(W["sem"]["nat"], W["count"]["nat"])
            for s in range(TOK // N):
                for j, w in enumerate((W["nq"], W["nk"])):
                    wait(pe, (q_ready, k_ready)[j], (s - 1, NH2 * (s - 1))[j])
                    nc.tensor.matmul(ps[:, 2 * (s % 2) + j, :], w[:, :], xsT[0:HID + 1, s * N:s * N + N],
                                     start=True, stop=True).then_inc(qk_done, 1)
            pe.wait_ge(q_ready, TOK // N)
            pe.wait_ge(k_ready, NH2 * TOK // N)
            pe.wait_ge(ones_set, ones_due)

            def turn_p(t, g):
                pe.wait_ge(p_ready, t + 1)
                for i in range(2 * NH2):
                    mm = nc.tensor.transpose(ps[0:HKEY, bt + i // 4, 128 * (i % 4):128 * (i % 4) + 128],
                                             pr[g][:, HKEY * i:HKEY * i + HKEY], W["ident"][:, :])
                    if i % 4 == 3:
                        mm.then_inc(p_turned, 1)

            def project(t, g):
                pe.wait_ge(oT_ready, t + 1)
                nc.tensor.matmul(ps[0:HID, bz, 0:128], W["np"][:, :], oT[:, :], start=True,
                                 stop=True).then_inc(proj_done, 1)

            def score(t, g):
                pe.wait_ge(window_ready, t + 1)
                wait(pe, masked, t)
                for j in range(2):
                    mm = nc.tensor.matmul(ps[:, j, 0:2 * NKEY], qw[g][:, :],
                                          k4[:, 2 * j:2 * j + 2, (B - KR) * g:(B - KR) * g + KR,
                                             ds(key_column(t, g), KCOL)], start=True, stop=True)
                mm.then_inc(scored, 1)

            def out(t, g):
                pe.wait_ge(zT_ready, t + 1)
                wait(pe, y_ready, t)
                nc.tensor.matmul(ps[:, by, 0:D], zT[:, :], W["fc2"][:, :], start=True, stop=True).then_inc(out_done, 1)

            def values(t, g):
                wait(pe, v_ready, t)
                for h in range(2):
                    mm = nc.tensor.matmul(ps[0:HKEY, bv, HID * h:HID * h + HID], xw[g][:, HKEY * h:HKEY * h + HKEY],
                                          W["nv"][:, :], start=True, stop=True)
                mm.then_inc(fronted, 1)

            def weigh(t, g):
                pe.wait_ge(pT_ready, 2 * t + 2)
                pe.wait_ge(v_ready, t + 1)
                wait(pe, oT_ready, t)
                for i in range(2 * NH2):
                    h, j = i // 2, i % 2
                    mm = nc.tensor.matmul(ps[0:HID, bo, 0:128], v[g][:, HID * (NH2 * j + h):HID * (NH2 * j + h + 1)],
                                          pT[:, 128 * i:128 * i + 128], start=i == 0, stop=i == 2 * NH2 - 1)
                mm.then_inc(weighed, 1)
            run(pe, [(turn_p, 3), (score, 1), (project, 4), (values, 1), (weigh, 3), (out, 4)])

        @block.scalar
        def _(act):
            for s in range(TOK // N):
                act.wait_ge(qk_done, 2 * s + 1)
                nc.scalar.mul(qT[:, s * N:s * N + N], ps[:, 2 * (s % 2), :], DH2 ** -0.5).then_inc(q_ready, 1)
            act.wait_ge(ones_set, ones_due)

            def copy_o(t, g):
                act.wait_ge(weighed, t + 1)
                nc.scalar.copy(oT[:, :], ps[0:HID, bo, 0:128]).then_inc(oT_ready, 1)

            def copy_v(t, g):
                act.wait_ge(fronted, t + 1)
                wait(act, weighed, t - 1)
                heads = v[g][:, :].rearrange("k (j m) -> k j m", j=2)
                for h in range(NH2):
                    at = HID * h + DH2 * h
                    cp = nc.scalar.copy(heads[:, :, at:at + DH2],
                                        ps[0:HKEY, bv, 0:2 * HID].rearrange("k (j m) -> k j m", j=2)[
                                            :, :, DH2 * h:DH2 * h + DH2])
                cp.then_inc(v_ready, 1)

            def copy_pT(t, g):
                act.wait_ge(p_turned, 2 * t + 1)
                nc.scalar.copy(pT[:, 0:512], ps[0:HKEY, bt, :]).then_inc(pT_ready, 1)

            def bias_z(t, g):
                act.wait_ge(proj_done, t + 1)
                nc.scalar.activation(zT[0:HID, :], ps[0:HID, bz, 0:128], ACT.Identity,
                                     bias=W["npb"][:, :]).then_inc(zT_ready, 1)

            def exp(t, g):
                act.wait_ge(shifted, t + 1)
                for h in range(NH2):
                    e = nc.scalar.activation(pr[g][:, h * NKEY:(h + 1) * NKEY], pr[g][:, h * NKEY:(h + 1) * NKEY],
                                             ACT.Exp, bias=nmax[g][:, h:h + 1], accum_out=total[g][:, h:h + 1])
                e.then_inc(exp_done, 1)

            def split_high(t, g):
                act.wait_ge(piece_loaded[g], 16 * (t - g) + 32)
                for m in SPLIT:
                    cp = nc.scalar.copy(W[m + "_high"][:, piece_columns(m, t)], piece[m][g][:, :])
                cp.then_inc(high_ready, 1)
            run(act, [(copy_o, 4), (copy_v, 2), (copy_pT, 3), (bias_z, 4), (split_high, 2), (exp, 1)])

        @block.vector
        def _(dve):
            nc.vector.memset(zT[HID:HID + 1, :], 1.0).then_inc(ones_set, 1)
            for p in range(2):
                nc.vector.memset(v[p][:, :], 0.0).then_inc(ones_set, 1)
            dve.wait_ge(ones_set, ones_due)
            for s in range(TOK // N):
                dve.wait_ge(qk_done, 2 * s + 2)
                for h in range(NH2):
                    nc.vector.tensor_copy(kd[32 * h:32 * h + 32, h * TOK + s * N:h * TOK + s * N + N],
                                          ps[32 * h:32 * h + 32, 2 * (s % 2) + 1, :]).then_inc(k_ready, 1)

            def copy_pT(t, g):
                dve.wait_ge(p_turned, 2 * t + 2)
                nc.vector.tensor_copy(pT[:, 512:1024], ps[0:HKEY, bt + 1, :]).then_inc(pT_ready, 1)

            def normalize(t, g):
                dve.wait_ge(exp_done, t + 1)
                nc.vector.reciprocal(rec[:, :], total[g][:, :])
                dve.drain()
                p3 = pr[g][:, :].rearrange("p (h n) -> p h n", h=NH2)
                nc.vector.tensor_tensor(p3, p3, rec[:, :, None].broadcast_to([128, NH2, NKEY]),
                                        ALU.mult).then_inc(p_ready, 1)

            def mask(t, g):
                dve.wait_ge(scored, t + 1)
                nc.vector.tensor_tensor(pr[g][:, :].rearrange("p (j n) -> p j n", j=2), scores,
                                        bias[kind(t)][g][:, :].rearrange("p (j n) -> p j n", j=2),
                                        ALU.add).then_inc(masked, 1)

            def copy_y(t, g):
                dve.wait_ge(out_done, t + 1)
                wait(dve, stored[g], 8 * (t - g))
                nc.vector.tensor_copy(y[g][:, :], ps[:, by, 0:D]).then_inc(y_ready, 1)

            def biggest(t, g):
                dve.drain()
                nc.vector.tensor_reduce(nmax[g][:, :], pr[g][:, :].rearrange("p (h n) -> p h n", h=NH2), AX.X,
                                        ALU.max, negate=True).then_inc(shifted, 1)
            run(dve, [(copy_pT, 3), (normalize, 2), (mask, 1), (biggest, 1), (copy_y, 4)])


def route_four(nc, W, ps, H, near_dram, xnT, share):
    with ExitStack() as ctx:
        S = Scope(W, ctx, "rf")
        n, G = NTILE, 4
        add = S.sb("add", [128, n * D])
        st, mv, rs = S.sb("st", [128, 6 * n]), S.sb("mv", [128, 3 * n]), S.sb("rs", [128, n])
        xn = [S.sb(f"xn{p}", [128, D]) for p in range(2)]
        xT = [S.sb(f"xT{p}", [HALF + 1, 256]) for p in range(2)]
        sc, sfc = S.sb("sc", [128, n * E]), S.sb("sfc", [128, n * E])
        pair = S.sb("pair", [128, n * G * 6])
        gs = S.sb("gs", [128, n * G])
        ge, gt = S.sb("ge", [128, n * G * G]), S.sb("gt", [128, n * G * G])
        gm = S.sb("gm", [128, n * G])
        top, at = S.sb("top", [128, 8 * n]), S.sb("at", [128, 8 * n], U32)
        atf = S.sb("atf", [128, 8 * n])
        hit = S.sb("hit", [128, n * 4 * E])
        sel = S.sb("sel", [128, n * E])
        tot = S.sb("tot", [128, n])
        (loaded, xn_ready, turned, xT_ready, gated, kept, sig_done) = map(S.sem, [
            "loaded", "xn_ready", "turned", "xT_ready", "gated", "kept",
            "sig_done"])
        ones_set, ones_due = W["ones_set"], W["due"]("ones_set", 2)
        stat_done, rstd_ready, norm_due = W["stat_done"], W["rstd_ready"], W["due"]("norm", 1)
        block = ctx.enter_context(nc.Block())

        @block.sync
        def _(sp):
            sp.dma_start(add[:, :].rearrange("p (t d) -> p t d", t=n),
                         near_dram.rearrange("(t p) d -> p t d", p=128)).then_inc(loaded, 16)

        @block.gpsimd
        def _(pool):
            pool.wait_ge(stat_done, norm_due)
            nc.gpsimd.tensor_tensor(rs[:, :], mv[:, n:2 * n], W["mhalf"][:, 0:1].broadcast_to([128, n]),
                                    ALU.pow).then_inc(rstd_ready, 1)

            def step(s, p):
                pool.wait_ge(xT_ready, s + 1)
                nc.gpsimd.tensor_copy(xnT[0:HALF, :].rearrange("f (k t) -> f k t", k=2)[:, :, ds(128 * s, 128)],
                                      xT[p][0:HALF, :].rearrange("f (k t) -> f k t", k=2)).then_inc(kept, 1)
            steady(pool, step, n, 2, n)

        @block.tensor
        def _(pe):
            pe.wait_ge(ones_set, ones_due)
            pe.wait_ge(W["sem"]["moe2"], W["count"]["moe2"])

            def step(s, p):
                if within(s, n):
                    pe.wait_ge(xn_ready, s + 1)
                    for k in range(2):
                        mm = nc.tensor.transpose(ps[0:HALF, p, 128 * k:128 * k + 128],
                                                 xn[p][:, HALF * k:HALF * k + HALF], W["ident"][:, :])
                    mm.then_inc(turned, 1)
                if within(s - 1, n):
                    wait(pe, xT_ready, s)
                    for k in range(2):
                        mm = nc.tensor.matmul(ps[:, 2, ds(E * (s - 1), E)], xT[1 - p][0:HALF + k, 128 * k:128 * k + 128],
                                              W["router"][0:HALF + k, E * k:E * k + E], start=k == 0, stop=k == 1)
                    mm.then_inc(gated, 1)
            steady(pe, step, n + 1, 2, n)

        @block.scalar
        def _(act):
            act.wait_ge(ones_set, ones_due)

            def step(s, p):
                act.wait_ge(turned, s + 1)
                wait(act, gated, s - 1)
                wait(act, kept, s - 1)
                nc.scalar.copy(xT[p][0:HALF, :], ps[0:HALF, p, 0:256]).then_inc(xT_ready, 1)
            steady(act, step, n, 2, n)
            act.wait_ge(gated, n)
            nc.scalar.activation(sc[:, :], ps[:, 2, 0:n * E], ACT.Sigmoid).then_inc(sig_done, 1)

        @block.vector
        def _(dve):
            for p in range(2):
                nc.vector.memset(xT[p][HALF:HALF + 1, :], 1.0).then_inc(ones_set, 1)
            dve.wait_ge(loaded, 16)
            nc.vector.tensor_tensor(H[:, :], H[:, :], add[:, :], ALU.add)
            dve.drain()
            with dve.Fori(0, n) as t:
                nc.vector.bn_stats(st[:, ds(6 * t, 6)], H[:, ds(t * D, D)])
            norm_stats(nc, dve, mv, st, n).then_inc(stat_done, 1)
            dve.wait_ge(rstd_ready, norm_due)

            def step(s, p):
                wait(dve, turned, s - 1)
                nc.vector.tensor_scalar(xn[p][:, :], H[:, ds(s * D, D)], mv[:, ds(s, 1)], rs[:, ds(s, 1)],
                                        ALU.subtract, ALU.mult).then_inc(xn_ready, 1)
            steady(dve, step, n, 2, n)
            dve.wait_ge(sig_done, 1)
            dve.wait_ge(W["sem"]["moe2"], W["count"]["moe2"])
            t3 = lambda x: x[:, :].rearrange("p (t e) -> p t e", t=n)
            nc.vector.tensor_tensor(t3(sfc), t3(sc), W["corr"][:, None, :].broadcast_to([128, n, E]), ALU.add)
            dve.drain()
            s4 = sfc[:, :].rearrange("p (g e) -> p g e", e=4)
            p6 = pair[:, :].rearrange("p (g e) -> p g e", e=6)
            nc.vector.tensor_tensor(p6[:, :, 0:3], s4[:, :, 0:3], s4[:, :, 1:4], ALU.add)
            nc.vector.tensor_tensor(p6[:, :, 3:5], s4[:, :, 0:2], s4[:, :, 2:4], ALU.add)
            nc.vector.tensor_tensor(p6[:, :, 5:6], s4[:, :, 0:1], s4[:, :, 3:4], ALU.add)
            dve.drain()
            nc.vector.tensor_reduce(gs[:, :], p6, AX.X, ALU.max)
            dve.drain()
            mine = gs[:, :].rearrange("p (t g) -> p t g", g=G)[:, :, :, None].broadcast_to([128, n, G, G])
            other = gs[:, :].rearrange("p (t g) -> p t g", g=G)[:, :, None, :].broadcast_to([128, n, G, G])
            q4 = lambda x: x[:, :].rearrange("p (t g h) -> p t g h", g=G, h=G)
            q3 = lambda x: x[:, :].rearrange("p (t g) -> p t g", g=G * G)
            nc.vector.tensor_tensor(q4(ge), other, mine, ALU.is_ge)
            nc.vector.tensor_tensor(q4(gt), other, mine, ALU.is_gt)
            dve.drain()
            nc.vector.tensor_tensor(q3(ge), q3(ge), W["earlier"][:, None, :].broadcast_to([128, n, G * G]), ALU.mult)
            nc.vector.tensor_tensor(q3(gt), q3(gt), W["later"][:, None, :].broadcast_to([128, n, G * G]), ALU.mult)
            dve.drain()
            nc.vector.tensor_tensor(ge[:, :], ge[:, :], gt[:, :], ALU.add)
            dve.drain()
            nc.vector.tensor_reduce(gm[:, :], ge[:, :].rearrange("p (g h) -> p g h", h=G), AX.X, ALU.add)
            dve.drain()
            nc.vector.tensor_scalar(gm[:, :], gm[:, :], 1.5, None, ALU.is_lt)
            dve.drain()
            nc.vector.tensor_tensor(s4, s4, gm[:, :, None].broadcast_to([128, n * G, 4]), ALU.mult)
            dve.drain()
            choose(nc, dve, top, at, sfc, n)
            nc.vector.tensor_copy(atf[:, :], at[:, :])
            dve.drain()
            h4 = hit[:, :].rearrange("p (t k e) -> p t k e", t=n, k=4)
            nc.vector.tensor_tensor(
                h4, W["iota"][:, None, None, 0:E].broadcast_to([128, n, 4, E]),
                atf[:, :].rearrange("p (t k) -> p t k", t=n)[:, :, 0:4, None].broadcast_to([128, n, 4, E]),
                ALU.is_equal)
            dve.drain()
            nc.vector.tensor_reduce(t3(sel), hit[:, :].rearrange("p (t k e) -> p t e k", t=n, k=4), AX.X, ALU.add)
            dve.drain()
            nc.vector.tensor_tensor(sel[:, :], sel[:, :], sc[:, :], ALU.mult)
            dve.drain()
            nc.vector.tensor_reduce(tot[:, :], t3(sel), AX.X, ALU.add)
            dve.drain()
            nc.vector.tensor_scalar(tot[:, :], tot[:, :], 1e-20, None, ALU.add)
            dve.drain()
            nc.vector.reciprocal(tot[:, :], tot[:, :])
            dve.drain()
            nc.vector.tensor_tensor(t3(sel), t3(sel), tot[:, :, None].broadcast_to([128, n, E]), ALU.mult)
            dve.drain()
            s18 = share[:, :].rearrange("p (t e) -> p t e", t=n)
            nc.vector.tensor_scalar(s18[:, :, 0:E], t3(sel), 2.5, None, ALU.mult)
            nc.vector.memset(s18[:, :, E:E + 2], 1.0)


def experts_four(nc, W, ps, H, xnT, share, out_dram):
    with ExitStack() as ctx:
        S = Scope(W, ctx, "e4")
        n, P3 = NTILE, 3
        WP = 4 * I2
        xb = [S.sb(f"xb{p}", [HALF + 1, 256], F32R) for p in range(2)]
        xlow = [S.sb(f"xlow{p}", [HALF + 1, 256], F32R) for p in range(2)]
        sg = [S.sb(f"sg{i}", [128, 2 * I2]) for i in range(P3)]
        hh = [S.sb(f"hh{i}", [128, 2 * (I2 + 1)]) for i in range(P3)]
        hT = [S.sb(f"hT{i}", [I2 + 1, 256], F32R) for i in range(P3)]
        hlow = [S.sb(f"hlow{i}", [I2 + 1, 256], F32R) for i in range(P3)]
        y = [S.sb(f"y{p}", [128, D]) for p in range(2)]
        stored = [S.sem(f"stored{p}") for p in range(2)]
        (xb_ready, up_done, sg_ready, hh_ready, turned, hT_ready, hlow_ready, summed, y_ready) = map(S.sem, [
            "xb_ready", "up_done", "sg_ready", "hh_ready", "turned", "hT_ready", "hlow_ready", "summed", "y_ready"])
        ones_set, ones_due = W["ones_set"], W["due"]("ones_set", 4)
        block = ctx.enter_context(nc.Block())

        def tiles(eng, tile, after):
            steady(eng, tile, n, 2, n)
            after()

        def lagging(t, q, lag):
            if q >= lag:
                return t, q - lag
            if isinstance(t, int) and t == 0:
                return None
            return t - 1, q - lag + PAIRS

        @block.sync
        def _(sp):
            def tile(t, p):
                sp.wait_ge(y_ready, t + 1)
                sp.dma_start(out_dram[ds(128 * t, 128), :], y[p][:, :]).then_inc(stored[p], 16)
            tiles(sp, tile, lambda: None)
            for p in range(2):
                sp.wait_ge(stored[p], 8 * n)

        @block.gpsimd
        def _(pool):

            def tile(t, p):
                wait(pool, up_done, PAIRS * (t - 1))
                x = xnT[0:HALF, :].rearrange("f (k t) -> f k t", k=2)[:, :, ds(128 * t, 128)]
                halves = lambda b: b[p][0:HALF, :].rearrange("f (k t) -> f k t", k=2)
                nc.gpsimd.tensor_copy(halves(xb), x)
                pool.drain()
                nc.gpsimd.tensor_tensor(halves(xlow), x, halves(xb).bitcast(F32), ALU.subtract).then_inc(xb_ready, 1)
            tiles(pool, tile, lambda: None)

        @block.tensor
        def _(pe):
            pe.wait_ge(ones_set, ones_due)

            def up(t, q, p):
                i = q % P3
                if q == 0:
                    pe.wait_ge(xb_ready, t + 1)
                wait(pe, hh_ready, PAIRS * t + q - 2)
                for k in range(2):
                    for x, w in ((xb, W["gu_high"]), (xb, W["gu_low"]), (xlow, W["gu_high"])):
                        mm = nc.tensor.matmul(ps[:, i, 0:WP], x[p][0:HALF + k, 128 * k:128 * k + 128],
                                              w[0:HALF + k, (2 * q + k) * WP:(2 * q + k + 1) * WP],
                                              start=k == 0 and w is not W["gu_low"] and x is xb,
                                              stop=k == 1 and x is xlow)
                mm.then_inc(up_done, 1)

            def turn(t, q):
                i = q % P3
                pe.wait_ge(hh_ready, PAIRS * t + q + 1)
                for j in range(2):
                    mm = nc.tensor.transpose(ps[0:I2 + 1, 3 + i, 128 * j:128 * j + 128],
                                             hh[i][:, (I2 + 1) * j:(I2 + 1) * (j + 1)], W["ident"][:, :])
                mm.then_inc(turned, 1)

            def down(t, q):
                i = q % P3
                pe.wait_ge(hT_ready, PAIRS * t + q + 1)
                pe.wait_ge(hlow_ready, PAIRS * t + q + 1)
                if q == 0:
                    wait(pe, y_ready, t)
                for j in range(2):
                    for h, w in ((hT, W["dn_high"]), (hT, W["dn_low"]), (hlow, W["dn_high"])):
                        mm = nc.tensor.matmul(ps[:, 6, 0:D], h[i][:, 128 * j:128 * j + 128],
                                              w[:, (2 * q + j) * D:(2 * q + j + 1) * D],
                                              start=q == 0 and j == 0 and w is not W["dn_low"] and h is hT,
                                              stop=q == PAIRS - 1 and j == 1 and h is hlow)
                mm.then_inc(summed, 1)

            def tile(t, p):
                for q in range(PAIRS):
                    up(t, q, p)
                    if lagging(t, q, 1):
                        turn(*lagging(t, q, 1))
                    if lagging(t, q, 2):
                        down(*lagging(t, q, 2))

            def after():
                turn(n - 1, PAIRS - 1)
                down(n - 1, PAIRS - 2)
                down(n - 1, PAIRS - 1)
            tiles(pe, tile, after)

        @block.scalar
        def _(act):
            def gate(t, q):
                i = q % P3
                act.wait_ge(up_done, PAIRS * t + q + 1)
                nc.scalar.activation(sg[i][:, :].rearrange("p (j n) -> p j n", j=2),
                                     ps[:, i, 0:WP].rearrange("p (j u n) -> p j u n", j=2, u=2)[:, :, 0, :],
                                     ACT.Silu).then_inc(sg_ready, 1)

            def copy_h(t, q):
                i = q % P3
                act.wait_ge(turned, PAIRS * t + q + 1)
                nc.scalar.copy(hT[i][:, :], ps[0:I2 + 1, 3 + i, 0:256]).then_inc(hT_ready, 1)

            def tile(t, p):
                for q in range(PAIRS):
                    gate(t, q)
                    if lagging(t, q, 1):
                        copy_h(*lagging(t, q, 1))
            tiles(act, tile, lambda: copy_h(n - 1, PAIRS - 1))

        @block.vector
        def _(dve):
            for p in range(2):
                for b, v in ((xb, W["ones"]), (xlow, W["zero"])):
                    nc.vector.tensor_copy(b[p][HALF:HALF + 1, :].rearrange("f (k t) -> f k t", k=2),
                                          v[HALF:HALF + 1, None, 0:128].broadcast_to([1, 2, 128])
                                          ).then_inc(ones_set, 1)

            def split_h(t, q):
                i = q % P3
                dve.wait_ge(hT_ready, PAIRS * t + q + 1)
                nc.vector.tensor_tensor(hlow[i][:, :], ps[0:I2 + 1, 3 + i, 0:256], hT[i][:, :].bitcast(F32),
                                        ALU.subtract).then_inc(hlow_ready, 1)

            def weigh(t, q):
                i = q % P3
                dve.wait_ge(sg_ready, PAIRS * t + q + 1)
                for j in range(2):
                    o = (I2 + 1) * j
                    c = share[:, ds(t * 2 * PAIRS + 2 * q + j, 1)]
                    last = nc.vector.scalar_tensor_tensor(
                        hh[i][:, o:o + I2], sg[i][:, I2 * j:I2 * j + I2], c,
                        ps[:, i, 2 * I2 * j + I2:2 * I2 * (j + 1)], ALU.mult, ALU.mult)
                nc.vector.tensor_copy(hh[i][:, I2:2 * (I2 + 1):I2 + 1],
                                      share[:, ds(t * 2 * PAIRS + 2 * q, 2)]).then_inc(hh_ready, 1)

            def finish(t, p):
                dve.wait_ge(summed, PAIRS * (t + 1))
                wait(dve, stored[p], 8 * (t - p))
                nc.vector.tensor_tensor(y[p][:, :], ps[:, 6, 0:D], H[:, ds(t * D, D)], ALU.add).then_inc(y_ready, 1)

            def tile(t, p):
                for q in range(PAIRS):
                    weigh(t, q)
                    if lagging(t, q, 1):
                        split_h(*lagging(t, q, 1))
                    if q == 1 and lagging(t, q, 2):
                        finish(t - 1, 1 - p)

            def after():
                split_h(n - 1, PAIRS - 1)
                finish(n - 1, (n - 1) % 2)
            tiles(dve, tile, after)


WEIGHTS = {
    "ident": (128, 128, "ident"),
    "pw": (128, KC * D, "embed"), "pb": (128, D, "embed"), "lng": (128, D, "embed"), "lnb": (128, D, "embed"),
    "pe": (128, D, "embed"),
    "ff1": (HALF, 2 * FF, "ff"), "ff1b": (128, KC, "ff"), "ff2": (128, KC * D, "ff"), "ff2b": (HALF, 2, "ff"),
    "qk_a": (HALF + 1, 2 * 768, "a"), "v_a": (HALF + 1, 2 * D, "a"), "proj_a": (HALF + 1, 2 * D, "a"),
    "apart": (128, 128, "a"),
    "qk_b": (HALF + 1, 2 * 768, "b"), "v_b": (HALF + 1, 2 * D, "b"), "proj_b": (HALF + 1, 2 * D, "b"),
    "temp": (NA, NH, "b"),
    "gate": (HALF + 1, 2 * E, "moe1"), "w1": (HALF + 1, E * 2 * D, "moe1"), "w2": (HALF + 1, E * 2 * D, "moe1"),
    "iota": (128, 32, "ident"), "steps": (128, 16, "moe1"), "below": (128, 128, "moe1"),
    "fc1": (HALF, 2 * HID, "nat"), "fc1b": (HID, 1, "nat"), "conva": (HID, 64, "nat"), "convab": (64, 1, "nat"),
    "convb": (64, HID, "nat"), "convbb": (HID, 1, "nat"), "nq": (HID + 1, 128, "nat"), "nk": (HID + 1, 128, "nat"),
    "nv": (HID + 1, HID, "nat"), "np": (HID, HID, "nat"), "npb": (HID, 1, "nat"), "fc2": (HID + 1, D, "nat"),
    "toep": (128, NH2 * (KR + 2) * (KCOL + 4), "nat"), "outside": (128, 6 * NKEY, "nat"),
    "router": (HALF + 1, 2 * E, "moe2"), "corr": (128, E, "moe2"),
    "earlier": (128, 16, "moe2"), "later": (128, 16, "moe2"),
}
SPLIT = {"gu": (HALF + 1, PAIRS * 2 * 4 * I2), "dn": (I2 + 1, PAIRS * 2 * D)}


EARLY = ("embed", "ff", "a", "b")
LATE = ("nat", "moe2")


def load(nc, W, args, groups, eng):
    for name, (_, _, g) in WEIGHTS.items():
        if g in groups:
            eng.dma_start(W[name][:, :], args[name]).then_inc(W["sem"][g], 16)


def build(nc, args):
    with ExitStack() as ctx:
        def hold(groups, scope):
            return {name: scope.enter_context(nc.sbuf_tensor("w_" + name, [p, c], F32))
                    for name, (p, c, g) in WEIGHTS.items() if g in groups}
        W = {"nc": nc, "whole": ctx, **hold(("ident",), ctx)}
        S = Scope(W, ctx, "w")
        for m, c in (("lnbpe", D), ("mhalf", 1), ("ones", 128), ("zero", D)):
            W[m] = S.sb(m, [128, c])
        groups = dict.fromkeys(g for _, _, g in WEIGHTS.values())
        W["sem"] = {g: S.sem("loaded_" + g) for g in groups}
        W["count"] = {g: 16 * sum(x[2] == g for x in WEIGHTS.values()) for g in groups}
        ps = ctx.enter_context(nc.psum_tensor("ps", [128, 8, 512], F32))
        slot = S.sb("slot", [128, NTILE], U32)
        owner = S.sb("owner", [1, SORT_TILES], I32)
        share = S.sb("share", [128, NTILE * 2 * PAIRS])
        set_ = S.sem("constants_set")
        for m in ("ones_set", "stat_done", "rstd_ready"):
            W[m] = S.sem(m)
        due = {"ones_set": 0, "norm": 0}

        def due_after(name, parts):
            due[name] += parts
            return due[name]
        W["due"] = due_after
        h_dram = nc.dram_tensor("h_rows", (TOK, D), F32, kind="Internal").ap()
        near_dram = nc.dram_tensor("near_rows", (TOK, D), F32, kind="Internal").ap()
        sorted_dram = nc.dram_tensor("sorted_rows", (SORT_TILES * 128, D), F32, kind="Internal").ap()
        done_dram = nc.dram_tensor("done_rows", (SORT_TILES * 128, D), F32, kind="Internal").ap()

        H = S.sb("H", [128, NTILE * D])
        middle = ctx.enter_context(ExitStack())
        W.update(hold(("moe1",), middle))
        early = ctx.enter_context(ExitStack())
        W.update(hold(EARLY, early))
        for m in ("qk", "v", "proj"):
            W[m] = {w: W[f"{m}_{w}"] for w in "ab"}
        with nc.Block() as block:
            @block.sync
            def _(sp):
                load(nc, W, args, ("ident", "embed"), sp)

            @block.gpsimd
            def _(pool):
                for t, v in ((W["mhalf"], -0.5), (W["ones"], 1.0), (W["zero"], 0.0)):
                    nc.gpsimd.memset(t[:, :], v).then_inc(set_, 1)

        with early:
            E1 = Scope(W, early, "h")
            txt = E1.sem("txt_loaded")
            h96 = E1.sb("h96", [NA, B * D])
            with ExitStack() as first:
                A = Scope(W, first, "x")
                x0T, x1T, yT = (A.sb(m, [HALF, 2 * B * NI]) for m in ("x0T", "x1T", "yT"))
                embed(nc, W, ps, args, x0T)
                feed_forward(nc, W, ps, "fa", x0T, yT, None)
                attention(nc, W, ps, "aa", 2 * NI, "a", yT, x0T, x1T, None, None)
                feed_forward(nc, W, ps, "fb", x1T, yT, x1T, h96)
            with nc.Block() as block:
                @block.sync
                def _(sp):
                    sp.dma_start(h96[NI:NA, :].rearrange("j (b d) -> j b d", b=B), args["txt"]).then_inc(txt, 16)
                    sp.wait_ge(txt, 16)
            attention(nc, W, ps, "ab", NA, "b", None, None, None, h96, h_dram)
        with middle:
            M = Scope(W, middle, "m")
            xn_all = M.sb("xn_all", [128, NTILE * D])
            route(nc, W, ps, H, h_dram, sorted_dram, xn_all, slot, owner)
            experts_one(nc, W, ps, H, sorted_dram, done_dram, xn_all, slot, owner)
        W.update(hold(LATE, ctx))
        for m, (p, c) in SPLIT.items():
            W[m + "_high"] = S.sb(m + "_high", [p, c], F32R)
            W[m + "_low"] = S.sb(m + "_low", [p, c], F32R)
        with ExitStack() as mid:
            M = Scope(W, mid, "s")
            xsT = M.sb("xsT", [HID + 1, TOK])
            bias = [[M.sb(f"bias{c}{g}", [128, NH2 * NKEY]) for g in range(2)] for c in range(3)]
            squeeze(nc, W, ps, args, H, xsT, bias)
            neighborhood(nc, W, ps, args, xsT, bias, near_dram)
        xnT = S.sb("xnT", [HALF, 2 * TOK])
        route_four(nc, W, ps, H, near_dram, xnT, share)
        experts_four(nc, W, ps, H, xnT, share, args["out"])


def laid_out(i):
    f = np.float32

    def halves(w, bias=None):
        o = np.zeros((HALF + 1, 2, w.shape[1]), f)
        o[:HALF] = w.reshape(2, HALF, -1).transpose(1, 0, 2)
        if bias is not None:
            o[HALF, 1] = bias
        return o

    def with_row(w, bias):
        return np.concatenate([w, bias[None]], 0)

    def rows(v, p=128):
        return np.broadcast_to(v, (p, v.shape[-1]))

    def padded_heads(w, nh, dh):
        o = np.zeros(w.shape[:-1] + (nh, 32), f)
        o[..., :dh] = w.reshape(w.shape[:-1] + (nh, dh))
        return o.reshape(w.shape[:-1] + (nh * 32,))

    def qk(w, b):
        q = [padded_heads(halves(w[:, D * j:D * j + D], None if b is None else b[D * j:D * j + D]), NH, DH)
             for j in range(2)]
        return np.concatenate(q, 2)

    o = {"ident": np.eye(128, dtype=f)}
    x = i["x"].reshape(B, 3, 8, 16, 8, 16).transpose(1, 3, 5, 0, 2, 4).reshape(KC, 128, 8, 128)
    o["x"] = x.transpose(1, 2, 0, 3).reshape(128, 8 * KC * 128)
    o["txt"] = i["txt"].transpose(1, 0, 2)
    o["pw"] = i["L0_tok_patch_w"].reshape(D, KC, 128).transpose(2, 1, 0)
    o["pb"], o["lng"], o["lnb"] = (rows(i["L0_tok_" + m]) for m in ("patch_b", "ln_g", "ln_b"))
    ang = (np.arange(NI, dtype=f)[:, None] / np.power(f(10000.0), f(2.0) * np.arange(D // 2, dtype=f)[None] / f(D))).astype(f)
    pe = np.zeros((NI, D), f)
    pe[:, 0::2], pe[:, 1::2] = np.sin(ang), np.cos(ang)
    o["pe"] = np.concatenate([pe, pe], 0)
    o["ff1"] = halves(i["L0_tok_ff1_w"])[:HALF]
    o["ff1b"] = i["L0_tok_ff1_b"].reshape(KC, 128).T
    o["ff2"] = i["L0_tok_ff2_w"].reshape(KC, 128, D).transpose(1, 0, 2)
    o["ff2b"] = i["L0_tok_ff2_b"].reshape(2, HALF).T
    w, b = i["L0_tok_qkv_w"], i["L0_tok_qkv_b"]
    o["qk_a"], o["v_a"] = qk(w, b), halves(w[:, 2 * D:], b[2 * D:])
    o["proj_a"] = halves(i["L0_tok_proj_w"], i["L0_tok_proj_b"])
    o["apart"] = np.kron(1 - np.eye(2, dtype=f), np.full((NI, NI), -1e30, f))
    w = i["L0_attn_w_qkv"]
    o["qk_b"], o["v_b"] = qk(w, None), halves(w[:, 2 * D:])
    o["proj_b"] = halves(i["L0_attn_w_proj"], i["L0_attn_b_proj"])
    o["temp"] = rows(i["L0_attn_temperature"].reshape(1, NH), NA)
    o["gate"] = halves(i["L0_ffn_Wg"].T, i["L0_ffn_bg"])
    for m, w, b in (("w1", "W1", "b1"), ("w2", "W2", "b2")):
        o[m] = np.stack([halves(i["L0_ffn_" + w][e].T, i["L0_ffn_" + b][e]) for e in range(E)], 1)
    o["iota"] = rows(np.arange(32, dtype=f)[None])
    o["steps"] = rows(128 * np.arange(16, dtype=f)[None])
    o["below"] = np.triu(np.ones((128, 128), f), 1)
    n = lambda m: i["L1_attn_" + m]
    o["fc1"], o["fc1b"] = halves(n("fc1_w").T)[:HALF], n("fc1_b")[:, None]
    o["conva"], o["convab"] = n("convA_w").T, n("convA_b")[:, None]
    o["convb"], o["convbb"] = n("convB_w").T, n("convB_b")[:, None]
    w = with_row(n("qkv_w").T, n("qkv_b"))
    o["nq"], o["nk"] = (padded_heads(w[:, HID * j:HID * j + HID], NH2, DH2) for j in range(2))
    o["nv"] = w[:, 2 * HID:]
    o["np"], o["npb"] = n("proj_w").T, n("proj_b")[:, None]
    o["fc2"] = with_row(n("fc2_w").T, n("fc2_b"))
    R = 2 * WIN - 1
    wide = np.zeros((NH2, QR + KR + 2 + R, QC + KCOL + 4 + R), f)
    wide[:, QR:QR + R, QC:QC + R] = n("rpb")
    toep = np.zeros((QR, QC, NH2, KR + 2, KCOL + 4), f)
    for r in range(QR):
        for c in range(QC):
            toep[r, c] = wide[:, QR + 2 - r:QR + 2 - r + KR + 2, QC - c:QC - c + KCOL + 4]
    o["toep"] = toep
    first = lambda at, length: np.clip(at - WIN // 2, 0, length - WIN)
    outside = np.full((128, 3, 2, KR, KCOL), -1e30, f)
    for kind, c in enumerate((0, 1, COLS - 1)):
        k0 = (0, QC - WIN // 2, NA - KCOL)[kind]
        for g in range(2):
            for r in range(QR):
                for j in range(QC):
                    a = first(QR * g + r, B) - (B - KR) * g
                    b = first(QC * c + j, NA) - k0
                    outside[r * QC + j, kind, g, a:a + WIN, b:b + WIN] = 0.0
    o["outside"] = outside
    m = lambda k: i["L1_ffn_" + k]
    o["router"], o["corr"] = halves(m("router_w").T, m("router_b")), rows(m("corr_bias"))
    o["earlier"] = rows(np.tril(np.ones((4, 4), f), -1).reshape(1, 16))
    o["later"] = rows(np.triu(np.ones((4, 4), f), 1).reshape(1, 16))
    gates = [(m("gWg")[e], m("gbg")[e], m("gWu")[e], m("gbu")[e], m("gWd")[e], m("gbd")[e]) for e in range(E)]
    for j in range(2):
        c = slice(I2 * j, I2 * j + I2)
        gates.append((m("sWg")[:, c], m("sbg")[c], m("sWu")[:, c], m("sbu")[c], m("sWd")[c],
                      m("sbd") if j == 0 else np.zeros(D, f)))
    gu = [np.concatenate([halves(x[0], x[1]), halves(x[2], x[3])], 2) for x in gates]
    o["gu"] = np.stack([np.concatenate([gu[2 * q], gu[2 * q + 1]], 2) for q in range(PAIRS)], 1)
    o["dn"] = np.stack([with_row(x[4], x[5]) for x in gates], 1)
    for name, (p, c) in [(name, x[:2]) for name, x in WEIGHTS.items()] + list(SPLIT.items()):
        o[name] = np.ascontiguousarray(o[name]).reshape(p, c)
    return {k: np.ascontiguousarray(v, f) for k, v in o.items()}


def kernel(**inputs):
    import concourse.bacc as _bacc
    from concourse.bass_utils import run_bass_kernel_spmd as _run

    arrays = laid_out({k: np.asarray(v) for k, v in inputs.items()})
    nc = _bacc.Bacc("TRN2", target_bir_lowering=False, num_devices=1)
    args = {k: nc.dram_tensor("in_" + k, v.shape, F32, kind="ExternalInput").ap() for k, v in arrays.items()}
    args["out"] = nc.dram_tensor("out_rows", (TOK, D), F32, kind="ExternalOutput").ap()
    build(nc, args)
    r = _run(nc, [{"in_" + k: v for k, v in arrays.items()}], core_ids=[0])
    return r.results[0]["out_rows"].reshape(B, NA, D)
```

```python
import concourse.bass as bass
from concourse import mybir
from contextlib import ExitStack
import numpy as np

F32 = mybir.dt.float32
F32R = mybir.dt.float32r
U32 = mybir.dt.uint32
I32 = mybir.dt.int32
ALU = mybir.AluOpType
ACT = mybir.ActivationFunctionType
AX = mybir.AxisListType
ds = bass.ds

B = 16
NI, NT = 64, 32
NA = NI + NT
D = 192
HALF = 96
FF = 768
KC = FF // 128
NH = 12
DH = D // NH
HB = NH // 4
TOK = B * NA
NTILE = TOK // 128
EARLY_TILES = 2 * NTILE // 3
E = 16
SORT_TILES = TOK // 128 + E - 1
EPS = 1e-5
WIN = 5
NH2, DH2 = 4, 24
HID = 96
QR, QC = 8, 16
KR, KCOL = 10, 20
NKEY = KR * KCOL
HKEY = NKEY // 2
COLS = NA // QC
PAIRS = E // 2 + 1
I2 = 96


def steady(eng, step, n, first, last, ring=2):
    assert first % ring == 0 and (last - first) % ring == 0 and first >= 2
    for s in range(first):
        step(s, s % ring)
    with eng.Fori(first // ring, last // ring) as i:
        for p in range(ring):
            step(ring * i + p, p)
    for s in range(last, n):
        step(s, s % ring)


def within(s, n):
    return 0 <= s < n if isinstance(s, int) else True


def wait(eng, sem, value):
    if not isinstance(value, int) or value > 0:
        eng.wait_ge(sem, value)


class Scope:

    def __init__(self, W, ctx, tag):
        self.nc, self.whole, self.ctx, self.tag = W["nc"], W["whole"], ctx, tag

    def sb(self, name, shape, dt=F32):
        return self.ctx.enter_context(self.nc.sbuf_tensor(f"{self.tag}_{name}", shape, dt))

    def sem(self, name):
        return self.whole.enter_context(self.nc.semaphore(f"{self.tag}_{name}"))


def norm_stats(nc, dve, mv, st, n, part=None):
    a, b = (part.start, part.stop) if part else (0, n)
    sv = st[:, 6 * a:6 * b].rearrange("p (n s) -> p n s", s=6)
    mean, var, dif = mv[:, a:b], mv[:, n + a:n + b], mv[:, 2 * n + a:2 * n + b]
    dve.drain()
    nc.vector.tensor_tensor(mean, sv[:, :, 1], sv[:, :, 4], ALU.add)
    nc.vector.tensor_tensor(dif, sv[:, :, 1], sv[:, :, 4], ALU.subtract)
    nc.vector.tensor_tensor(var, sv[:, :, 2], sv[:, :, 5], ALU.add)
    dve.drain()
    nc.vector.tensor_scalar(mean, mean, 0.5, None, ALU.mult)
    nc.vector.tensor_scalar(var, var, 1.0 / D, EPS, ALU.mult, ALU.add)
    nc.vector.tensor_tensor(dif, dif, dif, ALU.mult)
    dve.drain()
    return nc.vector.scalar_tensor_tensor(var, dif, 0.25, var, ALU.mult, ALU.add)


def row_parts(W):
    cuts = {"early_rows": slice(0, EARLY_TILES), "late_rows": slice(EARLY_TILES, NTILE)}
    return [(W[name], W["due"](name, 16), part) for name, part in cuts.items()]


def take_rows(nc, W, dve, parts, H, rows=None):
    for rows_in, rows_due, part in parts:
        dve.wait_ge(rows_in, rows_due)
        if rows is not None:
            cols = slice(D * part.start, D * part.stop)
            nc.vector.tensor_tensor(H[:, cols], H[:, cols], rows[:, cols], ALU.add)
            dve.drain()
        for t in range(part.start, part.stop):
            nc.vector.bn_stats(W["row_stats"][:, 6 * t:6 * t + 6], H[:, t * D:t * D + D])
        norm_stats(nc, dve, W["row_mv"], W["row_stats"], NTILE, part).then_inc(W["stat_done"], 1)


def rstd_rows(nc, W, pool, parts, norm_due):
    for i, (_, _, part) in enumerate(parts):
        pool.wait_ge(W["stat_done"], norm_due - 1 + i)
        nc.gpsimd.tensor_tensor(W["row_rs"][:, part], W["row_mv"][:, NTILE + part.start:NTILE + part.stop],
                                W["mhalf"][:, 0:1].broadcast_to([128, part.stop - part.start]),
                                ALU.pow).then_inc(W["rstd_ready"], 1)


def normalize_parts(W, dve, step, norm_due):
    dve.wait_ge(W["rstd_ready"], norm_due - 1)
    steady(dve, step, EARLY_TILES, 2, EARLY_TILES)
    dve.wait_ge(W["rstd_ready"], norm_due)
    with dve.Fori(EARLY_TILES // 2, NTILE // 2) as i:
        for p in range(2):
            step(2 * i + p, p)


def embed(nc, W, ps, args, x0T):
    with ExitStack() as ctx:
        S = Scope(W, ctx, "em")
        n = B * NI // 128
        xt = [S.sb(f"xt{p}", [128, KC * 128]) for p in range(2)]
        t1 = [S.sb(f"t1{p}", [128, D]) for p in range(2)]
        x0 = [S.sb(f"x0{p}", [128, D]) for p in range(2)]
        st = S.sb("st", [128, 6])
        mv = [S.sb(f"mv{p}", [128, 2]) for p in range(2)]
        rs = [S.sb(f"rs{p}", [128, 1]) for p in range(2)]
        whole = {m: S.sb(m, list(w)) for m, w in SPLIT_FF.items()}
        loaded = [S.sem(f"loaded{p}") for p in range(2)]
        patched, var_ready, rstd_ready, x0_ready, turned, x0T_ready, ff_loaded, ff_high = map(
            S.sem, ["patched", "var_ready", "rstd_ready", "x0_ready", "turned", "x0T_ready", "ff_loaded", "ff_high"])
        block = ctx.enter_context(nc.Block())

        @block.sync
        def _(sp):
            def step(s, p):
                wait(sp, patched, s - 1)
                sp.dma_start(xt[p][:, :], args["x"][:, ds(s * KC * 128, KC * 128)]).then_inc(loaded[p], 16)
                if isinstance(s, int) and s == 1:
                    for m in SPLIT_FF:
                        sp.dma_start(whole[m][:, :], args[m]).then_inc(ff_loaded, 16)
            steady(sp, step, n, 2, n)
            load(nc, W, args, ("ff", "a", "b"), sp)
            sp.dma_start(W["h96"][NI:NA, :].rearrange("j (b d) -> j b d", b=B), args["txt"]).then_inc(
                W["sem"]["b"], 16)
            load(nc, W, args, ("moe1",), sp)

        @block.tensor
        def _(pe):
            pe.wait_ge(W["sem"]["embed"], W["count"]["embed"])

            def step(s, p):
                if within(s, n):
                    pe.wait_ge(loaded[p], 8 * (s - p) + 16)
                    wait(pe, var_ready, s - 1)
                    for k in range(KC):
                        mm = nc.tensor.matmul(ps[:, p, 0:D], xt[p][:, 128 * k:128 * k + 128],
                                              W["pw"][:, k * D:k * D + D], start=k == 0, stop=k == KC - 1)
                    mm.then_inc(patched, 1)
                if within(s - 2, n):
                    pe.wait_ge(x0_ready, s - 1)
                    wait(pe, x0T_ready, s - 3)
                    for k in range(2):
                        mm = nc.tensor.transpose(ps[0:HALF, 2 + p, 128 * k:128 * k + 128],
                                                 x0[p][:, HALF * k:HALF * k + HALF], W["ident"][:, :])
                    mm.then_inc(turned, 1)
            steady(pe, step, n + 2, 4, n)

        @block.gpsimd
        def _(pool):
            def step(s, p):
                pool.wait_ge(var_ready, s + 1)
                nc.gpsimd.tensor_tensor(rs[p][:, :], mv[p][:, 1:2], W["mhalf"][:, 0:1], ALU.pow).then_inc(rstd_ready, 1)
                if not isinstance(s, int) or s >= 2:
                    for m, (_, c) in SPLIT_FF.items():
                        part = ds((s - 2) * (c // (n - 2)), c // (n - 2))
                        nc.gpsimd.tensor_tensor(W[m + "_low"][:, part], whole[m][:, part],
                                                W[m + "_high"][:, part].bitcast(F32), ALU.subtract)
                elif s == 1:
                    pool.wait_ge(ff_high, len(SPLIT_FF))
            steady(pool, step, n, 2, n)

        @block.vector
        def _(dve):
            def step(s, p):
                if within(s, n):
                    dve.wait_ge(patched, s + 1)
                    nc.vector.tensor_tensor(t1[p][:, :], ps[:, p, 0:D], W["pb"][:, :], ALU.add)
                    dve.drain()
                    nc.vector.bn_stats(st[:, :], t1[p][:, :])
                if within(s - 1, n):
                    q = 1 - p
                    dve.wait_ge(rstd_ready, s)
                    wait(dve, turned, s - 2)
                    nc.vector.tensor_scalar(x0[q][:, :], t1[q][:, :], mv[q][:, 0:1], rs[q][:, :], ALU.subtract,
                                            ALU.mult)
                dve.drain()
                if within(s, n):
                    nc.vector.bn_aggr(mv[p][:, :], st[:, :])
                if within(s - 1, n):
                    nc.vector.tensor_tensor(x0[q][:, :], x0[q][:, :], W["lng"][:, :], ALU.mult)
                dve.drain()
                if within(s, n):
                    nc.vector.tensor_scalar(mv[p][:, 1:2], mv[p][:, 1:2], EPS, None, ALU.add).then_inc(var_ready, 1)
                if within(s - 1, n):
                    nc.vector.tensor_tensor(x0[q][:, :], x0[q][:, :], W["lnbpe"][:, :], ALU.add).then_inc(x0_ready, 1)
            dve.wait_ge(W["sem"]["embed"], W["count"]["embed"])
            nc.vector.tensor_tensor(W["lnbpe"][:, :], W["lnb"][:, :], W["pe"][:, :], ALU.add)
            dve.drain()
            steady(dve, step, n + 1, 4, n)

        @block.scalar
        def _(act):
            def step(s, p):
                act.wait_ge(turned, s + 1)
                for k in range(2):
                    cp = nc.scalar.copy(x0T[:, ds(k * B * NI + 128 * s, 128)],
                                        ps[0:HALF, 2 + p, 128 * k:128 * k + 128])
                cp.then_inc(x0T_ready, 1)
            act.wait_ge(ff_loaded, 16 * len(SPLIT_FF))
            for m in SPLIT_FF:
                nc.scalar.copy(W[m + "_high"][:, :], whole[m][:, :]).then_inc(ff_high, 1)
            steady(act, step, n, 2, n)


def feed_forward(nc, W, ps, nth, xin, out, res, h96=None):
    with ExitStack() as ctx:
        S = Scope(W, ctx, f"f{nth}")
        N = B * NI // 2
        T = B * NI
        RING = 3
        x_high, x_low = ([S.sb(f"{m}{c}", [HALF, 2 * N], F32R) for c in range(2)] for m in ("x_high", "x_low"))
        g = [S.sb(f"g{r}", [128, N]) for r in range(RING)]
        g_high, g_low = ([S.sb(f"{m}{c}", [128, KC * N], F32R) for c in range(2)] for m in ("g_high", "g_low"))
        sems = W["ff_sems"]
        base = {m: nth * per for m, per in FF_COUNTS.items()}
        block = ctx.enter_context(nc.Block())

        def due(eng, m, value):
            if value > 0:
                eng.wait_ge(sems[m], base[m] + value)

        @block.tensor
        def _(pe):
            pe.wait_ge(W["sem"]["ff"], W["count"]["ff"])

            def up(c):
                due(pe, "x_split", c + 1)
                for f in range(KC):
                    i = c * KC + f
                    due(pe, "gelu_done", i - 3)
                    for k in range(2):
                        col = k * FF + 128 * f
                        for w, x in (("high", x_high), ("low", x_high), ("high", x_low)):
                            mm = nc.tensor.matmul(ps[:, i % 4, :], W["ff1_" + w][:, col:col + 128],
                                                  x[c][:, k * N:k * N + N],
                                                  start=k == 0 and w == "high" and x is x_high,
                                                  stop=k == 1 and x is x_low)
                    mm.then_inc(sems["hidden"], 1)

            def down(c):
                due(pe, "g_split", KC * (c + 1))
                for m in range(2):
                    for f in range(KC):
                        col = f * D + HALF * m
                        for w, x in (("high", g_high), ("low", g_high), ("high", g_low)):
                            mm = nc.tensor.matmul(ps[0:HALF, 4 + 2 * c + m, :], W["ff2_" + w][:, col:col + HALF],
                                                  x[c][:, f * N:f * N + N],
                                                  start=f == 0 and w == "high" and x is g_high,
                                                  stop=f == KC - 1 and x is g_low)
                    mm.then_inc(sems["summed"], 1)
            up(0)
            up(1)
            down(0)
            down(1)
            if h96 is not None:
                for b in range(0, B, 2):
                    i = b // 2
                    due(pe, "out_ready", 2 if b < B // 2 else 4)
                    wait(pe, W["h_ready"], i - 3)
                    for j in range(2):
                        for k in range(2):
                            mm = nc.tensor.transpose(ps[0:NI, i % 4, D * j + HALF * k:D * j + HALF * k + HALF],
                                                     out[0:HALF, k * T + NI * (b + j):k * T + NI * (b + j) + NI],
                                                     W["ident"][0:HALF, 0:HALF])
                    mm.then_inc(W["h_turned"], 1)

        def x_chunk(c):
            return xin[0:HALF, :].rearrange("f (k t) -> f k t", k=2)[:, :, c * N:c * N + N]

        def by_halves(x):
            return x.rearrange("f (k t) -> f k t", k=2)

        @block.scalar
        def _(act):
            for c in range(2):
                nc.scalar.copy(by_halves(x_high[c][:, :]), x_chunk(c)).then_inc(sems["x_high"], 1)
            for i in range(2 * KC):
                c, f = i // KC, i % KC
                due(act, "hidden", i + 1)
                due(act, "g_split", i + 1 - RING)
                nc.scalar.activation(g[i % RING][:, :], ps[:, i % 4, :], ACT.Gelu_apprx_tanh,
                                     bias=W["ff1b"][:, f:f + 1]).then_inc(sems["gelu_done"], 1)
                due(act, "gelu_done", i + 1)
                nc.scalar.copy(g_high[c][:, f * N:f * N + N], g[i % RING][:, :]).then_inc(sems["g_high"], 1)
            if h96 is not None:
                for i in range(B // 2):
                    act.wait_ge(W["h_turned"], i + 1)
                    nc.scalar.copy(h96[0:NI, 2 * D * i:2 * D * i + 2 * D],
                                   ps[0:NI, i % 4, 0:2 * D]).then_inc(W["h_ready"], 1)

        @block.vector
        def _(dve):
            for c in range(2):
                due(dve, "x_high", c + 1)
                nc.vector.tensor_tensor(by_halves(x_low[c][:, :]), x_chunk(c), by_halves(x_high[c][:, :].bitcast(F32)),
                                        ALU.subtract).then_inc(sems["x_split"], 1)
            for i in range(2 * KC):
                c, f = i // KC, i % KC
                due(dve, "g_high", i + 1)
                nc.vector.tensor_tensor(g_low[c][:, f * N:f * N + N], g[i % RING][:, :],
                                        g_high[c][:, f * N:f * N + N].bitcast(F32),
                                        ALU.subtract).then_inc(sems["g_split"], 1)
            for c in range(2):
                for m in range(2):
                    due(dve, "summed", 2 * c + m + 1)
                    src = ps[0:HALF, 4 + 2 * c + m, :]
                    at = slice(m * T + c * N, m * T + c * N + N)
                    if res is None:
                        nc.vector.tensor_scalar(out[0:HALF, at], src, W["ff2b"][:, m:m + 1], None,
                                                ALU.add).then_inc(sems["out_ready"], 1)
                    else:
                        nc.vector.scalar_tensor_tensor(out[0:HALF, at], src, W["ff2b"][:, m:m + 1],
                                                       res[0:HALF, at], ALU.add, ALU.add).then_inc(sems["out_ready"], 1)
            if h96 is not None:
                dve.wait_ge(W["sem"]["b"], W["count"]["b"])
                for i in range(B // 2):
                    dve.wait_ge(W["h_ready"], i + 1)
                    for b in (2 * i, 2 * i + 1):
                        nc.vector.bn_stats(W["h_stats"][:, 6 * b:6 * b + 6], h96[:, b * D:b * D + D])


def attention(nc, W, ps, tag, T, w, yT, x0T, x1T, h96, h_dram):
    full = h96 is not None
    n = B if full else B * NI // T
    TI = B * NI
    with ExitStack() as ctx:
        S = Scope(W, ctx, tag)
        xb = [S.sb(f"xb{p}", [HALF + 1, 2 * T]) for p in range(2)]
        qs = [S.sb(f"qs{p}", [128, 2 * T]) for p in range(2)]
        ks = S.sb("ks", [HALF, 2 * T])
        kd = [S.sb(f"kd{p}", [128, NH * T]) for p in range(2)]
        v = [S.sb(f"v{p}", [T, NH * (DH + 1)]) for p in range(2)]
        p_ = [S.sb(f"p{p}", [T, NH * T]) for p in range(2)]
        pT = S.sb("pT", [T, NH * T])
        nmax = S.sb("nmax", [T, NH])
        rec = S.sb("rec", [T, NH])
        on = S.sb("on", [T, D])
        oT = S.sb("oT", [HALF + 1, 2 * T])
        (xb_ready, q_done, keys_done, qkv_done, q_ready, k_ready, kd_ready, v_ready, scored, masked, shifted,
         exp_done, p_turned, pT_ready, weighed, on_ready, o_turned, oT_ready, projected, added) = map(S.sem, [
             "xb_ready", "q_done", "keys_done", "qkv_done", "q_ready", "k_ready", "kd_ready", "v_ready", "scored",
             "masked", "shifted", "exp_done", "p_turned", "pT_ready", "weighed", "on_ready", "o_turned", "oT_ready", "projected",
             "added"])
        if full:
            xn_ready, x_turned, stored = map(
                S.sem, ["xn_ready", "x_turned", "stored"])
            dm = S.sb("dm", [T, NH * T])
            ntemp = S.sb("ntemp", [T, NH])
            xn = [S.sb(f"xn{p}", [T, D]) for p in range(2)]
            mv = S.sb("mv", [T, 3 * B])
            rs = S.sb("rs", [T, B])
        scores = ps[0:T, 0:4, 0:HB * T]
        bq, bk, bo, bt = 4, 5, 6, 7
        RC = 2 * T
        XC = 2 * NA
        VC = 2 * T
        ones_set, ones_due = W["ones_set"], W["due"]("ones_set", 7)
        stat_done, rstd_ready, norm_due = W["stat_done"], W["rstd_ready"], W["due"]("norm", int(full))

        block = ctx.enter_context(nc.Block())

        if full:
            @block.sync
            def _(sp):
                def step(s, p):
                    sp.wait_ge(added, s + 1)
                    sp.dma_start(h_dram[ds(s * NA, NA), :], h96[:, ds(s * D, D)]).then_inc(stored, 16)
                steady(sp, step, B, 2, B)
                sp.wait_ge(stored, 16 * B)

        @block.gpsimd
        def _(pool):
            def clear(p):
                nc.gpsimd.memset(kd[p][:, :], 0.0)
                pool.drain()
            if full:
                for p in range(2):
                    clear(p)
                pool.wait_ge(stat_done, norm_due)
                nc.gpsimd.tensor_tensor(rs[:, :], mv[:, B:2 * B], W["mhalf"][0:T, 0:1].broadcast_to([T, B]),
                                        ALU.pow).then_inc(rstd_ready, 1)

            def window(b, p):
                wait(pool, qkv_done, b - 1)
                for k in range(2):
                    cp = nc.gpsimd.tensor_copy(xb[p][0:HALF, T * k:T * k + T], yT[:, ds(k * TI + b * T, T)])
                cp.then_inc(xb_ready, 1)

            def spread_k(b, p):
                pool.wait_ge(k_ready, b + 1)
                nc.gpsimd.tensor_tensor(
                    kd[p][0:HALF, :].rearrange("r (g m n) -> r g m n", g=2, m=NH // 2),
                    ks[:, :].rearrange("r (g n) -> r g n", g=2)[:, :, None, :].broadcast_to([HALF, 2, NH // 2, T]),
                    W["own"][:, None, :, None].broadcast_to([HALF, 2, NH // 2, T]), ALU.mult).then_inc(kd_ready, 1)

            def step(s, p):
                for stage, lag in ((window, 0), (spread_k, 1)):
                    if within(s - lag, n) and (not full or stage is not window):
                        stage(s - lag, (p + lag) % 2)
                        if stage is window and isinstance(s, int) and s < 2:
                            clear(s)
            steady(pool, step, n + 1, 4, n)

        @block.tensor
        def _(pe):
            pe.wait_ge(ones_set, ones_due)
            pe.wait_ge(W["sem"][w], W["count"][w])

            def turn_x(b, p):
                wait(pe, k_ready, b)
                pe.wait_ge(xn_ready, b + 1)
                for k in range(2):
                    mm = nc.tensor.transpose(ps[0:HALF, bk, XC + T * k:XC + T * k + T],
                                             xn[p][:, HALF * k:HALF * k + HALF], W["ident"][0:T, 0:T])
                mm.then_inc(x_turned, 1)

            def heads(p, at, bank):
                for g in range(2):
                    for k in range(2):
                        mm = nc.tensor.matmul(ps[0:HALF, bank, T * g:T * g + T],
                                              W["qk"][w][0:HALF + k, 2 * D * k + at + HALF * g:2 * D * k + at + HALF * (g + 1)],
                                              xb[p][0:HALF + k, T * k:T * k + T], start=k == 0, stop=k == 1)
                return mm

            def keys(b, p):
                pe.wait_ge(xb_ready, b + 1)
                heads(p, D, bk).then_inc(keys_done, 1)

            def queries(b, p):
                wait(pe, v_ready, b)
                heads(p, 0, bq).then_inc(q_done, 1)

            def values(b, p):
                pe.wait_ge(q_ready, b + 1)
                for k in range(2):
                    mm = nc.tensor.matmul(ps[0:T, bq, VC:VC + D], xb[p][0:HALF + k, T * k:T * k + T],
                                          W["v"][w][0:HALF + k, k * D:k * D + D], start=k == 0, stop=k == 1)
                mm.then_inc(qkv_done, 1)

            def score(b, p):
                pe.wait_ge(q_ready, b + 1)
                pe.wait_ge(kd_ready, b + 1)
                wait(pe, masked, b)
                for j in range(4):
                    g = j // 2
                    mm = nc.tensor.matmul(ps[0:T, j, 0:HB * T], qs[p][:, T * g:T * g + T],
                                          kd[p][:, HB * T * j:HB * T * (j + 1)], start=True, stop=True)
                mm.then_inc(scored, 1)

            def turn_p(b, p):
                pe.wait_ge(exp_done, b + 1)
                pe.wait_ge(masked, min(b + 2, n) if isinstance(b, int) else b + 2)
                for c in range(4):
                    for j in range(HB):
                        mm = nc.tensor.transpose(ps[0:T, c, T * j:T * j + T],
                                                 p_[p][:, T * (HB * c + j):T * (HB * c + j) + T],
                                                 W["ident"][0:T, 0:T])
                    mm.then_inc(p_turned, 1)

            def weigh(b, p, heads):
                for h in heads:
                    mm = nc.tensor.matmul(ps[0:T, bo, (DH + 1) * h:(DH + 1) * (h + 1)], pT[:, T * h:T * h + T],
                                          v[p][:, (DH + 1) * h:(DH + 1) * (h + 1)], start=True, stop=True)
                return mm

            def weigh_first(b, p):
                pe.wait_ge(pT_ready, 2 * b + 2)
                pe.wait_ge(v_ready, b + 1)
                weigh(b, p, range(0, 4))

            def weigh_second(b, p):
                weigh(b, p, range(4, 8))

            def weigh_third(b, p):
                weigh(b, p, range(8, NH)).then_inc(weighed, 1)

            def turn_o(b, p):
                pe.wait_ge(on_ready, b + 1)
                wait(pe, added, b)
                for k in range(2):
                    mm = nc.tensor.transpose(ps[0:HALF, bt, T * k:T * k + T], on[:, HALF * k:HALF * k + HALF],
                                             W["ident"][0:T, 0:T])
                mm.then_inc(o_turned, 1)

            def project(b, p):
                pe.wait_ge(oT_ready, b + 1)
                if full:
                    for k in range(2):
                        mm = nc.tensor.matmul(ps[0:T, bt, RC:RC + D], oT[0:HALF + k, T * k:T * k + T],
                                              W["proj"][w][0:HALF + k, k * D:k * D + D], start=k == 0, stop=k == 1)
                else:
                    for m in range(2):
                        for k in range(2):
                            mm = nc.tensor.matmul(ps[0:HALF, bt, RC + T * m:RC + T * m + T],
                                                  W["proj"][w][0:HALF + k, k * D + HALF * m:k * D + HALF * m + HALF],
                                                  oT[0:HALF + k, T * k:T * k + T], start=k == 0, stop=k == 1)
                mm.then_inc(projected, 1)

            def step(s, p):
                for stage, lag in ((score, 2), (weigh_third, 4), (keys, 1), (queries, 1), (turn_o, 4), (turn_p, 3),
                                   (values, 1), (project, 4), (weigh_first, 3), (turn_x, 0), (weigh_second, 3)):
                    if within(s - lag, n) and (full or stage is not turn_x):
                        stage(s - lag, (p + lag) % 2)
            steady(pe, step, n + 4, 6, n)

        @block.scalar
        def _(act):
            act.wait_ge(ones_set, ones_due)

            def copy_q(b, p):
                act.wait_ge(q_done, b + 1)
                nc.scalar.copy(qs[p][0:HALF, :], ps[0:HALF, bq, 0:2 * T]).then_inc(q_ready, 1)

            def copy_pT(b, p):
                act.wait_ge(p_turned, 4 * b + 3)
                nc.scalar.copy(pT[:, 0:3 * HB * T].rearrange("t (c n) -> t c n", c=3),
                               ps[0:T, 0:3, 0:HB * T]).then_inc(pT_ready, 1)

            def copy_k(b, p):
                act.wait_ge(keys_done, b + 1)
                nc.scalar.copy(ks[:, :], ps[0:HALF, bk, 0:2 * T]).then_inc(k_ready, 1)

            def copy_v(b, p):
                act.wait_ge(qkv_done, b + 1)
                wait(act, weighed, b - 1)
                nc.scalar.copy(v[p][:, :].rearrange("t (h d) -> t h d", h=NH)[:, :, 0:DH],
                               ps[0:T, bq, VC:VC + D].rearrange("t (h d) -> t h d", h=NH)).then_inc(v_ready, 1)

            def exp(b, p):
                act.wait_ge(shifted, b + 1)
                nc.scalar.activation(p_[p][:, :], p_[p][:, :], ACT.Exp, scale=DH ** -0.5).then_inc(exp_done, 1)

            def copy_x(b, p):
                act.wait_ge(x_turned, b + 1)
                nc.scalar.copy(xb[p][0:HALF, :], ps[0:HALF, bk, XC:XC + 2 * T]).then_inc(xb_ready, 1)

            def copy_o(b, p):
                act.wait_ge(o_turned, b + 1)
                nc.scalar.copy(oT[0:HALF, :], ps[0:HALF, bt, 0:2 * T]).then_inc(oT_ready, 1)

            def step(s, p):
                for stage, lag in ((copy_v, 2), (copy_k, 1), (copy_q, 1), (copy_o, 4), (copy_pT, 3), (copy_x, 0),
                                   (exp, 2)):
                    if within(s - lag, n) and (full or stage is not copy_x):
                        stage(s - lag, (p + lag) % 2)
            steady(act, step, n + 4, 6, n)

        @block.vector
        def _(dve):
            dve.wait_ge(W["sem"][w], W["count"][w])
            if full:
                norm_stats(nc, dve, mv, W["h_stats"], B).then_inc(stat_done, 1)
            for p in range(2):
                nc.vector.memset(xb[p][HALF:HALF + 1, :], 1.0).then_inc(ones_set, 1)
                nc.vector.memset(v[p][:, :], 1.0).then_inc(ones_set, 1)
                nc.vector.memset(qs[p][HALF:128, :], 0.0).then_inc(ones_set, 1)
            nc.vector.memset(oT[HALF:HALF + 1, :], 1.0).then_inc(ones_set, 1)
            if full:
                nc.vector.tensor_scalar(ntemp[:, :], W["temp"][:, :], -1.0, None, ALU.mult)
                dve.drain()
                for j in range(NH):
                    nc.vector.tensor_scalar(dm[:, T * j:T * j + T], W["ident"][0:T, 0:T], ntemp[:, j:j + 1], 1.0,
                                            ALU.mult, ALU.add)
                dve.wait_ge(rstd_ready, norm_due)

            def norm(b, p):
                wait(dve, x_turned, b - 1)
                nc.vector.tensor_scalar(xn[p][:, :], h96[:, ds(b * D, D)], mv[:, ds(b, 1)], rs[:, ds(b, 1)],
                                        ALU.subtract, ALU.mult).then_inc(xn_ready, 1)

            def mask(b, p):
                dve.wait_ge(scored, b + 1)
                if full:
                    nc.vector.tensor_tensor(p_[p][:, :].rearrange("t (c n) -> t c n", c=4), scores,
                                            dm[:, :].rearrange("t (c n) -> t c n", c=4), ALU.mult).then_inc(masked, 1)
                else:
                    nc.vector.tensor_tensor(p_[p][:, :].rearrange("t (c r n) -> t c r n", r=HB, c=4),
                                            scores.rearrange("t c (r n) -> t c r n", r=HB),
                                            W["apart"][:, None, None, :].broadcast_to([T, 4, HB, T]),
                                            ALU.add).then_inc(masked, 1)

            def biggest(b, p):
                dve.drain()
                nc.vector.tensor_reduce(nmax[:, :], p_[p][:, :].rearrange("t (h n) -> t h n", h=NH), AX.X, ALU.max,
                                        negate=True)

            def copy_pT(b, p):
                dve.wait_ge(p_turned, 4 * b + 4)
                nc.vector.tensor_copy(pT[:, 3 * HB * T:NH * T], ps[0:T, 3, 0:HB * T]).then_inc(pT_ready, 1)

            def shift(b, p):
                ph = p_[p][:, :].rearrange("t (h n) -> t h n", h=NH)
                dve.drain()
                nc.vector.tensor_tensor(ph, ph, nmax[:, :, None].broadcast_to([T, NH, T]),
                                        ALU.add).then_inc(shifted, 1)

            def normalize(b, p):
                dve.wait_ge(weighed, b + 1)
                o = ps[0:T, bo, 0:NH * (DH + 1)].rearrange("t (h d) -> t h d", h=NH)
                nc.vector.reciprocal(rec[:, :], o[:, :, DH])
                dve.drain()
                nc.vector.tensor_tensor(on[:, :].rearrange("t (h d) -> t h d", h=NH), o[:, :, 0:DH],
                                        rec[:, :, None].broadcast_to([T, NH, DH]), ALU.mult).then_inc(on_ready, 1)

            def add(b, p):
                dve.wait_ge(projected, b + 1)
                if full:
                    nc.vector.tensor_tensor(h96[:, ds(b * D, D)], h96[:, ds(b * D, D)], ps[0:T, bt, RC:RC + D],
                                            ALU.add).then_inc(added, 1)
                else:
                    out = x1T[:, :].rearrange("f (k t) -> f k t", k=2)[:, :, ds(b * T, T)]
                    res = x0T[:, :].rearrange("f (k t) -> f k t", k=2)[:, :, ds(b * T, T)]
                    nc.vector.tensor_tensor(out, ps[0:HALF, bt, RC:RC + 2 * T].rearrange("f (k t) -> f k t", k=2),
                                            res, ALU.add).then_inc(added, 1)

            def step(s, p):
                for stage, lag in ((mask, 2), (normalize, 4), (biggest, 2), (copy_pT, 3), (norm, 0), (shift, 2),
                                   (add, 4)):
                    if within(s - lag, n) and (full or stage is not norm):
                        stage(s - lag, (p + lag) % 2)
            steady(dve, step, n + 4, 6, n)


def prefix_sum(nc, dve, bufs, lead, n, width):
    a, b, d = bufs[0], bufs[1], 1
    P = a.shape[0]
    while d < n:
        o = lead * width
        nc.vector.tensor_tensor(b[:, o:o + n * width], a[:, o:o + n * width],
                                a[:, o - d * width:o + (n - d) * width], ALU.add)
        dve.drain()
        a, b, d = b, a, 2 * d
    return a


def choose(nc, dve, top, at, values, n):
    for t in range(n):
        nc.vector.max(top[:, 8 * t:8 * t + 8], values[:, E * t:E * t + E])
    dve.drain()
    for t in range(n):
        nc.vector.max_index(at[:, 8 * t:8 * t + 8], top[:, 8 * t:8 * t + 8], values[:, E * t:E * t + E])
    dve.drain()


def route(nc, W, ps, H, h_dram, sorted_dram, xn_all, slot, owner):
    with ExitStack() as ctx:
        S = Scope(W, ctx, "rt")
        n = NTILE
        mv, rs = W["row_mv"], W["row_rs"]
        xn = [S.sb(f"xn{p}", [128, D]) for p in range(2)]
        xT = [S.sb(f"xT{p}", [HALF + 1, 256]) for p in range(2)]
        logits = S.sb("logits", [128, n * E])
        top, at = S.sb("top", [128, 8 * n]), S.sb("at", [128, 8 * n], U32)
        first = S.sb("first", [128, n])
        oh = S.sb("oh", [128, n * E])
        LEAD = 8
        cum = [S.sb(f"cum{i}", [128, (LEAD + n) * E]) for i in range(2)]
        cnt = [S.sb(f"cnt{i}", [128, LEAD + E]) for i in range(2)]
        over = S.sb("over", [128, E * n])
        tiles, base = S.sb("tiles", [128, E]), S.sb("base", [128, E])
        rank = S.sb("rank", [128, n * E])
        posf = S.sb("posf", [128, n])
        before = S.sb("before", [1, SORT_TILES * E])
        ownf = S.sb("ownf", [1, SORT_TILES])
        (xn_ready, kept, turned, xT_ready, gated, oh_ready, counted,
         slot_ready, scattered, zeroed) = map(S.sem, [
             "xn_ready", "kept", "turned", "xT_ready", "gated",
             "oh_ready", "counted", "slot_ready", "scattered", "zeroed"])
        ones_set, ones_due = W["ones_set"], W["due"]("ones_set", 2)
        norm_due = W["due"]("norm", 2)
        parts = row_parts(W)
        block = ctx.enter_context(nc.Block())

        @block.sync
        def _(sp):
            for rows_in, _, part in parts:
                sp.dma_start(H[:, :].rearrange("p (t d) -> p t d", t=n)[:, part, :],
                             h_dram.rearrange("(t p) d -> p t d", p=128)[:, part, :]).then_inc(rows_in, 16)
            sp.dma_start(sorted_dram.rearrange("(t p) d -> p t d", p=128),
                         W["zero"][:, None, :].broadcast_to([128, SORT_TILES, D])).then_inc(zeroed, 16)

        @block.gpsimd
        def _(pool):
            rstd_rows(nc, W, pool, parts, norm_due)

            def step(s, p):
                pool.wait_ge(xn_ready, s + 1)
                nc.gpsimd.tensor_copy(xn_all[:, ds(s * D, D)], xn[p][:, :]).then_inc(kept, 1)
            steady(pool, step, n, 2, n)
            pool.wait_ge(slot_ready, 1)
            pool.wait_ge(zeroed, 16)
            pool.wait_ge(kept, n)
            for t in range(n):
                nc.gpsimd.indirect_dma_start(
                    out=sorted_dram, out_offset=bass.IndirectOffsetOnAxis(ap=slot[:, t:t + 1], axis=0),
                    in_=xn_all[:, t * D:t * D + D], in_offset=None).then_inc(scattered, 16)
            pool.wait_ge(scattered, 16 * n)

        @block.tensor
        def _(pe):
            pe.wait_ge(ones_set, ones_due)
            pe.wait_ge(W["sem"]["moe1"], W["count"]["moe1"])

            def step(s, p):
                if within(s, n):
                    pe.wait_ge(xn_ready, s + 1)
                    wait(pe, xT_ready, s - 1)
                    for k in range(2):
                        mm = nc.tensor.transpose(ps[0:HALF, p, 128 * k:128 * k + 128],
                                                 xn[p][:, HALF * k:HALF * k + HALF], W["ident"][:, :])
                    mm.then_inc(turned, 1)
                if within(s - 1, n):
                    wait(pe, xT_ready, s)
                    for k in range(2):
                        mm = nc.tensor.matmul(ps[:, 2, ds(E * (s - 1), E)], xT[1 - p][0:HALF + k, 128 * k:128 * k + 128],
                                              W["gate"][0:HALF + k, E * k:E * k + E], start=k == 0, stop=k == 1)
                    mm.then_inc(gated, 1)
            steady(pe, step, n + 1, 2, n)
            pe.wait_ge(oh_ready, 1)
            nc.tensor.matmul(ps[:, 3, 0:n * E], W["below"][:, :], oh[:, :], start=True, stop=True)
            nc.tensor.matmul(ps[:, 4, 0:n * E], W["ones"][:, :], oh[:, :], start=True, stop=True).then_inc(counted, 1)

        @block.scalar
        def _(act):
            def step(s, p):
                act.wait_ge(turned, s + 1)
                wait(act, gated, s - 1)
                nc.scalar.copy(xT[p][0:HALF, :], ps[0:HALF, p, 0:256]).then_inc(xT_ready, 1)
            act.wait_ge(ones_set, ones_due)
            steady(act, step, n, 2, n)

        @block.vector
        def _(dve):
            for p in range(2):
                nc.vector.memset(xT[p][HALF:HALF + 1, :], 1.0).then_inc(ones_set, 1)
            for c in cum + cnt:
                nc.vector.memset(c[:, :], 0.0)
            take_rows(nc, W, dve, parts, H)

            def step(s, p):
                wait(dve, turned, s - 1)
                wait(dve, kept, s - 1)
                nc.vector.tensor_scalar(xn[p][:, :], H[:, ds(s * D, D)], mv[:, ds(s, 1)], rs[:, ds(s, 1)],
                                        ALU.subtract, ALU.mult).then_inc(xn_ready, 1)
            normalize_parts(W, dve, step, norm_due)
            dve.wait_ge(gated, n)
            nc.vector.tensor_copy(logits[:, :], ps[:, 2, 0:n * E])
            dve.drain()
            choose(nc, dve, top, at, logits, n)
            nc.vector.tensor_copy(first[:, :], at[:, 0:8 * n:8])
            dve.drain()
            nc.vector.tensor_tensor(oh[:, :].rearrange("p (t e) -> p t e", t=n),
                                    W["iota"][:, None, 0:E].broadcast_to([128, n, E]),
                                    first[:, :, None].broadcast_to([128, n, E]), ALU.is_equal).then_inc(oh_ready, 1)
            dve.wait_ge(counted, 1)
            nc.vector.tensor_copy(cum[0][:, LEAD * E:], ps[:, 4, 0:n * E])
            dve.drain()
            c = prefix_sum(nc, dve, cum, LEAD, n, E)
            total = c[:, (LEAD + n - 1) * E:(LEAD + n) * E]
            nc.vector.tensor_tensor(over[:, :].rearrange("p (e k) -> p e k", e=E),
                                    total[:, :, None].broadcast_to([128, E, n]),
                                    W["steps"][:, None, 0:n].broadcast_to([128, E, n]), ALU.is_gt)
            dve.drain()
            nc.vector.tensor_reduce(tiles[:, :], over[:, :].rearrange("p (e k) -> p e k", e=E), AX.X, ALU.add)
            dve.drain()
            nc.vector.tensor_copy(cnt[0][:, LEAD:], tiles[:, :])
            dve.drain()
            ends = prefix_sum(nc, dve, cnt, LEAD, E, 1)[:, LEAD:]
            nc.vector.tensor_tensor(base[:, :], ends, tiles[:, :], ALU.subtract)
            nc.vector.tensor_tensor(rank[:, :], ps[:, 3, 0:n * E], c[:, (LEAD - 1) * E:(LEAD + n - 1) * E], ALU.add)
            dve.drain()
            nc.vector.tensor_scalar(base[:, :], base[:, :], 128.0, None, ALU.mult)
            dve.drain()
            r3 = rank[:, :].rearrange("p (t e) -> p t e", t=n)
            nc.vector.tensor_tensor(r3, r3, base[:, None, :].broadcast_to([128, n, E]), ALU.add)
            dve.drain()
            nc.vector.tensor_tensor(rank[:, :], rank[:, :], oh[:, :], ALU.mult)
            dve.drain()
            nc.vector.tensor_reduce(posf[:, :], r3, AX.X, ALU.add)
            dve.drain()
            nc.vector.tensor_copy(slot[:, :], posf[:, :]).then_inc(slot_ready, 1)
            nc.vector.tensor_tensor(before[:, :].rearrange("p (j e) -> p j e", j=SORT_TILES),
                                    ends[0:1, None, :].broadcast_to([1, SORT_TILES, E]),
                                    W["iota"][0:1, 0:SORT_TILES, None].broadcast_to([1, SORT_TILES, E]), ALU.is_le)
            dve.drain()
            nc.vector.tensor_reduce(ownf[:, :], before[:, :].rearrange("p (j e) -> p j e", j=SORT_TILES), AX.X,
                                    ALU.add)
            dve.drain()
            nc.vector.tensor_scalar(owner[:, :], ownf[:, :], float(E - 1), float(2 * D), ALU.min, ALU.mult)


def experts_one(nc, W, ps, args, H, sorted_dram, done_dram, xn_all, slot, owner):
    with ExitStack() as ctx:
        S = Scope(W, ctx, "e1")
        n = SORT_TILES
        RING = 4
        xr = [S.sb(f"xr{r}", [128, D]) for r in range(RING)]
        xT = [S.sb(f"xT{p}", [HALF + 1, 256]) for p in range(2)]
        g = [S.sb(f"g{p}", [128, D]) for p in range(2)]
        gT = [S.sb(f"gT{p}", [HALF + 1, 256]) for p in range(2)]
        y = [S.sb(f"y{r}", [128, D]) for r in range(RING)]
        loaded = [S.sem(f"loaded{r}") for r in range(RING)]
        stored = [S.sem(f"stored{r}") for r in range(RING)]
        (x_turned, xT_ready, up_done, g_ready, g_turned, gT_ready, down_done, y_ready) = map(S.sem, [
             "x_turned", "xT_ready", "up_done", "g_ready", "g_turned", "gT_ready", "down_done", "y_ready"])
        parts = [(S.sem("early_gathered"), 16 * EARLY_TILES, slice(0, EARLY_TILES)),
                 (S.sem("late_gathered"), 16 * (NTILE - EARLY_TILES), slice(EARLY_TILES, NTILE))]
        ones_set, ones_due = W["ones_set"], W["due"]("ones_set", 4)
        norm_due = W["due"]("norm", 2)
        block = ctx.enter_context(nc.Block())
        WE = 2 * D
        LAG = 7
        FIRST, LAST = 2 * RING, n - n % RING

        def each_stored(eng):
            for r in range(RING):
                eng.wait_ge(stored[r], 16 * len(range(r, n, RING)))

        @block.sync
        def _(sp):
            def step(s, r):
                if within(s, n):
                    wait(sp, x_turned, s - RING + 1)
                    sp.dma_start(xr[r][:, :], sorted_dram[ds(128 * s, 128), :]).then_inc(loaded[r], 16)
                if within(s - LAG, n):
                    ry = (r - LAG) % RING
                    sp.wait_ge(y_ready, s - LAG + 1)
                    sp.dma_start(done_dram[ds(128 * (s - LAG), 128), :], y[ry][:, :]).then_inc(stored[ry], 16)
            steady(sp, step, n + LAG, FIRST, LAST, RING)
            load(nc, W, args, ("nat",), sp)
            each_stored(sp)

        @block.tensor
        def _(pe):
            pe.wait_ge(ones_set, ones_due)
            pe.wait_ge(W["sem"]["moe1"], W["count"]["moe1"])

            def expert(s):
                return pe.value_load(owner[0:1, ds(s, 1)], min_val=0, max_val=(E - 1) * WE)

            starts = {}
            w1, w2 = ([W[m][0:HALF + k, D * k:] for k in range(2)] for m in ("w1", "w2"))

            def step(s, r):
                p = r % 2
                if within(s - 1, n):
                    up_at = starts[r] = expert(s - 1)
                if within(s - 3, n):
                    down_at = starts[r - 2] if r >= 2 else expert(s - 3)
                if within(s, n):
                    pe.wait_ge(loaded[r], 16 // RING * (s - r) + 16)
                    for k in range(2):
                        mm = nc.tensor.transpose(ps[0:HALF, p, 128 * k:128 * k + 128],
                                                 xr[r][:, HALF * k:HALF * k + HALF], W["ident"][:, :])
                    mm.then_inc(x_turned, 1)
                if within(s - 1, n):
                    pe.wait_ge(xT_ready, s)
                    for k in range(2):
                        mm = nc.tensor.matmul(ps[:, 3 - p, 0:D], xT[1 - p][0:HALF + k, 128 * k:128 * k + 128],
                                              w1[k][:, ds(up_at, D)], start=k == 0, stop=k == 1)
                    mm.then_inc(up_done, 1)
                if within(s - 2, n):
                    pe.wait_ge(g_ready, s - 1)
                    for k in range(2):
                        mm = nc.tensor.transpose(ps[0:HALF, 4 + p, 128 * k:128 * k + 128],
                                                 g[p][:, HALF * k:HALF * k + HALF], W["ident"][:, :])
                    mm.then_inc(g_turned, 1)
                if within(s - 3, n):
                    pe.wait_ge(gT_ready, s - 2)
                    wait(pe, y_ready, s - 4)
                    for k in range(2):
                        mm = nc.tensor.matmul(ps[:, 7 - p, 0:D], gT[1 - p][0:HALF + k, 128 * k:128 * k + 128],
                                              w2[k][:, ds(down_at, D)], start=k == 0, stop=k == 1)
                    mm.then_inc(down_done, 1)
            steady(pe, step, n + 3, FIRST, LAST, RING)

        @block.scalar
        def _(act):
            act.wait_ge(ones_set, ones_due)

            def step(s, p):
                if within(s, n):
                    act.wait_ge(x_turned, s + 1)
                    nc.scalar.copy(xT[p][0:HALF, :], ps[0:HALF, p, 0:256]).then_inc(xT_ready, 1)
                if within(s - 1, n):
                    wait(act, up_done, s)
                    nc.scalar.activation(g[1 - p][:, :], ps[:, 3 - p, 0:D], ACT.Gelu).then_inc(g_ready, 1)
            steady(act, step, n + 1, 2, n - 1)

        @block.vector
        def _(dve):
            for x in xT + gT:
                nc.vector.memset(x[HALF:HALF + 1, :], 1.0).then_inc(ones_set, 1)
            dve.wait_ge(ones_set, ones_due)

            def step(s, r):
                p = r % 2
                if within(s - 2, n):
                    dve.wait_ge(g_turned, s - 1)
                    nc.vector.tensor_copy(gT[p][0:HALF, :], ps[0:HALF, 4 + p, 0:256]).then_inc(gT_ready, 1)
                if within(s - 3, n):
                    ry = (r - 3) % RING
                    dve.wait_ge(down_done, s - 2)
                    wait(dve, stored[ry], 16 // RING * (s - 3 - ry))
                    nc.vector.tensor_copy(y[ry][:, :], ps[:, 7 - p, 0:D]).then_inc(y_ready, 1)
            steady(dve, step, n + 3, FIRST, LAST, RING)
            take_rows(nc, W, dve, parts, H, xn_all)

        @block.gpsimd
        def _(pool):
            each_stored(pool)
            for rows_in, _, part in parts:
                for t in range(part.start, part.stop):
                    nc.gpsimd.indirect_dma_start(
                        out=xn_all[:, t * D:t * D + D], out_offset=None, in_=done_dram,
                        in_offset=bass.IndirectOffsetOnAxis(ap=slot[:, t:t + 1], axis=0)).then_inc(rows_in, 16)
            rstd_rows(nc, W, pool, parts, norm_due)


def squeeze(nc, W, ps, args, H, xsT, bias):
    with ExitStack() as ctx:
        S = Scope(W, ctx, "sq")
        n, N = NTILE, 512
        mv, rs = W["row_mv"], W["row_rs"]
        RING = 4
        xn = [S.sb(f"xn{r}", [128, D]) for r in range(RING)]
        turned_banks = (0, 1, 6, 7)
        xnT = S.sb("xnT", [HALF, 2 * TOK])
        chunks = TOK // N
        f1 = [S.sb(f"f1{c}", [HID, N]) for c in range(chunks)]
        ca = [S.sb(f"ca{c}", [64, N]) for c in range(chunks)]
        cb = [S.sb(f"cb{c}", [HID, N]) for c in range(chunks)]
        (xn_ready, summed, turned, xnT_ready, fc_done, fc_ready, a_done, a_ready,
         b_done, b_ready) = map(S.sem, [
             "xn_ready", "summed", "turned", "xnT_ready", "fc_done", "fc_ready",
             "a_done", "a_ready", "b_done", "b_ready"])
        block = ctx.enter_context(nc.Block())

        @block.sync
        def _(sp):
            load(nc, W, args, LATE, sp)

        @block.gpsimd
        def _(pool):

            def step(s, r):
                pool.wait_ge(xn_ready, s + 1)
                nc.gpsimd.tensor_tensor(H[:, ds(s * D, D)], H[:, ds(s * D, D)], xn[r][:, :],
                                        ALU.add).then_inc(summed, 1)
            steady(pool, step, n, RING, n, RING)
            pool.wait_ge(W["sem"]["rest"], W["count"]["rest"])
            fill_bias(nc, W, bias, (0, 1))

        @block.tensor
        def _(pe):

            def step(s, r):
                pe.wait_ge(xn_ready, s + 1)
                wait(pe, xnT_ready, s - RING + 1)
                for k in range(2):
                    mm = nc.tensor.transpose(ps[0:HALF, turned_banks[r], 128 * k:128 * k + 128],
                                             xn[r][:, HALF * k:HALF * k + HALF], W["ident"][:, :])
                mm.then_inc(turned, 1)
            steady(pe, step, n, RING, n, RING)
            pe.wait_ge(W["sem"]["nat"], W["count"]["nat"])
            for s in range(chunks + 2):
                if s < chunks:
                    pe.wait_ge(xnT_ready, N // 128 * (s + 1))
                    wait(pe, fc_ready, s - 1)
                    for k in range(2):
                        mm = nc.tensor.matmul(ps[0:HID, 2 + s % 2, :], W["fc1"][:, HID * k:HID * k + HID],
                                              xnT[:, k * TOK + s * N:k * TOK + s * N + N], start=k == 0, stop=k == 1)
                    mm.then_inc(fc_done, 1)
                if 0 <= s - 1 < chunks:
                    pe.wait_ge(fc_ready, s)
                    nc.tensor.matmul(ps[0:64, 4 + (s - 1) % 2, :], W["conva"][:, :], f1[s - 1][:, :],
                                     start=True, stop=True).then_inc(a_done, 1)
                if 0 <= s - 2 < chunks:
                    pe.wait_ge(a_ready, s - 1)
                    nc.tensor.matmul(ps[0:HID, 6 + (s - 2) % 2, :], W["convb"][:, :], ca[s - 2][:, :],
                                     start=True, stop=True).then_inc(b_done, 1)

        @block.scalar
        def _(act):
            def step(s, r):
                act.wait_ge(turned, s + 1)
                nc.scalar.copy(xnT[:, :].rearrange("f (k t) -> f k t", k=2)[:, :, ds(128 * s, 128)],
                               ps[0:HALF, turned_banks[r], 0:256].rearrange("f (k t) -> f k t", k=2)).then_inc(xnT_ready, 1)
            steady(act, step, n, RING, n, RING)
            for s in range(chunks):
                act.wait_ge(b_ready, s + 1)
                nc.scalar.activation(xsT[0:HID, s * N:s * N + N], cb[s][:, :], ACT.Gelu)

        @block.vector
        def _(dve):

            def step(s, r):
                wait(dve, turned, s - RING + 1)
                wait(dve, summed, s - RING + 1)
                nc.vector.tensor_scalar(xn[r][:, :], H[:, ds(s * D, D)], mv[:, ds(s, 1)], rs[:, ds(s, 1)],
                                        ALU.subtract, ALU.mult).then_inc(xn_ready, 1)
            steady(dve, step, n, RING, n, RING)
            nc.vector.memset(xsT[HID:HID + 1, :], 1.0)
            dve.wait_ge(W["sem"]["nat"], W["count"]["nat"])
            for s in range(chunks + 2):
                if s < chunks:
                    dve.wait_ge(fc_done, s + 1)
                    nc.vector.tensor_scalar(f1[s][:, :], ps[0:HID, 2 + s % 2, :], W["fc1b"][:, :], None,
                                            ALU.add).then_inc(fc_ready, 1)
                if 0 <= s - 1 < chunks:
                    dve.wait_ge(a_done, s)
                    nc.vector.tensor_scalar(ca[s - 1][:, :], ps[0:64, 4 + (s - 1) % 2, :], W["convab"][:, :], None,
                                            ALU.add).then_inc(a_ready, 1)
                if 0 <= s - 2 < chunks:
                    dve.wait_ge(b_done, s - 1)
                    nc.vector.scalar_tensor_tensor(cb[s - 2][:, :], ps[0:HID, 6 + (s - 2) % 2, :],
                                                   W["convbb"][:, :], f1[s - 2][:, :], ALU.add,
                                                   ALU.add).then_inc(b_ready, 1)


def fill_bias(nc, W, bias, kinds):
    t4 = W["toep"][:, :].rearrange("p (n a b) -> p n a b", n=NH2, a=KR + 2)
    for c in kinds:
        for g in range(2):
            a0, b0 = (2, 0)[g], (4, 2, 0)[c]
            for h in range(NH2):
                nc.gpsimd.tensor_tensor(
                    bias[c][g][:, h * NKEY:(h + 1) * NKEY].rearrange("p (a b) -> p a b", a=KR),
                    t4[:, h, a0:a0 + KR, b0:b0 + KCOL],
                    W["outside"][:, (2 * c + g) * NKEY:(2 * c + g + 1) * NKEY].rearrange("p (a b) -> p a b", a=KR),
                    ALU.add)


def neighborhood(nc, W, ps, args, xsT, bias, near_dram):
    with ExitStack() as ctx:
        S = Scope(W, ctx, "nb")
        N = 512
        qT = S.sb("qT", [128, TOK])
        kd = S.sb("kd", [128, NH2 * TOK])
        xw = [S.sb(f"xw{p}", [HID + 1, NKEY]) for p in range(2)]
        qw = [S.sb(f"qw{p}", [128, 128]) for p in range(2)]
        v = [S.sb(f"v{p}", [HKEY, 2 * NH2 * HID]) for p in range(2)]
        pr = [S.sb(f"pr{p}", [128, NH2 * NKEY]) for p in range(2)]
        nmax = [S.sb(f"nmax{p}", [128, NH2]) for p in range(2)]
        total = [S.sb(f"total{p}", [128, NH2]) for p in range(2)]
        rec = S.sb("rec", [128, NH2])
        pT = S.sb("pT", [HKEY, 2 * NH2 * 128])
        oT = S.sb("oT", [HID, 128])
        zT = S.sb("zT", [HID + 1, 128])
        y = [S.sb(f"y{p}", [128, D]) for p in range(2)]
        piece = {m: [S.sb(f"{m}{p}", [w[0], w[1] // (2 * COLS)]) for p in range(2)] for m, w in SPLIT.items()}
        stored = [S.sem(f"stored{p}") for p in range(2)]
        piece_loaded = [S.sem(f"piece_loaded{p}") for p in range(2)]
        (qk_done, kd_cleared, q_ready, k_ready, window_ready, scored, fronted, v_ready, masked, shifted, exp_done, p_ready,
         p_turned, pT_ready, weighed, oT_ready, proj_done, zT_ready, out_done, y_ready, high_ready,
         low_ready) = map(S.sem, [
             "qk_done", "kd_cleared", "q_ready", "k_ready", "window_ready", "scored", "fronted", "v_ready", "masked", "shifted",
             "exp_done", "p_ready", "p_turned", "pT_ready", "weighed", "oT_ready", "proj_done",
             "zT_ready", "out_done", "y_ready", "high_ready", "low_ready"])
        ones_set, ones_due = W["ones_set"], W["due"]("ones_set", 3)
        block = ctx.enter_context(nc.Block())
        xs3 = xsT[0:HID + 1, :].rearrange("f (i j) -> f i j", i=B)
        q3 = qT[:, :].rearrange("f (i j) -> f i j", i=B)
        k4 = kd[:, :].rearrange("f (h i j) -> f h i j", h=NH2, i=B)

        def chunk(s):
            return kd[:, :].rearrange("f (h t) -> f h t", h=NH2)[:, :, N * s:N * s + N]

        def place_keys(copy, s, heads):
            for h in heads:
                cp = copy(chunk(s)[32 * h:32 * h + 32, h, :], ps[32 * h:32 * h + 32, 2 * (s % 2) + 1, :])
            return cp
        scores = ps[:, 0:2, 0:2 * NKEY]
        bt, bv, bo, bz, by = 2, 4, 5, 6, 7
        n = 2 * COLS
        FIRST, LAST = 6, n - 2

        def column(t, g):
            return (t - g) * (QC // 2)

        def kind(t):
            return 1 if not isinstance(t, int) or 2 <= t < n - 2 else 0 if t < 2 else 2

        def key_column(t, g):
            return (0, column(t, g) - WIN // 2, NA - KCOL)[kind(t)]

        def piece_columns(m, t):
            return ds(t * (SPLIT[m][1] // n), SPLIT[m][1] // n)

        def by_half(x):
            return x[:, :].rearrange("f (b n) -> f b n", n=HALF)

        def dn_piece(t, part):
            return W["dn_parts"][:, ds(2 * t * (SPLIT["dn"][1] // n), 2 * (SPLIT["dn"][1] // n))].rearrange(
                "f (b q n) -> f b q n", q=2, n=HALF)[:, :, part, :]

        def run(eng, stages):
            def step(s, p):
                for stage, lag in stages:
                    if within(s - lag, n):
                        stage(s - lag, (p + lag) % 2)
            steady(eng, step, n + 4, FIRST, LAST)

        @block.sync
        def _(sp):
            def store(t, g):
                sp.wait_ge(y_ready, t + 1)
                sp.dma_start(near_dram.rearrange("(i j) d -> i j d", i=B)[QR * g:QR * g + QR, ds(column(t, g), QC), :],
                             y[g][:, :]).then_inc(stored[g], 16)

            def load_piece(t, g):
                wait(sp, low_ready, t - 1)
                for m in SPLIT:
                    sp.dma_start(piece[m][g][:, :], args[m][:, piece_columns(m, t)]).then_inc(piece_loaded[g], 16)
            run(sp, [(load_piece, 0), (store, 4)])
            for g in range(2):
                sp.wait_ge(stored[g], 16 * COLS)

        @block.gpsimd
        def _(pool):
            for s in range(TOK // N):
                nc.gpsimd.memset(chunk(s), 0.0).then_inc(kd_cleared, 1)
            pool.wait_ge(q_ready, TOK // N)

            def window(t, g):
                if isinstance(t, int) and t == 2:
                    fill_bias(nc, W, bias, (2,))
                wait(pool, fronted, t - 1)
                nc.gpsimd.tensor_copy(qw[g][:, :].rearrange("f (a b) -> f a b", a=QR),
                                      q3[:, QR * g:QR * g + QR, ds(column(t, g), QC)])
                nc.gpsimd.tensor_copy(xw[g][:, :].rearrange("f (a b) -> f a b", a=KR),
                                      xs3[:, (B - KR) * g:(B - KR) * g + KR, ds(key_column(t, g), KCOL)]
                                      ).then_inc(window_ready, 1)

            def split_low(t, g):
                pool.wait_ge(high_ready, t + 1)
                nc.gpsimd.tensor_tensor(W["gu_low"][:, piece_columns("gu", t)], piece["gu"][g][:, :],
                                        W["gu_high"][:, piece_columns("gu", t)].bitcast(F32), ALU.subtract)
                nc.gpsimd.tensor_tensor(dn_piece(t, 1), by_half(piece["dn"][g]), dn_piece(t, 0).bitcast(F32),
                                        ALU.subtract).then_inc(low_ready, 1)
            run(pool, [(window, 0), (split_low, 2)])

        @block.tensor
        def _(pe):
            pe.wait_ge(W["sem"]["nat"], W["count"]["nat"])
            for s in range(TOK // N):
                for j, w in enumerate((W["nq"], W["nk"])):
                    for ready in (q_ready, k_ready)[:j + 1]:
                        wait(pe, ready, s - 1)
                    nc.tensor.matmul(ps[:, 2 * (s % 2) + j, :], w[:, :], xsT[0:HID + 1, s * N:s * N + N],
                                     start=True, stop=True).then_inc(qk_done, 1)
            pe.wait_ge(q_ready, TOK // N)
            pe.wait_ge(k_ready, TOK // N)
            pe.wait_ge(ones_set, ones_due)

            def turn_p(t, g):
                pe.wait_ge(p_ready, t + 1)
                for i in range(2 * NH2):
                    mm = nc.tensor.transpose(ps[0:HKEY, bt + i // 4, 128 * (i % 4):128 * (i % 4) + 128],
                                             pr[g][:, HKEY * i:HKEY * i + HKEY], W["ident"][:, :])
                    if i % 4 == 3:
                        mm.then_inc(p_turned, 1)

            def project(t, g):
                pe.wait_ge(oT_ready, t + 1)
                nc.tensor.matmul(ps[0:HID, bz, 0:128], W["np"][:, :], oT[:, :], start=True,
                                 stop=True).then_inc(proj_done, 1)

            def score(t, g):
                pe.wait_ge(window_ready, t + 1)
                wait(pe, masked, t)
                for j in range(2):
                    mm = nc.tensor.matmul(ps[:, j, 0:2 * NKEY], qw[g][:, :],
                                          k4[:, 2 * j:2 * j + 2, (B - KR) * g:(B - KR) * g + KR,
                                             ds(key_column(t, g), KCOL)], start=True, stop=True)
                mm.then_inc(scored, 1)

            def out(t, g):
                pe.wait_ge(zT_ready, t + 1)
                wait(pe, y_ready, t)
                nc.tensor.matmul(ps[:, by, 0:D], zT[:, :], W["fc2"][:, :], start=True, stop=True).then_inc(out_done, 1)

            def values(t, g):
                wait(pe, v_ready, t)
                for h in range(2):
                    mm = nc.tensor.matmul(ps[0:HKEY, bv, HID * h:HID * h + HID], xw[g][:, HKEY * h:HKEY * h + HKEY],
                                          W["nv"][:, :], start=True, stop=True)
                mm.then_inc(fronted, 1)

            def weigh(t, g):
                pe.wait_ge(pT_ready, 2 * t + 2)
                pe.wait_ge(v_ready, t + 1)
                wait(pe, oT_ready, t)
                for i in range(2 * NH2):
                    h, j = i // 2, i % 2
                    mm = nc.tensor.matmul(ps[0:HID, bo, 0:128], v[g][:, HID * (NH2 * j + h):HID * (NH2 * j + h + 1)],
                                          pT[:, 128 * i:128 * i + 128], start=i == 0, stop=i == 2 * NH2 - 1)
                mm.then_inc(weighed, 1)
            run(pe, [(turn_p, 3), (score, 1), (project, 4), (values, 1), (weigh, 3), (out, 4)])

        @block.scalar
        def _(act):
            for s in range(TOK // N):
                act.wait_ge(qk_done, 2 * s + 2)
                act.wait_ge(kd_cleared, s + 1)
                place_keys(nc.scalar.copy, s, (2, 3))
                nc.scalar.mul(qT[:, s * N:s * N + N], ps[:, 2 * (s % 2), :], DH2 ** -0.5).then_inc(q_ready, 1)
            act.wait_ge(ones_set, ones_due)

            def copy_o(t, g):
                act.wait_ge(weighed, t + 1)
                nc.scalar.copy(oT[:, :], ps[0:HID, bo, 0:128]).then_inc(oT_ready, 1)

            def copy_v(t, g):
                act.wait_ge(fronted, t + 1)
                wait(act, weighed, t - 1)
                heads = v[g][:, :].rearrange("k (j m) -> k j m", j=2)
                for h in range(NH2):
                    at = HID * h + DH2 * h
                    cp = nc.scalar.copy(heads[:, :, at:at + DH2],
                                        ps[0:HKEY, bv, 0:2 * HID].rearrange("k (j m) -> k j m", j=2)[
                                            :, :, DH2 * h:DH2 * h + DH2])
                cp.then_inc(v_ready, 1)

            def copy_pT(t, g):
                act.wait_ge(p_turned, 2 * t + 1)
                nc.scalar.copy(pT[:, 0:512], ps[0:HKEY, bt, :]).then_inc(pT_ready, 1)

            def bias_z(t, g):
                act.wait_ge(proj_done, t + 1)
                nc.scalar.activation(zT[0:HID, :], ps[0:HID, bz, 0:128], ACT.Identity,
                                     bias=W["npb"][:, :]).then_inc(zT_ready, 1)

            def exp(t, g):
                act.wait_ge(shifted, t + 1)
                for h in range(NH2):
                    e = nc.scalar.activation(pr[g][:, h * NKEY:(h + 1) * NKEY], pr[g][:, h * NKEY:(h + 1) * NKEY],
                                             ACT.Exp, bias=nmax[g][:, h:h + 1], accum_out=total[g][:, h:h + 1])
                e.then_inc(exp_done, 1)

            def split_high(t, g):
                act.wait_ge(piece_loaded[g], 16 * (t - g) + 32)
                nc.scalar.copy(W["gu_high"][:, piece_columns("gu", t)], piece["gu"][g][:, :])
                nc.scalar.copy(dn_piece(t, 0), by_half(piece["dn"][g])).then_inc(high_ready, 1)
            run(act, [(copy_o, 4), (copy_v, 2), (copy_pT, 3), (bias_z, 4), (split_high, 2), (exp, 1)])

        @block.vector
        def _(dve):
            nc.vector.memset(zT[HID:HID + 1, :], 1.0).then_inc(ones_set, 1)
            for p in range(2):
                nc.vector.memset(v[p][:, :], 0.0).then_inc(ones_set, 1)
            dve.wait_ge(ones_set, ones_due)
            for s in range(TOK // N):
                dve.wait_ge(qk_done, 2 * s + 2)
                dve.wait_ge(kd_cleared, s + 1)
                place_keys(nc.vector.tensor_copy, s, (0, 1)).then_inc(k_ready, 1)

            def copy_pT(t, g):
                dve.wait_ge(p_turned, 2 * t + 2)
                nc.vector.tensor_copy(pT[:, 512:1024], ps[0:HKEY, bt + 1, :]).then_inc(pT_ready, 1)

            def normalize(t, g):
                dve.wait_ge(exp_done, t + 1)
                nc.vector.reciprocal(rec[:, :], total[g][:, :])
                dve.drain()
                p3 = pr[g][:, :].rearrange("p (h n) -> p h n", h=NH2)
                nc.vector.tensor_tensor(p3, p3, rec[:, :, None].broadcast_to([128, NH2, NKEY]),
                                        ALU.mult).then_inc(p_ready, 1)

            def mask(t, g):
                dve.wait_ge(scored, t + 1)
                nc.vector.tensor_tensor(pr[g][:, :].rearrange("p (j n) -> p j n", j=2), scores,
                                        bias[kind(t)][g][:, :].rearrange("p (j n) -> p j n", j=2),
                                        ALU.add).then_inc(masked, 1)

            def copy_y(t, g):
                dve.wait_ge(out_done, t + 1)
                wait(dve, stored[g], 8 * (t - g))
                nc.vector.tensor_copy(y[g][:, :], ps[:, by, 0:D]).then_inc(y_ready, 1)

            def biggest(t, g):
                dve.drain()
                nc.vector.tensor_reduce(nmax[g][:, :], pr[g][:, :].rearrange("p (h n) -> p h n", h=NH2), AX.X,
                                        ALU.max, negate=True).then_inc(shifted, 1)
            run(dve, [(copy_pT, 3), (normalize, 2), (mask, 1), (biggest, 1), (copy_y, 4)])


def route_four(nc, W, ps, H, near_dram, xnT, sc, sig_done):
    with ExitStack() as ctx:
        S = Scope(W, ctx, "rf")
        n = NTILE
        add = S.sb("add", [128, n * D])
        mv, rs = W["row_mv"], W["row_rs"]
        xn = [S.sb(f"xn{p}", [128, D]) for p in range(2)]
        xT = [S.sb(f"xT{p}", [HALF + 1, 256]) for p in range(2)]
        (xn_ready, turned, xT_ready, gated, kept) = map(S.sem, [
            "xn_ready", "turned", "xT_ready", "gated", "kept"])
        parts = row_parts(W)
        ones_set, ones_due = W["ones_set"], W["due"]("ones_set", 2)
        norm_due = W["due"]("norm", 2)
        block = ctx.enter_context(nc.Block())

        @block.sync
        def _(sp):
            for rows_in, _, part in parts:
                sp.dma_start(add[:, :].rearrange("p (t d) -> p t d", t=n)[:, part, :],
                             near_dram.rearrange("(t p) d -> p t d", p=128)[:, part, :]).then_inc(rows_in, 16)

        @block.gpsimd
        def _(pool):
            rstd_rows(nc, W, pool, parts, norm_due)

            def step(s, p):
                pool.wait_ge(xT_ready, s + 1)
                nc.gpsimd.tensor_copy(xnT[0:HALF, :].rearrange("f (k t) -> f k t", k=2)[:, :, ds(128 * s, 128)],
                                      xT[p][0:HALF, :].rearrange("f (k t) -> f k t", k=2)).then_inc(kept, 1)
            steady(pool, step, n, 2, n)

        @block.tensor
        def _(pe):
            pe.wait_ge(ones_set, ones_due)
            pe.wait_ge(W["sem"]["rest"], W["count"]["rest"])

            def step(s, p):
                if within(s, n):
                    pe.wait_ge(xn_ready, s + 1)
                    for k in range(2):
                        mm = nc.tensor.transpose(ps[0:HALF, p, 128 * k:128 * k + 128],
                                                 xn[p][:, HALF * k:HALF * k + HALF], W["ident"][:, :])
                    mm.then_inc(turned, 1)
                if within(s - 1, n):
                    wait(pe, xT_ready, s)
                    for k in range(2):
                        mm = nc.tensor.matmul(ps[:, 2, ds(E * (s - 1), E)], xT[1 - p][0:HALF + k, 128 * k:128 * k + 128],
                                              W["router"][0:HALF + k, E * k:E * k + E], start=k == 0, stop=k == 1)
                    mm.then_inc(gated, 1)
            steady(pe, step, n + 1, 2, n)

        @block.scalar
        def _(act):
            act.wait_ge(ones_set, ones_due)

            def step(s, p):
                act.wait_ge(turned, s + 1)
                wait(act, gated, s - 1)
                wait(act, kept, s - 1)
                nc.scalar.copy(xT[p][0:HALF, :], ps[0:HALF, p, 0:256]).then_inc(xT_ready, 1)
            steady(act, step, n, 2, n)
            act.wait_ge(gated, n)
            nc.scalar.activation(sc[:, :], ps[:, 2, 0:n * E], ACT.Sigmoid).then_inc(sig_done, 1)

        @block.vector
        def _(dve):
            for p in range(2):
                nc.vector.memset(xT[p][HALF:HALF + 1, :], 1.0).then_inc(ones_set, 1)
            take_rows(nc, W, dve, parts, H, add)

            def step(s, p):
                wait(dve, turned, s - 1)
                nc.vector.tensor_scalar(xn[p][:, :], H[:, ds(s * D, D)], mv[:, ds(s, 1)], rs[:, ds(s, 1)],
                                        ALU.subtract, ALU.mult).then_inc(xn_ready, 1)
            normalize_parts(W, dve, step, norm_due)


def share_buffers(S):
    n, G, bufs = NTILE, 4, {}
    for name, cols in (("sfc", n * E), ("pair", n * G * 6), ("gs", n * G), ("ge", n * G * G), ("gt", n * G * G),
                       ("gm", n * G), ("top", 8 * n), ("atf", 8 * n), ("hit", n * 4 * E), ("sel", n * E), ("tot", n)):
        bufs[name] = S.sb(name, [128, cols])
    bufs["at"] = S.sb("at", [128, 8 * n], U32)
    return bufs


def expert_shares(nc, W, dve, bufs, sc, sig_done, share):
    n, G = NTILE, 4
    sfc, pair, gs, ge, gt, gm, top, at, atf, hit, sel, tot = (
        bufs[m] for m in ("sfc", "pair", "gs", "ge", "gt", "gm", "top", "at", "atf", "hit", "sel", "tot"))
    dve.wait_ge(sig_done, 1)
    dve.wait_ge(W["sem"]["rest"], W["count"]["rest"])
    t3 = lambda x: x[:, :].rearrange("p (t e) -> p t e", t=n)
    nc.vector.tensor_tensor(t3(sfc), t3(sc), W["corr"][:, None, :].broadcast_to([128, n, E]), ALU.add)
    dve.drain()
    s4 = sfc[:, :].rearrange("p (g e) -> p g e", e=4)
    p6 = pair[:, :].rearrange("p (g e) -> p g e", e=6)
    nc.vector.tensor_tensor(p6[:, :, 0:3], s4[:, :, 0:3], s4[:, :, 1:4], ALU.add)
    nc.vector.tensor_tensor(p6[:, :, 3:5], s4[:, :, 0:2], s4[:, :, 2:4], ALU.add)
    nc.vector.tensor_tensor(p6[:, :, 5:6], s4[:, :, 0:1], s4[:, :, 3:4], ALU.add)
    dve.drain()
    nc.vector.tensor_reduce(gs[:, :], p6, AX.X, ALU.max)
    dve.drain()
    mine = gs[:, :].rearrange("p (t g) -> p t g", g=G)[:, :, :, None].broadcast_to([128, n, G, G])
    other = gs[:, :].rearrange("p (t g) -> p t g", g=G)[:, :, None, :].broadcast_to([128, n, G, G])
    q4 = lambda x: x[:, :].rearrange("p (t g h) -> p t g h", g=G, h=G)
    q3 = lambda x: x[:, :].rearrange("p (t g) -> p t g", g=G * G)
    nc.vector.tensor_tensor(q4(ge), other, mine, ALU.is_ge)
    nc.vector.tensor_tensor(q4(gt), other, mine, ALU.is_gt)
    dve.drain()
    nc.vector.tensor_tensor(q3(ge), q3(ge), W["earlier"][:, None, :].broadcast_to([128, n, G * G]), ALU.mult)
    nc.vector.tensor_tensor(q3(gt), q3(gt), W["later"][:, None, :].broadcast_to([128, n, G * G]), ALU.mult)
    dve.drain()
    nc.vector.tensor_tensor(ge[:, :], ge[:, :], gt[:, :], ALU.add)
    dve.drain()
    nc.vector.tensor_reduce(gm[:, :], ge[:, :].rearrange("p (g h) -> p g h", h=G), AX.X, ALU.add)
    dve.drain()
    nc.vector.tensor_scalar(gm[:, :], gm[:, :], 1.5, None, ALU.is_lt)
    dve.drain()
    nc.vector.tensor_tensor(s4, s4, gm[:, :, None].broadcast_to([128, n * G, 4]), ALU.mult)
    dve.drain()
    choose(nc, dve, top, at, sfc, n)
    nc.vector.tensor_copy(atf[:, :], at[:, :])
    dve.drain()
    h4 = hit[:, :].rearrange("p (t k e) -> p t k e", t=n, k=4)
    nc.vector.tensor_tensor(
        h4, W["iota"][:, None, None, 0:E].broadcast_to([128, n, 4, E]),
        atf[:, :].rearrange("p (t k) -> p t k", t=n)[:, :, 0:4, None].broadcast_to([128, n, 4, E]),
        ALU.is_equal)
    dve.drain()
    nc.vector.tensor_reduce(t3(sel), hit[:, :].rearrange("p (t k e) -> p t e k", t=n, k=4), AX.X, ALU.add)
    dve.drain()
    nc.vector.tensor_tensor(sel[:, :], sel[:, :], sc[:, :], ALU.mult)
    dve.drain()
    nc.vector.tensor_reduce(tot[:, :], t3(sel), AX.X, ALU.add)
    dve.drain()
    nc.vector.tensor_scalar(tot[:, :], tot[:, :], 1e-20, None, ALU.add)
    dve.drain()
    nc.vector.reciprocal(tot[:, :], tot[:, :])
    dve.drain()
    nc.vector.tensor_tensor(t3(sel), t3(sel), tot[:, :, None].broadcast_to([128, n, E]), ALU.mult)
    dve.drain()
    s18 = share[:, :].rearrange("p (t e) -> p t e", t=n)
    nc.vector.tensor_scalar(s18[:, :, 0:E], t3(sel), 2.5, None, ALU.mult)
    nc.vector.memset(s18[:, :, E:E + 2], 1.0)


def experts_four(nc, W, ps, H, xnT, sc, sig_done, share, out_dram):
    with ExitStack() as ctx:
        S = Scope(W, ctx, "e4")
        n, P3 = NTILE, 3
        WP = 4 * I2
        xb = [S.sb(f"xb{p}", [HALF + 1, 256], F32R) for p in range(2)]
        xlow = [S.sb(f"xlow{p}", [HALF + 1, 256], F32R) for p in range(2)]
        sg = [S.sb(f"sg{i}", [128, 2 * I2]) for i in range(P3)]
        hh = [S.sb(f"hh{i}", [128, 2 * (I2 + 1)]) for i in range(P3)]
        hT = [S.sb(f"hT{i}", [I2 + 1, 256], F32R) for i in range(P3)]
        hlow = [S.sb(f"hlow{i}", [I2 + 1, 256], F32R) for i in range(P3)]
        y = [S.sb(f"y{p}", [128, D]) for p in range(2)]
        share_bufs = share_buffers(S)
        stored = [S.sem(f"stored{p}") for p in range(2)]
        (xb_ready, up_done, sg_ready, hh_ready, turned, hT_ready, hlow_ready, summed, y_ready) = map(S.sem, [
            "xb_ready", "up_done", "sg_ready", "hh_ready", "turned", "hT_ready", "hlow_ready", "summed", "y_ready"])
        ones_set, ones_due = W["ones_set"], W["due"]("ones_set", 4)
        block = ctx.enter_context(nc.Block())

        def out_parts(part):
            return ps[:, 6, 0:2 * D].rearrange("p (b q n) -> p b q n", q=2, n=HALF)[:, :, part, :]

        def tiles(eng, tile, after):
            steady(eng, tile, n, 2, n)
            after()

        def lagging(t, q, lag):
            if q >= lag:
                return t, q - lag
            if isinstance(t, int) and t == 0:
                return None
            return t - 1, q - lag + PAIRS

        @block.sync
        def _(sp):
            def tile(t, p):
                sp.wait_ge(y_ready, t + 1)
                sp.dma_start(out_dram[ds(128 * t, 128), :], y[p][:, :]).then_inc(stored[p], 16)
            tiles(sp, tile, lambda: None)
            for p in range(2):
                sp.wait_ge(stored[p], 8 * n)

        @block.gpsimd
        def _(pool):

            def tile(t, p):
                wait(pool, up_done, PAIRS * (t - 1))
                x = xnT[0:HALF, :].rearrange("f (k t) -> f k t", k=2)[:, :, ds(128 * t, 128)]
                halves = lambda b: b[p][0:HALF, :].rearrange("f (k t) -> f k t", k=2)
                nc.gpsimd.tensor_copy(halves(xb), x)
                pool.drain()
                nc.gpsimd.tensor_tensor(halves(xlow), x, halves(xb).bitcast(F32), ALU.subtract).then_inc(xb_ready, 1)
            tiles(pool, tile, lambda: None)

        @block.tensor
        def _(pe):
            pe.wait_ge(ones_set, ones_due)

            def up(t, q, p):
                i = q % P3
                if q == 0:
                    pe.wait_ge(xb_ready, t + 1)
                wait(pe, hh_ready, PAIRS * t + q - 2)
                for k in range(2):
                    for x, w in ((xb, W["gu_high"]), (xb, W["gu_low"]), (xlow, W["gu_high"])):
                        mm = nc.tensor.matmul(ps[:, i, 0:WP], x[p][0:HALF + k, 128 * k:128 * k + 128],
                                              w[0:HALF + k, (2 * q + k) * WP:(2 * q + k + 1) * WP],
                                              start=k == 0 and w is not W["gu_low"] and x is xb,
                                              stop=k == 1 and x is xlow)
                mm.then_inc(up_done, 1)

            def turn(t, q):
                i = q % P3
                pe.wait_ge(hh_ready, PAIRS * t + q + 1)
                for j in range(2):
                    mm = nc.tensor.transpose(ps[0:I2 + 1, 3 + i, 128 * j:128 * j + 128],
                                             hh[i][:, (I2 + 1) * j:(I2 + 1) * (j + 1)], W["ident"][:, :])
                mm.then_inc(turned, 1)

            def down(t, q):
                i = q % P3
                pe.wait_ge(hT_ready, PAIRS * t + q + 1)
                pe.wait_ge(hlow_ready, PAIRS * t + q + 1)
                if q == 0:
                    wait(pe, y_ready, t)
                for j in range(2):
                    parts = W["dn_parts"][:, 2 * (2 * q + j) * D:2 * (2 * q + j + 1) * D]
                    nc.tensor.matmul(ps[:, 6, 0:2 * D], hT[i][:, 128 * j:128 * j + 128], parts,
                                     start=q == 0 and j == 0, stop=False)
                    mm = nc.tensor.matmul(out_parts(0), hlow[i][:, 128 * j:128 * j + 128],
                                          parts.rearrange("f (b q n) -> f b q n", q=2, n=HALF)[:, :, 0, :],
                                          start=False, stop=q == PAIRS - 1 and j == 1)
                mm.then_inc(summed, 1)

            def tile(t, p):
                for q in range(PAIRS):
                    up(t, q, p)
                    if lagging(t, q, 1):
                        turn(*lagging(t, q, 1))
                    if lagging(t, q, 2):
                        down(*lagging(t, q, 2))

            def after():
                turn(n - 1, PAIRS - 1)
                down(n - 1, PAIRS - 2)
                down(n - 1, PAIRS - 1)
            tiles(pe, tile, after)

        @block.scalar
        def _(act):
            def gate(t, q):
                i = q % P3
                act.wait_ge(up_done, PAIRS * t + q + 1)
                nc.scalar.activation(sg[i][:, :].rearrange("p (j n) -> p j n", j=2),
                                     ps[:, i, 0:WP].rearrange("p (j u n) -> p j u n", j=2, u=2)[:, :, 0, :],
                                     ACT.Silu).then_inc(sg_ready, 1)

            def copy_h(t, q):
                i = q % P3
                act.wait_ge(turned, PAIRS * t + q + 1)
                nc.scalar.copy(hT[i][:, :], ps[0:I2 + 1, 3 + i, 0:256]).then_inc(hT_ready, 1)

            def tile(t, p):
                for q in range(PAIRS):
                    gate(t, q)
                    if lagging(t, q, 1):
                        copy_h(*lagging(t, q, 1))
            tiles(act, tile, lambda: copy_h(n - 1, PAIRS - 1))

        @block.vector
        def _(dve):
            for p in range(2):
                for b, v in ((xb, W["ones"]), (xlow, W["zero"])):
                    nc.vector.tensor_copy(b[p][HALF:HALF + 1, :].rearrange("f (k t) -> f k t", k=2),
                                          v[HALF:HALF + 1, None, 0:128].broadcast_to([1, 2, 128])
                                          ).then_inc(ones_set, 1)
            expert_shares(nc, W, dve, share_bufs, sc, sig_done, share)
            dve.drain()

            def split_h(t, q):
                i = q % P3
                dve.wait_ge(hT_ready, PAIRS * t + q + 1)
                nc.vector.tensor_tensor(hlow[i][:, :], ps[0:I2 + 1, 3 + i, 0:256], hT[i][:, :].bitcast(F32),
                                        ALU.subtract).then_inc(hlow_ready, 1)

            def weigh(t, q):
                i = q % P3
                dve.wait_ge(sg_ready, PAIRS * t + q + 1)
                for j in range(2):
                    o = (I2 + 1) * j
                    c = share[:, ds(t * 2 * PAIRS + 2 * q + j, 1)]
                    last = nc.vector.scalar_tensor_tensor(
                        hh[i][:, o:o + I2], sg[i][:, I2 * j:I2 * j + I2], c,
                        ps[:, i, 2 * I2 * j + I2:2 * I2 * (j + 1)], ALU.mult, ALU.mult)
                nc.vector.tensor_copy(hh[i][:, I2:2 * (I2 + 1):I2 + 1],
                                      share[:, ds(t * 2 * PAIRS + 2 * q, 2)]).then_inc(hh_ready, 1)

            def finish(t, p):
                dve.wait_ge(summed, PAIRS * (t + 1))
                wait(dve, stored[p], 8 * (t - p))
                halves = lambda x: x.rearrange("p (b n) -> p b n", n=HALF)
                nc.vector.tensor_tensor(halves(y[p][:, :]), out_parts(1), halves(H[:, ds(t * D, D)]), ALU.add)
                dve.drain()
                nc.vector.tensor_tensor(halves(y[p][:, :]), out_parts(0), halves(y[p][:, :]), ALU.add).then_inc(y_ready, 1)

            def tile(t, p):
                for q in range(PAIRS):
                    weigh(t, q)
                    if lagging(t, q, 1):
                        split_h(*lagging(t, q, 1))
                    if q == 1 and lagging(t, q, 2):
                        finish(t - 1, 1 - p)

            def after():
                split_h(n - 1, PAIRS - 1)
                finish(n - 1, (n - 1) % 2)
            tiles(dve, tile, after)


WEIGHTS = {
    "ident": (128, 128, "ident"),
    "pw": (128, KC * D, "embed"), "pb": (128, D, "embed"), "lng": (128, D, "embed"), "lnb": (128, D, "embed"),
    "pe": (128, D, "embed"),
    "ff1b": (128, KC, "ff"), "ff2b": (HALF, 2, "ff"),
    "own": (HALF, NH // 2, "ident"),
    "qk_a": (HALF + 1, 4 * D, "a"), "v_a": (HALF + 1, 2 * D, "a"), "proj_a": (HALF + 1, 2 * D, "a"),
    "apart": (128, 128, "a"),
    "qk_b": (HALF + 1, 4 * D, "b"), "v_b": (HALF + 1, 2 * D, "b"), "proj_b": (HALF + 1, 2 * D, "b"),
    "temp": (NA, NH, "b"),
    "gate": (HALF + 1, 2 * E, "moe1"), "w1": (HALF + 1, E * 2 * D, "moe1"), "w2": (HALF + 1, E * 2 * D, "moe1"),
    "iota": (128, 32, "ident"), "steps": (128, 16, "moe1"), "below": (128, 128, "moe1"),
    "fc1": (HALF, 2 * HID, "nat"), "fc1b": (HID, 1, "nat"), "conva": (HID, 64, "nat"), "convab": (64, 1, "nat"),
    "convb": (64, HID, "nat"), "convbb": (HID, 1, "nat"), "nq": (HID + 1, 128, "nat"), "nk": (HID + 1, 128, "nat"),
    "nv": (HID + 1, HID, "nat"), "np": (HID, HID, "nat"), "npb": (HID, 1, "nat"), "fc2": (HID + 1, D, "nat"),
    "toep": (128, NH2 * (KR + 2) * (KCOL + 4), "rest"), "outside": (128, 6 * NKEY, "rest"),
    "router": (HALF + 1, 2 * E, "rest"), "corr": (128, E, "rest"),
    "earlier": (128, 16, "rest"), "later": (128, 16, "rest"),
}
SPLIT_FF = {"ff1": (HALF, 2 * FF), "ff2": (128, KC * D)}
FF_COUNTS = {"hidden": 2 * KC, "gelu_done": 2 * KC, "x_high": 2, "x_split": 2, "g_high": 2 * KC, "g_split": 2 * KC,
             "summed": 4, "out_ready": 4}
SPLIT = {"gu": (HALF + 1, PAIRS * 2 * 4 * I2), "dn": (I2 + 1, PAIRS * 2 * D)}


EARLY = ("ff", "a", "b")
LATE = ("rest",)


def load(nc, W, args, groups, eng):
    for name, (_, _, g) in WEIGHTS.items():
        if g in groups:
            eng.dma_start(W[name][:, :], args[name]).then_inc(W["sem"][g], 16)


def build(nc, args):
    with ExitStack() as ctx:
        def hold(groups, scope):
            return {name: scope.enter_context(nc.sbuf_tensor("w_" + name, [p, c], F32))
                    for name, (p, c, g) in WEIGHTS.items() if g in groups}
        W = {"nc": nc, "whole": ctx, **hold(("ident",), ctx)}
        S = Scope(W, ctx, "w")
        for m, c in (("mhalf", 1), ("ones", 128), ("zero", D)):
            W[m] = S.sb(m, [128, c])
        groups = dict.fromkeys(g for _, _, g in WEIGHTS.values())
        W["sem"] = {g: S.sem("loaded_" + g) for g in groups if g != "ident"}
        W["count"] = {g: 16 * sum(x[2] == g for x in WEIGHTS.values()) for g in groups}
        W["count"]["b"] += 16
        W["sem"]["ident"] = W["sem"]["embed"]
        W["count"]["embed"] += W["count"]["ident"]
        ps = ctx.enter_context(nc.psum_tensor("ps", [128, 8, 512], F32))
        slot = S.sb("slot", [128, NTILE], U32)
        owner = S.sb("owner", [1, SORT_TILES], I32)
        for m, c in (("row_stats", 6), ("row_mv", 3), ("row_rs", 1)):
            W[m] = S.sb(m, [128, c * NTILE])
        share = S.sb("share", [128, NTILE * 2 * PAIRS])
        set_ = S.sem("constants_set")
        for m in ("ones_set", "stat_done", "rstd_ready", "early_rows", "late_rows"):
            W[m] = S.sem(m)
        due = {"ones_set": 0, "norm": 0, "early_rows": 0, "late_rows": 0}

        def due_after(name, parts):
            due[name] += parts
            return due[name]
        W["due"] = due_after
        h_dram = nc.dram_tensor("h_rows", (TOK, D), F32, kind="Internal").ap()
        near_dram = nc.dram_tensor("near_rows", (TOK, D), F32, kind="Internal").ap()
        sorted_dram = nc.dram_tensor("sorted_rows", (SORT_TILES * 128, D), F32, kind="Internal").ap()
        done_dram = nc.dram_tensor("done_rows", (SORT_TILES * 128, D), F32, kind="Internal").ap()

        H = S.sb("H", [128, NTILE * D])
        W.update(hold(("nat",), ctx))
        middle = ctx.enter_context(ExitStack())
        W.update(hold(("moe1",), middle))
        early = ctx.enter_context(ExitStack())
        W.update(hold(EARLY, early))
        for m, w in SPLIT_FF.items():
            for part in ("_high", "_low"):
                W[m + part] = early.enter_context(nc.sbuf_tensor("w_" + m + part, list(w), F32R))
        W["ff_sems"] = {m: S.sem("ff_" + m) for m in FF_COUNTS}
        for m in ("h_turned", "h_ready"):
            W[m] = S.sem(m)
        for m in ("qk", "v", "proj"):
            W[m] = {w: W[f"{m}_{w}"] for w in "ab"}
        with early:
            E1 = Scope(W, early, "h")
            h96 = W["h96"] = E1.sb("h96", [NA, B * D])
            W["h_stats"] = E1.sb("h_stats", [NA, 6 * B])
            with ExitStack() as first:
                A = Scope(W, first, "x")
                x0T, x1T, yT = (A.sb(m, [HALF, 2 * B * NI]) for m in ("x0T", "x1T", "yT"))
                with ExitStack() as start:
                    W.update(hold(("embed",), start))
                    W["lnbpe"] = Scope(W, start, "w").sb("lnbpe", [128, D])
                    with nc.Block() as block:
                        @block.sync
                        def _(sp):
                            load(nc, W, args, ("ident", "embed"), sp)

                        @block.gpsimd
                        def _(pool):
                            for t, v in ((W["mhalf"], -0.5), (W["ones"], 1.0), (W["zero"], 0.0)):
                                nc.gpsimd.memset(t[:, :], v).then_inc(set_, 1)
                    embed(nc, W, ps, args, x0T)
                feed_forward(nc, W, ps, 0, x0T, yT, None)
                attention(nc, W, ps, "aa", 2 * NI, "a", yT, x0T, x1T, None, None)
                feed_forward(nc, W, ps, 1, x1T, yT, x1T, h96)
            attention(nc, W, ps, "ab", NA, "b", None, None, None, h96, h_dram)
        with middle:
            M = Scope(W, middle, "m")
            xn_all = M.sb("xn_all", [128, NTILE * D])
            route(nc, W, ps, H, h_dram, sorted_dram, xn_all, slot, owner)
            experts_one(nc, W, ps, args, H, sorted_dram, done_dram, xn_all, slot, owner)
        W.update(hold(LATE, ctx))
        for m in ("gu_high", "gu_low"):
            W[m] = S.sb(m, list(SPLIT["gu"]), F32R)
        W["dn_parts"] = S.sb("dn_parts", [I2 + 1, 2 * SPLIT["dn"][1]], F32R)
        with ExitStack() as mid:
            M = Scope(W, mid, "s")
            xsT = M.sb("xsT", [HID + 1, TOK])
            bias = [[M.sb(f"bias{c}{g}", [128, NH2 * NKEY]) for g in range(2)] for c in range(3)]
            squeeze(nc, W, ps, args, H, xsT, bias)
            neighborhood(nc, W, ps, args, xsT, bias, near_dram)
        xnT = S.sb("xnT", [HALF, 2 * TOK])
        scores, scores_ready = S.sb("scores", [128, NTILE * E]), S.sem("scores_ready")
        route_four(nc, W, ps, H, near_dram, xnT, scores, scores_ready)
        experts_four(nc, W, ps, H, xnT, scores, scores_ready, share, args["out"])


def laid_out(i):
    f = np.float32

    def halves(w, bias=None):
        o = np.zeros((HALF + 1, 2, w.shape[1]), f)
        o[:HALF] = w.reshape(2, HALF, -1).transpose(1, 0, 2)
        if bias is not None:
            o[HALF, 1] = bias
        return o

    def with_row(w, bias):
        return np.concatenate([w, bias[None]], 0)

    def rows(v, p=128):
        return np.broadcast_to(v, (p, v.shape[-1]))

    def padded_heads(w, nh, dh):
        o = np.zeros(w.shape[:-1] + (nh, 32), f)
        o[..., :dh] = w.reshape(w.shape[:-1] + (nh, dh))
        return o.reshape(w.shape[:-1] + (nh * 32,))

    o = {"ident": np.eye(128, dtype=f)}
    x = i["x"].reshape(B, 3, 8, 16, 8, 16).transpose(1, 3, 5, 0, 2, 4).reshape(KC, 128, 8, 128)
    o["x"] = x.transpose(1, 2, 0, 3).reshape(128, 8 * KC * 128)
    o["txt"] = i["txt"].transpose(1, 0, 2)
    o["pw"] = i["L0_tok_patch_w"].reshape(D, KC, 128).transpose(2, 1, 0)
    o["pb"], o["lng"], o["lnb"] = (rows(i["L0_tok_" + m]) for m in ("patch_b", "ln_g", "ln_b"))
    ang = (np.arange(NI, dtype=f)[:, None] / np.power(f(10000.0), f(2.0) * np.arange(D // 2, dtype=f)[None] / f(D))).astype(f)
    pe = np.zeros((NI, D), f)
    pe[:, 0::2], pe[:, 1::2] = np.sin(ang), np.cos(ang)
    o["pe"] = np.concatenate([pe, pe], 0)
    o["ff1"] = halves(i["L0_tok_ff1_w"])[:HALF]
    o["ff1b"] = i["L0_tok_ff1_b"].reshape(KC, 128).T
    o["ff2"] = i["L0_tok_ff2_w"].reshape(KC, 128, D).transpose(1, 0, 2)
    o["ff2b"] = i["L0_tok_ff2_b"].reshape(2, HALF).T
    w, b = i["L0_tok_qkv_w"], i["L0_tok_qkv_b"]
    o["qk_a"], o["v_a"] = halves(w[:, :2 * D], b[:2 * D]), halves(w[:, 2 * D:], b[2 * D:])
    o["proj_a"] = halves(i["L0_tok_proj_w"], i["L0_tok_proj_b"])
    o["apart"] = np.kron(1 - np.eye(2, dtype=f), np.full((NI, NI), -1e30, f))
    w = i["L0_attn_w_qkv"]
    o["qk_b"], o["v_b"] = halves(w[:, :2 * D]), halves(w[:, 2 * D:])
    o["proj_b"] = halves(i["L0_attn_w_proj"], i["L0_attn_b_proj"])
    o["own"] = np.kron(np.eye(NH // 2, dtype=f), np.ones((DH, 1), f))
    o["temp"] = rows(i["L0_attn_temperature"].reshape(1, NH), NA)
    o["gate"] = halves(i["L0_ffn_Wg"].T, i["L0_ffn_bg"])
    for m, w, b in (("w1", "W1", "b1"), ("w2", "W2", "b2")):
        o[m] = np.stack([halves(i["L0_ffn_" + w][e].T, i["L0_ffn_" + b][e]) for e in range(E)], 1)
    o["iota"] = rows(np.arange(32, dtype=f)[None])
    o["steps"] = rows(128 * np.arange(16, dtype=f)[None])
    o["below"] = np.triu(np.ones((128, 128), f), 1)
    n = lambda m: i["L1_attn_" + m]
    o["fc1"], o["fc1b"] = halves(n("fc1_w").T)[:HALF], n("fc1_b")[:, None]
    o["conva"], o["convab"] = n("convA_w").T, n("convA_b")[:, None]
    o["convb"], o["convbb"] = n("convB_w").T, n("convB_b")[:, None]
    w = with_row(n("qkv_w").T, n("qkv_b"))
    o["nq"], o["nk"] = (padded_heads(w[:, HID * j:HID * j + HID], NH2, DH2) for j in range(2))
    o["nv"] = w[:, 2 * HID:]
    o["np"], o["npb"] = n("proj_w").T, n("proj_b")[:, None]
    o["fc2"] = with_row(n("fc2_w").T, n("fc2_b"))
    R = 2 * WIN - 1
    wide = np.zeros((NH2, QR + KR + 2 + R, QC + KCOL + 4 + R), f)
    wide[:, QR:QR + R, QC:QC + R] = n("rpb")
    toep = np.zeros((QR, QC, NH2, KR + 2, KCOL + 4), f)
    for r in range(QR):
        for c in range(QC):
            toep[r, c] = wide[:, QR + 2 - r:QR + 2 - r + KR + 2, QC - c:QC - c + KCOL + 4]
    o["toep"] = toep
    first = lambda at, length: np.clip(at - WIN // 2, 0, length - WIN)
    outside = np.full((128, 3, 2, KR, KCOL), -1e30, f)
    for kind, c in enumerate((0, 1, COLS - 1)):
        k0 = (0, QC - WIN // 2, NA - KCOL)[kind]
        for g in range(2):
            for r in range(QR):
                for j in range(QC):
                    a = first(QR * g + r, B) - (B - KR) * g
                    b = first(QC * c + j, NA) - k0
                    outside[r * QC + j, kind, g, a:a + WIN, b:b + WIN] = 0.0
    o["outside"] = outside
    m = lambda k: i["L1_ffn_" + k]
    o["router"], o["corr"] = halves(m("router_w").T, m("router_b")), rows(m("corr_bias"))
    o["earlier"] = rows(np.tril(np.ones((4, 4), f), -1).reshape(1, 16))
    o["later"] = rows(np.triu(np.ones((4, 4), f), 1).reshape(1, 16))
    gates = [(m("gWg")[e], m("gbg")[e], m("gWu")[e], m("gbu")[e], m("gWd")[e], m("gbd")[e]) for e in range(E)]
    for j in range(2):
        c = slice(I2 * j, I2 * j + I2)
        gates.append((m("sWg")[:, c], m("sbg")[c], m("sWu")[:, c], m("sbu")[c], m("sWd")[c],
                      m("sbd") if j == 0 else np.zeros(D, f)))
    gu = [np.concatenate([halves(x[0], x[1]), halves(x[2], x[3])], 2) for x in gates]
    o["gu"] = np.stack([np.concatenate([gu[2 * q], gu[2 * q + 1]], 2) for q in range(PAIRS)], 1)
    o["dn"] = np.stack([with_row(x[4], x[5]) for x in gates], 1)
    for name, (p, c) in [(name, x[:2]) for name, x in WEIGHTS.items()] + list(SPLIT.items()) + list(SPLIT_FF.items()):
        o[name] = np.ascontiguousarray(o[name]).reshape(p, c)
    return {k: np.ascontiguousarray(v, f) for k, v in o.items()}


def kernel(**inputs):
    import concourse.bacc as _bacc
    from concourse.bass_utils import run_bass_kernel_spmd as _run

    arrays = laid_out({k: np.asarray(v) for k, v in inputs.items()})
    nc = _bacc.Bacc("TRN2", target_bir_lowering=False, num_devices=1)
    args = {k: nc.dram_tensor("in_" + k, v.shape, F32, kind="ExternalInput").ap() for k, v in arrays.items()}
    args["out"] = nc.dram_tensor("out_rows", (TOK, D), F32, kind="ExternalOutput").ap()
    build(nc, args)
    r = _run(nc, [{"in_" + k: v for k, v in arrays.items()}], core_ids=[0])
    return r.results[0]["out_rows"].reshape(B, NA, D)
```
